# Optimizing a Trainium2 kernel written in Bass

```python
import numpy as np
import jax
import jax.numpy as jnp

def _softmax(x, axis=-1):
    return jax.nn.softmax(x, axis=axis)

def _gelu(x):
    return jax.nn.gelu(x, approximate=True)

def _silu(x):
    return jax.nn.silu(x)

def _sigmoid(x):
    return jax.nn.sigmoid(x)

def _layernorm(x, axis=-1, eps=1e-05):
    m = jnp.mean(x, axis=axis, keepdims=True)
    v = jnp.var(x, axis=axis, keepdims=True)
    return (x - m) / jnp.sqrt(v + eps)

def _scatter_add(tgt, idx, src, axis=0):
    return tgt.at[idx].add(src)

def _segment_sum(src, seg, n):
    return jax.ops.segment_sum(src, seg, n)
kernel_name = 'mk_adaln_attn_ffn_d1_seqx_r4_3a0bcf'

def setup_inputs(seed: int=0):
    np.random.seed(seed)
    _w = jnp.asarray

    def _rec_inputs():
        import jax
        import jax.numpy as jnp
        _rk = jax.random.key(seed)
        x = -0.000125 + 0.9999 * jax.random.normal(jax.random.fold_in(_rk, 1), (2, 1024, 256), jnp.float32)
        _lenS = 1024 - jax.random.randint(jax.random.fold_in(_rk, 7), (2,), 0, max(1, 1024 // 4) + 1, jnp.int32)
        _lenS2 = 1024 - jax.random.randint(jax.random.fold_in(_rk, 8), (2,), 0, max(1, 1024 // 4) + 1, jnp.int32)
        cond_1024 = -0.00493535 + 1.00056 * jax.random.normal(jax.random.fold_in(_rk, 11), (2, 256), jnp.float32)
        return (x, cond_1024)
    x, cond_1024 = _rec_inputs()

    def _L0_cond_setup():
        import jax, jax.numpy as jnp
        import numpy as np
        import math
        D = 256
        H = 256
        key = jax.random.key(seed)
        k1, k2, k3, k4 = jax.random.split(key, 4)
        x = jax.random.normal(k1, (64, 128, D), dtype=jnp.float32)
        h0 = jax.random.normal(k2, (64, H), dtype=jnp.float32)
        Wx = jax.random.normal(k3, (D, 4 * H), dtype=jnp.float32) / math.sqrt(D)
        Wh = jax.random.normal(k4, (H, 4 * H), dtype=jnp.float32) / math.sqrt(H)
        b = jnp.zeros((4 * H,), dtype=jnp.float32)
        return {'x': x, 'h0': h0, 'Wx': Wx, 'Wh': Wh, 'b': b}
    _L0_cond_all = _L0_cond_setup()
    _L0_cond_in = {k: v for k, v in _L0_cond_all.items() if k in ('Wx', 'Wh', 'b')}
    del _L0_cond_all

    def _L0_attn_setup():
        import jax, jax.numpy as jnp
        import numpy as np
        B, N, D, H = (2, 512, 256, 8)
        HD = D // H
        EPS = 1e-06

        def _interleave(a, b):
            return jnp.stack([a, b], axis=2).reshape(a.shape[0], 2 * a.shape[1], a.shape[2], a.shape[3])

        def _l2norm(x):
            return x / jnp.sqrt(jnp.sum(x * x, axis=-1, keepdims=True) + EPS)

        def _dense_rnn(x, Wq, Wk, Wv, Wf1, Wf2, Wbeta, Wog1, Wog2, norm_w, Wo):
            b, n, d = x.shape
            q = jax.nn.silu(x @ Wq)
            k = jax.nn.silu(x @ Wk)
            v = jax.nn.silu(x @ Wv)
            f = x @ Wf1 @ Wf2
            log_f = jax.nn.log_sigmoid(f)
            beta = jax.nn.sigmoid(x @ Wbeta) * 2.0
            shp = (b, n, H, HD)
            q, k, v, log_f = (t.reshape(shp) for t in (q, k, v, log_f))
            k = _l2norm(k)
            k_ = -beta[..., None] * k
            zero = jnp.zeros(shp, x.dtype)
            gk = _interleave(log_f, zero)
            a = _interleave(k_ * jnp.exp(log_f), k_)
            bb = _interleave(k, k)
            kk = _interleave(zero, k)
            vv = _interleave(zero, v)
            qq = _interleave(zero, q)
            seq = tuple((jnp.moveaxis(t, 1, 0) for t in (gk, a, bb, kk, vv, qq)))
            S0 = jnp.zeros((b, H, HD, HD), x.dtype)

            def step(S, inp):
                g, a_t, b_t, k_t, v_t, q_t = inp
                bS = jnp.einsum('bhk,bhkv->bhv', b_t, S)
                S = jnp.exp(g)[..., None] * S + a_t[..., None] * bS[:, :, None, :] + k_t[..., None] * v_t[:, :, None, :]
                o = jnp.einsum('bhk,bhkv->bhv', q_t, S)
                return (S, o)
            _, o = jax.lax.scan(step, S0, seq)
            o = jnp.moveaxis(o, 0, 1)[:, 1::2]
            out = o.reshape(b, n, d)
            gate = x @ Wog1 @ Wog2
            y = out * jax.nn.sigmoid(gate)
            yh = y.reshape(b, n, H, HD)
            yh = yh / jnp.sqrt(jnp.mean(yh * yh, axis=-1, keepdims=True) + EPS)
            y = yh.reshape(b, n, d) * norm_w
            return y @ Wo
        key = jax.random.key(seed)
        ks = jax.random.split(key, 11)
        std = 0.02
        w = lambda k, shape: jax.random.normal(k, shape, dtype=jnp.float32) * std
        return {'x': jax.random.normal(ks[0], (B, N, D), dtype=jnp.float32), 'Wq': w(ks[1], (D, D)), 'Wk': w(ks[2], (D, D)), 'Wv': w(ks[3], (D, D)), 'Wf1': w(ks[4], (D, HD)), 'Wf2': w(ks[5], (HD, D)), 'Wbeta': w(ks[6], (D, H)), 'Wog1': w(ks[7], (D, HD)), 'Wog2': w(ks[8], (HD, D)), 'norm_w': jnp.ones((D,), dtype=jnp.float32), 'Wo': w(ks[9], (D, D))}
    _L0_attn_all = _L0_attn_setup()
    _L0_attn_in = {k: v for k, v in _L0_attn_all.items() if k in ('Wq', 'Wk', 'Wv', 'Wf1', 'Wf2', 'Wbeta', 'Wog1', 'Wog2', 'norm_w', 'Wo')}
    del _L0_attn_all

    def _L0_cond2_setup():
        import jax, jax.numpy as jnp
        import numpy as np
        N, T, D, H = (64, 64, 256, 256)
        key = jax.random.key(seed)
        k1, k2, k3, k4 = jax.random.split(key, 4)
        x = jax.random.normal(k1, (N, T, D), dtype=jnp.float32)
        h0 = jax.random.normal(k2, (N, H), dtype=jnp.float32)
        Wx = jax.random.normal(k3, (D, H), dtype=jnp.float32) / jnp.sqrt(jnp.float32(D))
        Wh = jax.random.normal(k4, (H, H), dtype=jnp.float32) / jnp.sqrt(jnp.float32(H))
        b = jnp.zeros((H,), dtype=jnp.float32)
        return {'x': x, 'h0': h0, 'Wx': Wx, 'Wh': Wh, 'b': b}
    _L0_cond2_all = _L0_cond2_setup()
    _L0_cond2_in = {k: v for k, v in _L0_cond2_all.items() if k in ('Wx', 'Wh', 'b')}
    del _L0_cond2_all

    def _L0_ffn_setup():
        import jax, jax.numpy as jnp
        import numpy as np
        B, S, D, H, E, K, F = (1, 256, 256, 16, 8, 2, 1024)

        def layernorm(x, g, b, eps=1e-05):
            m = x.mean(-1, keepdims=True)
            v = ((x - m) ** 2).mean(-1, keepdims=True)
            return (x - m) * jax.lax.rsqrt(v + eps) * g + b
        key = jax.random.key(seed)
        ks = jax.random.split(key, 8)
        n = lambda k, shape, sc: jax.random.normal(k, shape, dtype=jnp.float32) * sc
        return {'x': n(ks[0], (B, S, D), 1.0), 'w_qkv': n(ks[1], (D, 3 * D), D ** (-0.5)), 'w_o': n(ks[2], (D, D), D ** (-0.5)), 'g1': jnp.ones((D,), jnp.float32), 'b1': jnp.zeros((D,), jnp.float32), 'wg': n(ks[3], (D, E), D ** (-0.5)), 'w1': n(ks[4], (E, D, F), D ** (-0.5)), 'bb1': jnp.zeros((E, F), jnp.float32), 'w2': n(ks[5], (E, F, D), F ** (-0.5)), 'bb2': jnp.zeros((E, D), jnp.float32), 'g2': jnp.ones((D,), jnp.float32), 'b2': jnp.zeros((D,), jnp.float32)}
    _L0_ffn_all = _L0_ffn_setup()
    _L0_ffn_in = {k: v for k, v in _L0_ffn_all.items() if k in ('w_qkv', 'w_o', 'g1', 'b1', 'wg', 'w1', 'bb1', 'w2', 'bb2', 'g2', 'b2')}
    del _L0_ffn_all
    return {'x': x, 'cond_1024': cond_1024, 'L0_cond_Wx': _L0_cond_in['Wx'], 'L0_cond_Wh': _L0_cond_in['Wh'], 'L0_cond_b': _L0_cond_in['b'], 'L0_attn_Wq': _L0_attn_in['Wq'], 'L0_attn_Wk': _L0_attn_in['Wk'], 'L0_attn_Wv': _L0_attn_in['Wv'], 'L0_attn_Wf1': _L0_attn_in['Wf1'], 'L0_attn_Wf2': _L0_attn_in['Wf2'], 'L0_attn_Wbeta': _L0_attn_in['Wbeta'], 'L0_attn_Wog1': _L0_attn_in['Wog1'], 'L0_attn_Wog2': _L0_attn_in['Wog2'], 'L0_attn_norm_w': _L0_attn_in['norm_w'], 'L0_attn_Wo': _L0_attn_in['Wo'], 'L0_cond2_Wx': _L0_cond2_in['Wx'], 'L0_cond2_Wh': _L0_cond2_in['Wh'], 'L0_cond2_b': _L0_cond2_in['b'], 'L0_ffn_w_qkv': _L0_ffn_in['w_qkv'], 'L0_ffn_w_o': _L0_ffn_in['w_o'], 'L0_ffn_g1': _L0_ffn_in['g1'], 'L0_ffn_b1': _L0_ffn_in['b1'], 'L0_ffn_wg': _L0_ffn_in['wg'], 'L0_ffn_w1': _L0_ffn_in['w1'], 'L0_ffn_bb1': _L0_ffn_in['bb1'], 'L0_ffn_w2': _L0_ffn_in['w2'], 'L0_ffn_bb2': _L0_ffn_in['bb2'], 'L0_ffn_g2': _L0_ffn_in['g2'], 'L0_ffn_b2': _L0_ffn_in['b2']}

def reference(x, cond_1024, L0_cond_Wx, L0_cond_Wh, L0_cond_b, L0_attn_Wq, L0_attn_Wk, L0_attn_Wv, L0_attn_Wf1, L0_attn_Wf2, L0_attn_Wbeta, L0_attn_Wog1, L0_attn_Wog2, L0_attn_norm_w, L0_attn_Wo, L0_cond2_Wx, L0_cond2_Wh, L0_cond2_b, L0_ffn_w_qkv, L0_ffn_w_o, L0_ffn_g1, L0_ffn_b1, L0_ffn_wg, L0_ffn_w1, L0_ffn_bb1, L0_ffn_w2, L0_ffn_bb2, L0_ffn_g2, L0_ffn_b2):
    import jax
    import jax.numpy as jnp

    def _L0_cond_ref(x, h0, Wx, Wh, b):
        import jax, jax.numpy as jnp
        import numpy as np
        import math
        D = 256
        H = 256
        xz = jnp.einsum('ntd,dk->ntk', x, Wx) + b
        c0 = jnp.zeros_like(h0)

        def step(carry, xz_t):
            prev_h, prev_c = carry
            z = xz_t + prev_h @ Wh
            ai, af, ao, ag = jnp.split(z, 4, axis=1)
            i = jax.nn.sigmoid(ai)
            f = jax.nn.sigmoid(af)
            o = jax.nn.sigmoid(ao)
            g = jnp.tanh(ag)
            next_c = f * prev_c + i * g
            next_h = o * jnp.tanh(next_c)
            return ((next_h, next_c), next_h)
        _, hs = jax.lax.scan(step, (h0, c0), jnp.swapaxes(xz, 0, 1))
        return jnp.swapaxes(hs, 0, 1)

    def _L0_attn_ref(x, Wq, Wk, Wv, Wf1, Wf2, Wbeta, Wog1, Wog2, norm_w, Wo):
        import jax, jax.numpy as jnp
        import numpy as np
        B, N, D, H = (2, 512, 256, 8)
        HD = D // H
        EPS = 1e-06

        def _interleave(a, b):
            return jnp.stack([a, b], axis=2).reshape(a.shape[0], 2 * a.shape[1], a.shape[2], a.shape[3])

        def _l2norm(x):
            return x / jnp.sqrt(jnp.sum(x * x, axis=-1, keepdims=True) + EPS)

        def _dense_rnn(x, Wq, Wk, Wv, Wf1, Wf2, Wbeta, Wog1, Wog2, norm_w, Wo):
            b, n, d = x.shape
            q = jax.nn.silu(x @ Wq)
            k = jax.nn.silu(x @ Wk)
            v = jax.nn.silu(x @ Wv)
            f = x @ Wf1 @ Wf2
            log_f = jax.nn.log_sigmoid(f)
            beta = jax.nn.sigmoid(x @ Wbeta) * 2.0
            shp = (b, n, H, HD)
            q, k, v, log_f = (t.reshape(shp) for t in (q, k, v, log_f))
            k = _l2norm(k)
            k_ = -beta[..., None] * k
            zero = jnp.zeros(shp, x.dtype)
            gk = _interleave(log_f, zero)
            a = _interleave(k_ * jnp.exp(log_f), k_)
            bb = _interleave(k, k)
            kk = _interleave(zero, k)
            vv = _interleave(zero, v)
            qq = _interleave(zero, q)
            seq = tuple((jnp.moveaxis(t, 1, 0) for t in (gk, a, bb, kk, vv, qq)))
            S0 = jnp.zeros((b, H, HD, HD), x.dtype)

            def step(S, inp):
                g, a_t, b_t, k_t, v_t, q_t = inp
                bS = jnp.einsum('bhk,bhkv->bhv', b_t, S)
                S = jnp.exp(g)[..., None] * S + a_t[..., None] * bS[:, :, None, :] + k_t[..., None] * v_t[:, :, None, :]
                o = jnp.einsum('bhk,bhkv->bhv', q_t, S)
                return (S, o)
            _, o = jax.lax.scan(step, S0, seq)
            o = jnp.moveaxis(o, 0, 1)[:, 1::2]
            out = o.reshape(b, n, d)
            gate = x @ Wog1 @ Wog2
            y = out * jax.nn.sigmoid(gate)
            yh = y.reshape(b, n, H, HD)
            yh = yh / jnp.sqrt(jnp.mean(yh * yh, axis=-1, keepdims=True) + EPS)
            y = yh.reshape(b, n, d) * norm_w
            return y @ Wo
        return _dense_rnn(x, Wq, Wk, Wv, Wf1, Wf2, Wbeta, Wog1, Wog2, norm_w, Wo)

    def _L0_cond2_ref(x, h0, Wx, Wh, b):
        import jax, jax.numpy as jnp
        import numpy as np
        N, T, D, H = (64, 64, 256, 256)
        xW = jnp.einsum('ntd,dh->nth', x, Wx) + b

        def step(prev_h, xw_t):
            next_h = jnp.tanh(xw_t + prev_h @ Wh)
            return (next_h, next_h)
        _, hs = jax.lax.scan(step, h0, jnp.swapaxes(xW, 0, 1))
        return jnp.swapaxes(hs, 0, 1)

    def _L0_ffn_ref(x, w_qkv, w_o, g1, b1, wg, w1, bb1, w2, bb2, g2, b2):
        import jax, jax.numpy as jnp
        import numpy as np
        B, S, D, H, E, K, F = (1, 256, 256, 16, 8, 2, 1024)

        def layernorm(x, g, b, eps=1e-05):
            m = x.mean(-1, keepdims=True)
            v = ((x - m) ** 2).mean(-1, keepdims=True)
            return (x - m) * jax.lax.rsqrt(v + eps) * g + b
        b, s, d = x.shape
        hd = d // H
        qkv = x @ w_qkv
        q, k, v = jnp.split(qkv, 3, axis=-1)
        to_heads = lambda t: t.reshape(b, s, H, hd).transpose(0, 2, 1, 3)
        q, k, v = (to_heads(q), to_heads(k), to_heads(v))
        scores = jnp.einsum('bhqd,bhkd->bhqk', q, k) / jnp.sqrt(jnp.float32(hd))
        causal = jnp.tril(jnp.ones((s, s), bool))
        scores = jnp.where(causal, scores, jnp.finfo(scores.dtype).min)
        attn = jax.nn.softmax(scores, axis=-1)
        o = jnp.einsum('bhqk,bhkd->bhqd', attn, v)
        o = o.transpose(0, 2, 1, 3).reshape(b, s, d) @ w_o
        h = layernorm(x + o, g1, b1)
        probs = jax.nn.softmax(h @ wg, axis=-1)
        topv, topi = jax.lax.top_k(probs, K)
        topv = topv / topv.sum(-1, keepdims=True)
        w = (topv[..., None] * jax.nn.one_hot(topi, E, dtype=h.dtype)).sum(-2)
        h1 = jax.nn.gelu(jnp.einsum('bsd,edf->ebsf', h, w1) + bb1[:, None, None, :])
        y = jnp.einsum('ebsf,efd->ebsd', h1, w2) + bb2[:, None, None, :]
        moe = jnp.einsum('ebsd,bse->bsd', y, w)
        return layernorm(h + moe, g2, b2)
    x = x + _L0_attn_ref(_L0_cond_ref(x, cond_1024, L0_cond_Wx, L0_cond_Wh, L0_cond_b), L0_attn_Wq, L0_attn_Wk, L0_attn_Wv, L0_attn_Wf1, L0_attn_Wf2, L0_attn_Wbeta, L0_attn_Wog1, L0_attn_Wog2, L0_attn_norm_w, L0_attn_Wo)
    x = x + _L0_ffn_ref(_L0_cond2_ref(x, cond_1024, L0_cond2_Wx, L0_cond2_Wh, L0_cond2_b), L0_ffn_w_qkv, L0_ffn_w_o, L0_ffn_g1, L0_ffn_b1, L0_ffn_wg, L0_ffn_w1, L0_ffn_bb1, L0_ffn_w2, L0_ffn_bb2, L0_ffn_g2, L0_ffn_b2)
    return x

_drawn_inputs = setup_inputs


def setup_inputs(seed=0):
    import zlib

    import numpy as np

    out = dict(_drawn_inputs(seed))
    spreads = {'L0_cond_b': (0.0, 0.1),
     'L0_attn_norm_w': (1.0, 0.2),
     'L0_cond2_b': (0.0, 0.1),
     'L0_ffn_g1': (1.0, 0.2),
     'L0_ffn_b1': (0.0, 0.1),
     'L0_ffn_bb1': (0.0, 0.1),
     'L0_ffn_bb2': (0.0, 0.1),
     'L0_ffn_g2': (1.0, 0.2),
     'L0_ffn_b2': (0.0, 0.1)}
    factors = {'L0_attn_Wf1': 8.0,
     'L0_attn_Wf2': 8.0,
     'L0_attn_Wbeta': 32.891,
     'L0_attn_Wog1': 8.0,
     'L0_attn_Wog2': 8.0}
    for name, (base, spread) in spreads.items():
        noise = np.random.default_rng([zlib.crc32(name.encode()), seed]).standard_normal(out[name].shape)
        drawn = base * np.exp(spread * noise) if base else spread * noise
        out[name] = jnp.asarray(drawn.astype(out[name].dtype))
    for name, factor in factors.items():
        out[name] = (out[name] * factor).astype(out[name].dtype)
    return out
```

```python
import concourse.bass as bass
from concourse import mybir
from contextlib import ExitStack

f32 = mybir.dt.float32
f16 = mybir.dt.float16
bf16 = mybir.dt.bfloat16
i32 = mybir.dt.int32
ALU = mybir.AluOpType
ACT = mybir.ActivationFunctionType
AX = mybir.AxisListType

B, T, D = 2, 1024, 256
TOK = B * T
KT = D // 128
G4 = 4 * D
NB = TOK // 512
RH, RD = 8, 32
AH, AD = 16, 16
EX, FF = 8, 1024
FT = FF // 128
HS = 1024.0


class Core:

    def __init__(self, nc, args, stack):
        self.nc = nc
        self.a = args
        self.stack = stack

    def sb(self, name, shape, dt=f32, stack=None):
        return (stack or self.stack).enter_context(self.nc.sbuf_tensor(name, shape, dt))

    def pb(self, name, stack, n=512, dt=f32):
        return stack.enter_context(self.nc.psum_tensor(name, [128, n], dt))

    def sem(self, name):
        return self.stack.enter_context(self.nc.semaphore(name))


def col(v):
    return v.rearrange("(k p) -> p k", p=128)


def blk(t, n, size=512):
    return t[:, n * size:(n + 1) * size]


def phase_load(c):
    nc, a = c.nc, c.a
    st = ExitStack()
    with st:
        xin = c.sb("x_rows", [128, 2, T // 128, D], f32, st)
        wx = c.sb("lstm_Wx", [128, KT, G4], f32, st)
        wsc = c.sb("lstm_Wh_scaled", [128, KT, G4], f32, st)
        wbig = c.sb("wh_absmax", [128, 2], f32, st)
        wrow = c.sb("wh_absmax_row", [1, 2, 128], f32, st)
        wmax = c.sb("wh_scale_row", [1, 4], f32, st)
        scl = c.sb("wh_scale", [128, 2], f32, st)
        wr2 = c.sb("rnn_Wh_scaled", [128, KT, D], f32, st)
        bias = c.sb("lstm_b", [128, G4 // 128], f32, st)
        pt = [c.pb(f"x_turned{i}", st) for i in range(2)]
        pz = [c.pb(f"xz_psum{i}", st) for i in range(2)]
        pm = c.pb("absmax_turned", st)
        ps = c.pb("scale_spread", st)
        s_x, s_w, s_b = c.sem("x_loaded"), c.sem("weights_loaded"), c.sem("bias_loaded")
        s_c, s_t, s_e = c.sem("constants_made"), c.sem("x_turned"), c.sem("x_evacuated")
        s_m, s_mt, s_md = c.sem("absmax_made"), c.sem("absmax_turned_s"), c.sem("scale_row_made")
        s_sp, s_sd, s_z, s_ze = c.sem("scale_spread_s"), c.sem("split_step"), c.sem("xz_made"), c.sem("xz_evacuated")
        s_g = c.sem("pool_step")
        xz = c.xz
        with nc.Block() as block:
            @block.sync
            def _(sp):
                for b in range(B):
                    sp.dma_start(xin[:, b], a["x"][b].rearrange("(i p) c -> p i c", p=128)).then_inc(s_x, 16)
                sp.dma_start(wx[:], a["L0_cond_Wx"].rearrange("(k p) n -> p k n", p=128)).then_inc(s_w, 16)
                sp.dma_start(c.wh[:], a["L0_cond_Wh"].rearrange("(k p) n -> p k n", p=128)).then_inc(s_w, 16)
                sp.dma_start(c.wh2[:], a["L0_cond2_Wh"].rearrange("(k p) n -> p k n", p=128)).then_inc(s_w, 16)
                with nc.allow_non_contiguous_dma("small vectors"):
                    sp.dma_start(bias[:], col(a["L0_cond_b"])).then_inc(s_b, 16)
                    for k in range(KT):
                        sp.dma_start(c.h0[:, k, :], a["cond_1024"][:, k * 128:(k + 1) * 128].rearrange("b p -> p b"))\
                          .then_inc(s_b, 16)

            @block.gpsimd
            def _(pool):
                pool.memset(c.ident[:], 0.0).then_inc(s_g, 1)
                pool.memset(c.headones[:], 1.0).then_inc(s_g, 1)
                pool.memset(c.ones[:], 1.0).then_inc(s_c, 1)
                pool.wait_ge(s_g, 2)
                pool.affine_select(out=c.ident[:], in_=c.ident[:], compare_op=ALU.not_equal, fill=1.0, base=0,
                                   pattern=[[-1, 128]], channel_multiplier=1).then_inc(s_c, 1)
                hv = c.headones[:].rearrange("p (h q) -> p h q", q=32)
                pool.affine_select(out=hv, in_=hv, compare_op=ALU.is_ge, fill=0.0, base=0,
                                   pattern=[[-32, 4], [0, 32]], channel_multiplier=1).then_inc(s_g, 1)
                pool.wait_ge(s_g, 3)
                pool.affine_select(out=hv, in_=hv, compare_op=ALU.is_ge, fill=0.0, base=31,
                                   pattern=[[32, 4], [0, 32]], channel_multiplier=-1).then_inc(s_c, 1)

            @block.tensor
            def _(pe):
                pe.wait_ge(s_c, 3)
                pe.wait_ge(s_x, 16 * B)
                n = 0
                for b in range(B):
                    for k in range(KT):
                        for half in range(2):
                            if n >= 2:
                                pe.wait_ge(s_e, n - 1)
                            for j in range(4):
                                mm = pe.transpose(pt[n % 2][:, j * 128:(j + 1) * 128],
                                                  xin[:, b, half * 4 + j, k * 128:(k + 1) * 128], c.ident[:])
                            mm.then_inc(s_t, 1)
                            n += 1
                pe.wait_ge(s_m, 2)
                for w in range(2):
                    mm = pe.transpose(pm[0:1, w * 128:(w + 1) * 128], wbig[:, w:w + 1], c.ident[:])
                mm.then_inc(s_mt, 1)
                pe.wait_ge(s_md, 5)
                pe.matmul(ps[:, 0:4], c.ones[0:1, :], wmax[0:1, :], start=True, stop=True).then_inc(s_sp, 1)
                pe.wait_ge(s_w, 48)
                pe.wait_ge(s_e, 8)
                for q in range(G4 // 128):
                    for n in range(NB):
                        u = q * NB + n
                        if u >= 2:
                            pe.wait_ge(s_ze, u - 1)
                        for k in range(KT):
                            mm = pe.matmul(pz[u % 2][:], wx[:, k, q * 128:(q + 1) * 128], blk(c.xT[:, k], n),
                                           start=(k == 0), stop=(k == KT - 1))
                        mm.then_inc(s_z, 1)

            @block.vector
            def _(v):
                n = 0
                for b in range(B):
                    for k in range(KT):
                        for half in range(2):
                            v.wait_ge(s_t, n + 1)
                            dst = c.xT[:, k, :].rearrange("p (t b) -> p b t", b=B)[:, b, half * 512:(half + 1) * 512]
                            v.tensor_copy(dst, pt[n % 2][:]).then_inc(s_e, 1)
                            n += 1
                v.wait_ge(s_w, 48)
                for w, t in enumerate((c.wh, c.wh2)):
                    v.tensor_reduce(wbig[:, w:w + 1], t[:], AX.XY, ALU.max, apply_absolute_value=True).then_inc(s_m, 1)
                v.wait_ge(s_mt, 1)
                v.tensor_copy(wrow[0:1].rearrange("p a b -> p (a b)"), pm[0:1, 0:256]).then_inc(s_md, 1)
                v.wait_ge(s_md, 1)
                v.tensor_reduce(wmax[0:1, 0:2], wrow[0:1], AX.X, ALU.max).then_inc(s_md, 1)
                v.wait_ge(s_md, 2)
                v.tensor_scalar(wmax[0:1, 2:4], wmax[0:1, 0:2], 1e-30, None, ALU.max).then_inc(s_md, 1)
                v.wait_ge(s_md, 3)
                v.tensor_scalar(wmax[0:1, 0:2].bitcast(i32), wmax[0:1, 2:4].bitcast(i32), 0x7F800000, None,
                                ALU.bitwise_and).then_inc(s_md, 1)
                v.wait_ge(s_md, 4)
                v.reciprocal(wmax[0:1, 2:4], wmax[0:1, 0:2]).then_inc(s_md, 1)
                v.wait_ge(s_sp, 1)
                v.tensor_scalar(scl[:], ps[:, 2:4], 2.0 ** 14, None, ALU.mult).then_inc(s_sd, 1)
                v.tensor_scalar(c.unscale[:], ps[:, 0:2], 2.0 ** -14 / HS, None, ALU.mult).then_inc(s_sd, 1)
                v.wait_ge(s_sd, 2)
                for w, (src, big, wa, wb) in enumerate(((c.wh, wsc, c.wa, c.wb), (c.wh2, wr2, c.wa2, c.wb2))):
                    v.tensor_scalar(big[:], src[:], scl[:, w:w + 1], None, ALU.mult).then_inc(s_sd, 1)
                    v.wait_ge(s_sd, 3 + 3 * w)
                    v.tensor_copy(wa[:], big[:]).then_inc(s_sd, 1)
                    v.wait_ge(s_sd, 4 + 3 * w)
                    v.tensor_tensor(wb[:], big[:], wa[:], ALU.subtract).then_inc(s_sd, 1)
                v.wait_ge(s_sd, 8)

            @block.scalar
            def _(act):
                act.wait_ge(s_b, 48)
                order = {3: 0, 0: 1, 1: 2, 2: 3}
                for q in range(G4 // 128):
                    for n in range(NB):
                        u = q * NB + n
                        act.wait_ge(s_z, u + 1)
                        m = order[q // 2] * 2 + q % 2
                        dst = xz[:, n * 256:(n + 1) * 256, m, :]
                        act.activation(dst, pz[u % 2][:].rearrange("p (t b) -> p t b", b=B), ACT.Identity,
                                       bias=bias[:, q:q + 1]).then_inc(s_ze, 1)


def phase_lstm(c):
    nc = c.nc
    st = ExitStack()
    with st:
        ha = c.sb("h_high", [128, KT, B], f16, st)
        hb = c.sb("h_low", [128, KT, B], f16, st)
        hf = c.sb("h_scaled", [128, KT * B], f32, st)
        z = c.sb("z", [128, 16], f32, st)
        tg = c.sb("tanh_g", [128, 4], f32, st)
        sif = c.sb("sig_if", [128, 8], f32, st)
        so = c.sb("sig_o", [128, 4], f32, st)
        cc = c.sb("cell", [128, 4], f32, st)
        fc = c.sb("f_cell", [128, 4], f32, st)
        ig = c.sb("i_g", [128, 4], f32, st)
        tc = c.sb("tanh_cell", [128, 4], f32, st)
        pg = c.pb("z_gif", st)
        po = c.pb("z_o", st)
        s_c0, s_gif, s_o = c.sem("cell_zeroed"), c.sem("gif_made"), c.sem("o_made")
        s_z, s_zo, s_g, s_if, s_so = (c.sem(n) for n in ("z_gif_s", "z_o_s", "tanh_g_s", "sig_if_s", "sig_o_s"))
        s_fc, s_c, s_tc = c.sem("cell_parts"), c.sem("cell_made"), c.sem("tanh_cell_s")
        s_ha, s_hf, s_hb, s_h = c.sem("h_high_s"), c.sem("h_scaled_s"), c.sem("h_low_s"), c.sem("h_stored")
        xz = c.xz[:].rearrange("p t m b -> p t (m b)")
        gates = [("g", 3, 0), ("i", 0, 1), ("f", 1, 2), ("o", 2, 3)]
        with nc.Block() as block:
            @block.tensor
            def _(pe):
                def out(place, m):
                    bank, at = (po, 0) if place == 3 else (pg, place * 4)
                    return bank[:, at + 2 * m:at + 2 * m + 2]

                def w(t, q, m, k):
                    return t[:, k, (2 * q + m) * 128:(2 * q + m + 1) * 128]

                for group, done in ((gates[:3], s_gif), (gates[3:], s_o)):
                    first = True
                    for _, q, place in group:
                        for m in range(2):
                            for k in range(KT):
                                mm = pe.matmul(out(place, m), w(c.wh, q, m, k), c.h0[:, k, :], start=first,
                                               stop=(place >= 2 and m == 1 and k == 1))
                                first = False
                    mm.then_inc(done, 1)

                with pe.Fori(1, T) as t:
                    pe.wait_ge(s_ha, t)
                    for group, done in ((gates[:3], s_gif), (gates[3:], s_o)):
                        first = True
                        for _, q, place in group:
                            for m in range(2):
                                for k in range(KT):
                                    for part in (c.wa, c.wb):
                                        pe.matmul(out(place, m), w(part, q, m, k), ha[:, k, :], start=first, stop=False)
                                        first = False
                        if done is s_gif:
                            pe.wait_ge(s_hb, t)
                        for _, q, place in group:
                            for m in range(2):
                                for k in range(KT):
                                    mm = pe.matmul(out(place, m), w(c.wa, q, m, k), hb[:, k, :], start=False,
                                                   stop=(place >= 2 and m == 1 and k == 1))
                        mm.then_inc(done, 1)

            @block.scalar
            def _(act):
                act.activation(tc[:], c.ones[:, 0:4], ACT.Sigmoid)
                def step(t, first):
                    act.wait_ge(s_z, t + 1)
                    act.activation(sif[:], z[:, 4:12], ACT.Sigmoid).then_inc(s_if, 1)
                    act.activation(tg[:], z[:, 0:4], ACT.Tanh).then_inc(s_g, 1)
                    act.wait_ge(s_zo, t + 1)
                    if not first:
                        act.wait_ge(s_h, t)
                    act.activation(so[:], z[:, 12:16], ACT.Sigmoid).then_inc(s_so, 1)
                    act.wait_ge(s_c, t + 1)
                    act.activation(tc[:], cc[:], ACT.Tanh).then_inc(s_tc, 1)

                step(0, True)
                with act.Fori(1, T) as t:
                    step(t, False)

            @block.vector
            def _(v):
                v.memset(cc[:], 0.0).then_inc(s_c0, 1)
                v.wait_ge(s_c0, 1)

                def step(t, first):
                    v.wait_ge(s_gif, t + 1)
                    if first:
                        v.tensor_tensor(z[:, 0:12], pg[:, 0:12], xz[:, 0, 0:12], ALU.add).then_inc(s_z, 1)
                    else:
                        v.scalar_tensor_tensor(z[:, 0:12], pg[:, 0:12], c.unscale[:, 0:1], xz[:, t, 0:12],
                                               ALU.mult, ALU.add).then_inc(s_z, 1)
                    v.wait_ge(s_o, t + 1)
                    if first:
                        v.tensor_tensor(z[:, 12:16], po[:, 0:4], xz[:, 0, 12:16], ALU.add).then_inc(s_zo, 1)
                    else:
                        v.scalar_tensor_tensor(z[:, 12:16], po[:, 0:4], c.unscale[:, 0:1], xz[:, t, 12:16],
                                               ALU.mult, ALU.add).then_inc(s_zo, 1)
                    v.wait_ge(s_if, t + 1)
                    v.tensor_tensor(fc[:], sif[:, 4:8], cc[:], ALU.mult).then_inc(s_fc, 1)
                    v.wait_ge(s_g, t + 1)
                    v.tensor_tensor(ig[:], sif[:, 0:4], tg[:], ALU.mult).then_inc(s_fc, 1)
                    v.wait_ge(s_fc, 2 * t + 2)
                    v.tensor_tensor(cc[:], fc[:], ig[:], ALU.add).then_inc(s_c, 1)
                    v.wait_ge(s_tc, t + 1)
                    v.scalar_tensor_tensor(ha[:].rearrange("p k b -> p (k b)"), so[:], HS, tc[:],
                                           ALU.mult, ALU.mult).then_inc(s_ha, 1)
                    v.scalar_tensor_tensor(hf[:], so[:], HS, tc[:], ALU.mult, ALU.mult).then_inc(s_hf, 1)
                    v.wait_ge(s_hf, t + 1)
                    v.tensor_tensor(hb[:].rearrange("p k b -> p (k b)"), hf[:], ha[:].rearrange("p k b -> p (k b)"),
                                    ALU.subtract).then_inc(s_hb, 1)

                step(0, True)
                with v.Fori(1, T) as t:
                    step(t, False)

            @block.gpsimd
            def _(pool):
                with pool.Fori(0, T) as t:
                    pool.wait_ge(s_tc, t + 1)
                    pool.tensor_tensor(c.hT[:, :, bass.ds(t * B, B)], so[:].rearrange("p (k b) -> p k b", b=B),
                                       tc[:].rearrange("p (k b) -> p k b", b=B), ALU.mult).then_inc(s_h, 1)


def phase_project(c):
    nc, a = c.nc, c.a
    st = ExitStack()
    with st:
        used = [0]

        def room(*shape):
            size = 1
            for s in shape:
                size *= s
            t = c.room[:, used[0]:used[0] + size]
            used[0] += size
            names = "abc"[:len(shape)]
            inner = " ".join(names)
            return t.rearrange(f"p ({inner}) -> p {inner}", **dict(zip(names, shape))) if len(shape) > 1 else t

        wq, wk, wv = (room(KT, D) for _ in range(3))
        wf1 = room(KT, RD)
        wf2 = room(D)[0:RD]
        wb0 = room(KT, RH)
        wb = room(KT, RH, RD)
        f1 = room(512)[0:RD]
        sk, sv, sq, sbt = (room(512) for _ in range(4))
        fd = room(512)
        kk, t1, t2, kn, w = (room(512) for _ in range(5))
        pk, pv, pq, pf, pb, ps, pf1 = (c.pb(n, st) for n in
                                       ("k_psum", "v_psum", "q_psum", "f_psum", "beta_psum", "sum_psum", "f1_psum"))
        s_w, s_spread = c.sem("delta_weights"), c.sem("beta_spread")
        s_p, s_f1, s_f1e = c.sem("projected"), c.sem("f1_made"), c.sem("f1_evacuated")
        s_sig, s_d, s_ss, s_rt, s_gm = (c.sem(n) for n in
                                        ("gated", "project_dve", "square_sum", "norm_root", "gamma_made"))
        s_done, s_y = c.sem("unit_done"), c.sem("y_part")
        with nc.Block() as block:
            @block.sync
            def _(sp):
                for t, n in ((wq, "Wq"), (wk, "Wk"), (wv, "Wv"), (wf1, "Wf1"), (wb0, "Wbeta")):
                    sp.dma_start(t[:], a["L0_attn_" + n].rearrange("(k p) n -> p k n", p=128)).then_inc(s_w, 16)
                sp.dma_start(wf2[:], a["L0_attn_Wf2"]).then_inc(s_w, 16)

            @block.gpsimd
            def _(pool):
                pool.wait_ge(s_w, 96)
                pool.tensor_copy(wb[:], wb0[:].rearrange("p k (h o) -> p k h o", o=1).to_broadcast([128, KT, RH, RD]))\
                    .then_inc(s_spread, 1)

            @block.tensor
            def _(pe):
                pe.wait_ge(s_w, 96)
                pe.wait_ge(s_spread, 1)

                def unit(n, m, u, first):
                    rows = [c.hT[:, k, bass.ds(n * 512, 512)] for k in range(KT)]
                    if not first:
                        pe.wait_ge(s_done, u)
                    if m == 0:
                        for k in range(KT):
                            mm = pe.matmul(pf1[0:RD, :], wf1[:, k, :], rows[k], start=(k == 0), stop=(k == KT - 1))
                        mm.then_inc(s_f1, 1)
                    for bank, wt in ((pk, wk), (pv, wv), (pq, wq)):
                        for k in range(KT):
                            pe.matmul(bank[:], wt[:, k, m * 128:(m + 1) * 128], rows[k],
                                      start=(k == 0), stop=(k == KT - 1))
                    for k in range(KT):
                        pe.matmul(pb[:], wb[:, k, m * 4:(m + 1) * 4, :].rearrange("p h r -> p (h r)"), rows[k],
                                  start=(k == 0), stop=(k == KT - 1))
                    pe.wait_ge(s_f1e, n + 1)
                    pe.matmul(pf[:], wf2[:, m * 128:(m + 1) * 128], f1[:], start=True, stop=True).then_inc(s_p, 1)
                    pe.wait_ge(s_d, 11 * u + 4)
                    pe.matmul(ps[:], c.headones[:], t1[:], start=True, stop=True).then_inc(s_ss, 1)
                    pe.wait_ge(s_d, 11 * u + 9)
                    pe.matmul(ps[:], c.headones[:], t1[:], start=True, stop=True).then_inc(s_gm, 1)

                for m in range(2):
                    unit(0, m, m, m == 0)
                with pe.Fori(1, NB) as n:
                    for m in range(2):
                        unit(n, m, n * 2 + m, False)

            @block.scalar
            def _(act):
                with act.Fori(0, NB) as n:
                    for m in range(2):
                        u = n * 2 + m
                        if m == 0:
                            act.wait_ge(s_f1, n + 1)
                            act.activation(f1[:], pf1[0:RD, :], ACT.Copy).then_inc(s_f1e, 1)
                        act.wait_ge(s_p, u + 1)
                        for dst, src in ((sk, pk), (sv, pv), (sq, pq), (sbt, pb), (fd, pf)):
                            act.activation(dst[:], src[:], ACT.Sigmoid).then_inc(s_sig, 1)
                        act.wait_ge(s_d, 11 * u + 6)
                        act.activation(t1[:], t2[:], ACT.Sqrt).then_inc(s_rt, 1)

            @block.vector
            def _(v):
                v.tensor_reduce(c.diag[:], c.ident[:].rearrange("p (h v) -> p v h", v=32), AX.X, ALU.add)
                v.tensor_scalar(c.negones[:], c.headones[:], -1.0, None, ALU.mult)
                with v.Fori(0, NB) as n:
                    for m in range(2):
                        u = n * 2 + m
                        d = 11 * u

                        def tile(t, j=0, width=4):
                            return t[:, bass.ds(n * 256, 256), j * 4 + m * 2:j * 4 + m * 2 + 2]

                        def tb(t):
                            return t[:].rearrange("p (t b) -> p t b", b=B)

                        v.wait_ge(s_sig, 5 * u + 5)
                        v.tensor_tensor(kk[:], pk[:], sk[:], ALU.mult).then_inc(s_d, 1)
                        v.tensor_tensor(tile(c.v), tb(pv), tb(sv), ALU.mult).then_inc(s_d, 1)
                        v.tensor_tensor(tile(c.q), tb(pq), tb(sq), ALU.mult).then_inc(s_d, 1)
                        v.wait_ge(s_d, d + 1)
                        v.tensor_tensor(t1[:], kk[:], kk[:], ALU.mult).then_inc(s_d, 1)
                        v.wait_ge(s_ss, u + 1)
                        v.tensor_scalar(t2[:], ps[:], 1e-6, None, ALU.add).then_inc(s_d, 1)
                        v.wait_ge(s_d, d + 5)
                        v.reciprocal(t2[:], t2[:]).then_inc(s_d, 1)
                        v.wait_ge(s_rt, u + 1)
                        v.tensor_tensor(kn[:], kk[:], t1[:], ALU.mult).then_inc(s_d, 1)
                        v.wait_ge(s_d, d + 7)
                        v.tensor_tensor(w[:], fd[:], kn[:], ALU.mult).then_inc(s_d, 1)
                        v.wait_ge(s_d, d + 8)
                        v.tensor_tensor(t1[:], kn[:], w[:], ALU.mult).then_inc(s_d, 1)
                        v.tensor_copy(tile(c.kyk, 0), tb(kn))
                        v.tensor_copy(tile(c.kyk, 2), tb(kn))
                        v.tensor_copy(tile(c.f), tb(fd))
                        v.tensor_tensor(sk[:], sbt[:], kn[:], ALU.mult).then_inc(s_d, 1)
                        v.scalar_tensor_tensor(sv[:], sbt[:], 2.0, w[:], ALU.mult, ALU.mult)
                        v.wait_ge(s_d, d + 10)
                        v.tensor_tensor(sq[:], sk[:], sbt[:], ALU.mult).then_inc(s_d, 1)
                        v.wait_ge(s_gm, u + 1)
                        v.wait_ge(s_d, d + 11)
                        v.scalar_tensor_tensor(t2[:], ps[:], 2.0, sq[:], ALU.mult, ALU.mult).then_inc(s_y, 1)
                        v.wait_ge(s_y, u + 1)
                        v.tensor_tensor(tile(c.kyk, 1), tb(sv), tb(t2), ALU.subtract).then_inc(s_done, 1)


def phase_delta(c):
    nc = c.nc
    st = ExitStack()
    with st:
        S = [c.sb(f"state{i}", [128, 4, RD], f32, st) for i in range(2)]
        prod = c.sb("k_and_y_times_state", [128, 2, 4, RD], f32, st)
        ds = c.sb("decayed_state", [128, 4, RD], f32, st)
        p2 = c.sb("updates", [128, 2, 4, RD], f32, st)
        s1 = c.sb("half_updated", [128, 4, RD], f32, st)
        vd = [c.sb(f"v_on_diagonal{i}", [128, 4, RD], f32, st) for i in range(2)]
        qs = [c.sb(f"q_per_head{i}", [128, 4, 4], f32, st) for i in range(2)]
        pu = [c.pb(f"projections_of_state{i}", st) for i in range(2)]
        po = [c.pb(f"o_psum{i}", st) for i in range(2)]
        s_0, s_S, s_prod, s_ds, s_p2, s_h = (c.sem(n) for n in
                                             ("state_zeroed", "state_made", "prod_made", "decayed", "updates_made",
                                              "half_made"))
        s_u, s_vd, s_q, s_o, s_oe = (c.sem(n) for n in ("u_made", "vd_made", "qs_made", "o_made_s", "o_evacuated"))
        shape = [128, 4, RD]
        with nc.Block() as block:
            def two_by_two(eng, step):
                for t in range(2):
                    step(t, t, t)
                with eng.Fori(1, T // 2) as i:
                    for j in range(2):
                        step(i * 2 + j, j, 2)

            @block.vector
            def _(v):
                v.memset(S[0][:], 0.0).then_inc(s_0, 1)
                v.wait_ge(s_0, 1)

                def step(t, j, age):
                    old, new = S[j], S[1 - j]
                    ky = c.kyk[:, t:t + 1, 0:8] if age < 2 else c.kyk[:, bass.ds(t, 1), 0:8]
                    yk = c.kyk[:, t:t + 1, 4:12] if age < 2 else c.kyk[:, bass.ds(t, 1), 4:12]
                    f = c.f[:, t:t + 1, :] if age < 2 else c.f[:, bass.ds(t, 1), :]
                    if age:
                        v.wait_ge(s_S, t)
                    for half in range(2):
                        last = v.tensor_tensor(prod[:, half], old[:],
                                        ky[:, :, half * 4:half * 4 + 4].rearrange("p o g -> p g o").to_broadcast(shape),
                                        ALU.mult)
                    last.then_inc(s_prod, 1)
                    v.tensor_tensor(ds[:], old[:], f.rearrange("p o g -> p g o").to_broadcast(shape), ALU.mult)\
                        .then_inc(s_ds, 1)
                    v.wait_ge(s_u, t + 1)
                    v.tensor_tensor(p2[:].rearrange("p a g v -> p (a g) v"),
                                    pu[j][:, 0:256].rearrange("p (g v) -> p g v", v=RD),
                                    yk.rearrange("p o g -> p g o").to_broadcast([128, 8, RD]), ALU.mult)\
                        .then_inc(s_p2, 1)
                    v.wait_ge(s_p2, t + 1)
                    v.tensor_tensor(s1[:], ds[:], p2[:, 0], ALU.subtract).then_inc(s_h, 1)
                    v.wait_ge(s_h, t + 1)
                    if age == 2:
                        v.wait_ge(s_o, t - 1)
                    v.tensor_tensor(new[:], s1[:], p2[:, 1], ALU.subtract).then_inc(s_S, 1)

                two_by_two(v, step)

            @block.tensor
            def _(pe):
                def o_of(t, j, old):
                    pe.wait_ge(s_q, t + 1)
                    if old:
                        pe.wait_ge(s_oe, t - 1)
                    for g in range(4):
                        mm = pe.matmul(po[j][0:RD, g * 4:(g + 1) * 4], S[1 - j][:, g, :], qs[j][:, g, :],
                                       start=(g == 0), stop=(g == 3))
                    mm.then_inc(s_o, 1)

                def step(t, j, age):
                    pe.wait_ge(s_vd, t + 1)
                    if age == 2:
                        pe.wait_ge(s_p2, t - 1)
                    pe.matmul(pu[j][:, 128:256], c.negones[:], vd[j][:].rearrange("p g v -> p (g v)"),
                              start=True, stop=True, skip_group_check=True)
                    pe.wait_ge(s_prod, t + 1)
                    pe.matmul(pu[j][:, 0:256], c.headones[:], prod[:].rearrange("p a g v -> p (a g v)"),
                              start=False, stop=True, skip_group_check=True).then_inc(s_u, 1)

                for t in range(4):
                    step(t, t % 2, min(t, 2))
                    if t:
                        o_of(t - 1, (t - 1) % 2, t - 1 >= 2)
                with pe.Fori(2, T // 2) as i:
                    for j in range(2):
                        step(i * 2 + j, j, 2)
                        o_of(i * 2 + (j - 1), 1 - j, True)
                pe.wait_ge(s_S, T)
                o_of(T - 1, 1, True)

            @block.gpsimd
            def _(pool):
                def step(t, j, age):
                    vt = c.v[:, t:t + 1, :] if age < 2 else c.v[:, bass.ds(t, 1), :]
                    qt = c.q[:, t:t + 1, :] if age < 2 else c.q[:, bass.ds(t, 1), :]
                    if age == 2:
                        pool.wait_ge(s_u, t - 1)
                    pool.tensor_tensor(vd[j][:], vt.rearrange("p o g -> p g o").to_broadcast(shape),
                                       c.diag[:].rearrange("p (o v) -> p o v", o=1).to_broadcast(shape), ALU.mult)\
                        .then_inc(s_vd, 1)
                    if age == 2:
                        pool.wait_ge(s_o, t - 1)
                    pool.tensor_tensor(qs[j][:], qt.rearrange("p o g -> p g o").to_broadcast([128, 4, 4]),
                                       c.headones[:, 0:128:32].rearrange("p (o h) -> p o h", o=1)
                                       .to_broadcast([128, 4, 4]), ALU.mult).then_inc(s_q, 1)

                two_by_two(pool, step)

            @block.scalar
            def _(act):
                def step(t, j, age):
                    act.wait_ge(s_o, t + 1)
                    dst = c.o[:, t:t + 1, :] if age < 2 else c.o[:, bass.ds(t, 1), :]
                    act.activation(dst, po[j][0:RD, 0:16].rearrange("p (o x) -> p o x", o=1), ACT.Copy)\
                        .then_inc(s_oe, 1)

                two_by_two(act, step)


def phase_mix(c):
    nc, a = c.nc, c.a
    st = ExitStack()
    with st:
        wg1 = c.sb("gate_W1", [128, KT, RD], f32, st)
        wg2 = c.sb("gate_W2", [RD, D + RD], f32, st)
        wo = c.sb("mix_Wo", [RD, RH, D], f32, st)
        nw = c.sb("norm_w", [RD, RH], f32, st)
        wx = c.sb("rnn_Wx", [128, KT, D], f32, st)
        bias = c.sb("rnn_b", [128, KT], f32, st)
        g1 = c.sb("gate_inner", [RD, 512], f32, st)
        sg = c.sb("gate", [RD, 2, 512], f32, st)
        y = c.sb("gated", [RD, RH, 512], f32, st)
        y2 = c.sb("gated_squared", [RD, RH, 512], f32, st)
        pg1, pga, pgb, pm0, pm1, px0, px1 = (c.pb(n, st) for n in ("g1_psum", "gate_psum0", "gate_psum1", "ms_psum0",
                                                                   "ms_psum1", "mix_psum0", "mix_psum1"))
        pg, pm, px = (pga, pgb), (pm0, pm1), (px0, px1)
        s_w, s_g1, s_g1e, s_g, s_sg, s_y = (c.sem(n) for n in ("mix_weights", "g1_made", "g1_evac", "gate_made",
                                                               "gate_sig", "gated_made"))
        s_y2, s_ms, s_r, s_rt, s_yn = (c.sem(n) for n in ("gated_sq", "ms_made", "ms_recip", "ms_root", "normed"))
        s_pad = c.sem("gate_W2_padded")
        s_x, s_x1, s_xw, s_xwe, s_e = (c.sem(n) for n in ("mix_made", "x1_made", "xw_made", "xw_evac", "ms_plus_eps"))
        with nc.Block() as block:
            @block.sync
            def _(sp):
                sp.dma_start(wg1[:], a["L0_attn_Wog1"].rearrange("(k p) n -> p k n", p=128)).then_inc(s_w, 16)
                sp.dma_start(wg2[:, 0:D], a["L0_attn_Wog2"]).then_inc(s_w, 16)
                sp.dma_start(wo[:], a["L0_attn_Wo"].rearrange("(h v) n -> v h n", v=RD)).then_inc(s_w, 16)
                sp.dma_start(wx[:], a["L0_cond2_Wx"].rearrange("(k p) n -> p k n", p=128)).then_inc(s_w, 16)
                with nc.allow_non_contiguous_dma("small vectors"):
                    sp.dma_start(nw[:], a["L0_attn_norm_w"].rearrange("(h v) -> v h", v=RD)).then_inc(s_w, 16)
                    sp.dma_start(bias[:], col(a["L0_cond2_b"])).then_inc(s_w, 16)

            @block.gpsimd
            def _(pool):
                pool.memset(wg2[:, D:D + RD], 0.0).then_inc(s_pad, 1)

            @block.tensor
            def _(pe):
                pe.wait_ge(s_w, 96)
                pe.wait_ge(s_pad, 1)
                with pe.Fori(0, NB) as n:
                    for k in range(KT):
                        mm = pe.matmul(pg1[0:RD, :], wg1[:, k, :], c.hT[:, k, bass.ds(n * 512, 512)],
                                       start=(k == 0), stop=(k == KT - 1))
                    mm.then_inc(s_g1, 1)
                    pe.wait_ge(s_g1e, n + 1)
                    for h in range(RH):
                        if h >= 2:
                            pe.wait_ge(s_sg, n * RH + (h - 1))
                        pe.matmul(pg[h % 2][0:2 * RD, :], wg2[:, h * RD:(h + 2) * RD], g1[:], start=True, stop=True)\
                          .then_inc(s_g, 1)
                    for h in range(RH):
                        pe.wait_ge(s_y2, n * RH + (h + 1))
                        if h >= 2:
                            pe.wait_ge(s_e, n * RH + (h - 1))
                        pe.matmul(pm[h % 2][0:2 * RD, :], c.ones[0:RD, 0:2 * RD], y2[:, h, :], start=True, stop=True)\
                          .then_inc(s_ms, 1)
                    pe.wait_ge(s_yn, (n + 1) * RH)
                    for m in range(KT):
                        for h in range(RH):
                            mm = pe.matmul(px[m][:], wo[:, h, m * 128:(m + 1) * 128], y[:, h, :],
                                           start=(h == 0), stop=(h == RH - 1))
                        mm.then_inc(s_x, 1)
                    pe.wait_ge(s_x1, (n + 1) * KT)
                    for m in range(KT):
                        for k in range(KT):
                            mm = pe.matmul(px[m][:], wx[:, k, m * 128:(m + 1) * 128], c.xT[:, k, bass.ds(n * 512, 512)],
                                           start=(k == 0), stop=(k == KT - 1))
                        mm.then_inc(s_xw, 1)
                    pe.wait_ge(s_xwe, (n + 1) * KT)

            @block.scalar
            def _(act):
                act.wait_ge(s_w, 96)
                with act.Fori(0, NB) as n:
                    act.wait_ge(s_g1, n + 1)
                    act.activation(g1[:], pg1[0:RD, :], ACT.Copy).then_inc(s_g1e, 1)
                    for h in range(RH):
                        act.wait_ge(s_g, n * RH + (h + 1))
                        if h >= 2:
                            act.wait_ge(s_y, n * RH + (h - 1))
                        act.activation(sg[:, h % 2], pg[h % 2][0:RD, :], ACT.Sigmoid).then_inc(s_sg, 1)
                    for h in range(RH):
                        act.wait_ge(s_r, n * RH + (h + 1))
                        act.activation(y2[:, h, :], y2[:, h, :], ACT.Sqrt).then_inc(s_rt, 1)
                    for m in range(KT):
                        act.wait_ge(s_xw, n * KT + (m + 1))
                        act.activation(c.xw[:, bass.ds(n * 256, 256), m, :],
                                       px[m][:].rearrange("p (t b) -> p t b", b=B), ACT.Identity,
                                       bias=bias[:, m:m + 1]).then_inc(s_xwe, 1)

            @block.vector
            def _(v):
                v.wait_ge(s_w, 96)
                with v.Fori(0, NB) as n:
                    for h in range(RH):
                        v.wait_ge(s_sg, n * RH + (h + 1))
                        m, hl = h // 4, h % 4
                        o = c.o[:, bass.ds(n * 256, 256), :].rearrange("p t (m b h) -> p t m b h", m=KT, b=B)[:, :, m, :, hl]
                        v.tensor_tensor(y[:, h, :].rearrange("p (t b) -> p t b", b=B), o,
                                        sg[:, h % 2].rearrange("p (t b) -> p t b", b=B), ALU.mult).then_inc(s_y, 1)
                        v.wait_ge(s_y, n * RH + (h + 1))
                        v.tensor_tensor(y2[:, h, :], y[:, h, :], y[:, h, :], ALU.mult).then_inc(s_y2, 1)
                    for h in range(RH):
                        v.wait_ge(s_ms, n * RH + (h + 1))
                        v.tensor_scalar(y2[:, h, :], pm[h % 2][0:RD, :], 1.0 / RD, 1e-6, ALU.mult, ALU.add)\
                         .then_inc(s_e, 1)
                        v.wait_ge(s_e, n * RH + (h + 1))
                        v.reciprocal(y2[:, h, :], y2[:, h, :]).then_inc(s_r, 1)
                    for h in range(RH):
                        v.wait_ge(s_rt, n * RH + (h + 1))
                        v.scalar_tensor_tensor(y[:, h, :], y[:, h, :], nw[:, h:h + 1], y2[:, h, :], ALU.mult, ALU.mult)\
                         .then_inc(s_yn, 1)
                    for m in range(KT):
                        v.wait_ge(s_x, n * KT + (m + 1))
                        x1 = c.xT[:, m, bass.ds(n * 512, 512)]
                        v.tensor_tensor(x1, px[m][:], x1, ALU.add).then_inc(s_x1, 1)


def phase_rnn(c):
    nc = c.nc
    st = ExitStack()
    with st:
        ha = c.sb("r_high", [128, KT, B], f16, st)
        hb = c.sb("r_low", [128, KT, B], f16, st)
        z = c.sb("r_z", [128, KT, B], f32, st)
        pz = c.pb("r_psum", st)
        s_p, s_z, s_h, s_ha, s_hb = (c.sem(n) for n in ("r_products", "r_sum", "r_state", "r_high_s", "r_low_s"))
        with nc.Block() as block:
            @block.tensor
            def _(pe):
                first = True
                for m in range(KT):
                    for k in range(KT):
                        mm = pe.matmul(pz[:, 2 * m:2 * m + 2], c.wh2[:, k, m * 128:(m + 1) * 128], c.h0[:, k, :],
                                       start=first, stop=(m == 1 and k == 1))
                        first = False
                mm.then_inc(s_p, 1)
                with pe.Fori(1, T) as t:
                    pe.wait_ge(s_ha, t)
                    first = True
                    for m in range(KT):
                        for k in range(KT):
                            for part in (c.wa2, c.wb2):
                                pe.matmul(pz[:, 2 * m:2 * m + 2], part[:, k, m * 128:(m + 1) * 128], ha[:, k, :],
                                          start=first, stop=False)
                                first = False
                    pe.wait_ge(s_hb, t)
                    for m in range(KT):
                        for k in range(KT):
                            mm = pe.matmul(pz[:, 2 * m:2 * m + 2], c.wa2[:, k, m * 128:(m + 1) * 128], hb[:, k, :],
                                           start=False, stop=(m == 1 and k == 1))
                    mm.then_inc(s_p, 1)

            @block.scalar
            def _(act):
                act.activation(c.scratch[:, 0:2], c.ones[:, 0:2], ACT.Tanh)
                with act.Fori(0, T) as t:
                    act.wait_ge(s_z, t + 1)
                    act.activation(c.hT[:, :, bass.ds(t * B, B)], z[:], ACT.Tanh).then_inc(s_h, 1)

            @block.vector
            def _(v):
                def step(t, first):
                    pz4 = pz[:, 0:4].rearrange("p (m b) -> p m b", b=B)
                    v.wait_ge(s_p, t + 1)
                    if first:
                        v.tensor_tensor(z[:], pz4, c.xw[:, 0], ALU.add).then_inc(s_z, 1)
                    else:
                        v.scalar_tensor_tensor(z[:], pz4, c.unscale[:, 1:2],
                                               c.xw[:, bass.ds(t, 1)].rearrange("p o m b -> p (o m) b"),
                                               ALU.mult, ALU.add).then_inc(s_z, 1)
                    h = c.hT[:, :, 0:B] if first else c.hT[:, :, bass.ds(t * B, B)]
                    v.wait_ge(s_h, t + 1)
                    v.tensor_scalar(ha[:], h, HS, None, ALU.mult).then_inc(s_ha, 1)
                    v.wait_ge(s_ha, t + 1)
                    v.scalar_tensor_tensor(hb[:], h, HS, ha[:], ALU.mult, ALU.subtract).then_inc(s_hb, 1)

                step(0, True)
                with v.Fori(1, T) as t:
                    step(t, False)


def phase_heads(c):
    nc, a = c.nc, c.a
    st = ExitStack()
    with st:
        w = c.sb("w_qkv", [128, KT, 3 * D], f32, st)
        wp = c.sb("w_qk_padded", [128, KT, 2, 4, 128], f32, st)
        pq = [c.pb(f"qk_psum{i}", st) for i in range(2)]
        pv = [c.pb(f"v_psum{i}", st) for i in range(2)]
        s_w, s_0, s_pad = c.sem("qkv_weights"), c.sem("qk_zeroed"), c.sem("qk_padded")
        s_q, s_qe, s_v, s_ve, s_m = c.sem("qk_made"), c.sem("qk_evac"), c.sem("v_made"), c.sem("v_evac"), c.sem("masks")
        with nc.Block() as block:
            @block.sync
            def _(sp):
                sp.dma_start(w[:], a["L0_ffn_w_qkv"].rearrange("(k p) n -> p k n", p=128)).then_inc(s_w, 16)

            @block.gpsimd
            def _(pool):
                pool.memset(wp[:], 0.0).then_inc(s_0, 1)
                pool.memset(c.rowmax[:], 0.0).then_inc(s_0, 1)
                pool.memset(c.vt[:], 0.0).then_inc(s_0, 1)
                pool.memset(c.mask_q[:], 0.0).then_inc(s_0, 1)
                pool.memset(c.mask_k[:], 0.0).then_inc(s_0, 1)
                pool.wait_ge(s_0, 5)
                pool.affine_select(out=c.mask_q[:], in_=c.mask_q[:], compare_op=ALU.is_ge, fill=-1e30, base=0,
                                   pattern=[[-1, 128]], channel_multiplier=1).then_inc(s_m, 1)
                pool.affine_select(out=c.mask_k[:], in_=c.mask_k[:], compare_op=ALU.is_ge, fill=-1e30, base=0,
                                   pattern=[[1, 128]], channel_multiplier=-1).then_inc(s_m, 1)
                pool.memset(c.vt[:, :, :, AD:AD + 1], 1.0).then_inc(s_m, 1)

            @block.tensor
            def _(pe):
                pe.wait_ge(s_pad, 2 * KT)
                with pe.Fori(0, NB) as n:
                    for j in range(2):
                        for g in range(4):
                            i = j * 4 + g
                            pe.wait_ge(s_qe, n * 8 + (i + 1))
                            for k in range(KT):
                                mm = pe.matmul(pq[i % 2][:], wp[:, k, j, g, :], c.hT[:, k, bass.ds(n * 512, 512)],
                                               start=(k == 0), stop=(k == KT - 1))
                            mm.then_inc(s_q, 1)
                for b in range(B):
                    for i in range(T // 128):
                        u = b * (T // 128) + i
                        if u >= 2:
                            pe.wait_ge(s_ve, u - 1)
                        for k in range(KT):
                            rows = c.hT[:, k, :].rearrange("p (t b) -> p b t", b=B)[:, b, i * 128:(i + 1) * 128]
                            mm = pe.matmul(pv[u % 2][:, 0:D], rows, w[:, k, 2 * D:3 * D], start=(k == 0), stop=(k == KT - 1))
                        mm.then_inc(s_v, 1)

            @block.vector
            def _(v):
                v.wait_ge(s_0, 1)
                v.wait_ge(s_w, 16)
                for k in range(KT):
                    for j in range(2):
                        v.tensor_copy(wp[:, k, j].rearrange("p g (h r) -> p (g h) r", r=32)[:, :, 0:AD],
                                      w[:, k, j * D:(j + 1) * D].rearrange("p (h d) -> p h d", d=AD)).then_inc(s_pad, 1)
                v.tensor_copy(c.ident16[:], c.ident[:])
                v.tensor_scalar(c.dsel[:], c.headones[:], c.diag[:, AD:AD + 1], None, ALU.mult)
                v.wait_ge(s_m, 3)
                for b in range(B):
                    for i in range(T // 128):
                        u = b * (T // 128) + i
                        v.wait_ge(s_v, u + 1)
                        v.tensor_copy(c.vt[:, u, :, 0:AD], pv[u % 2][:, 0:D].rearrange("p (h d) -> p h d", d=AD))\
                         .then_inc(s_ve, 1)

            @block.scalar
            def _(act):
                act.activation(c.scratch[:, 0:2], c.ones[:, 0:2], ACT.Copy).then_inc(s_qe, 2)
                with act.Fori(0, NB) as n:
                    for j, dst in enumerate((c.qT, c.kT)):
                        for g in range(4):
                            i = j * 4 + g
                            act.wait_ge(s_q, n * 8 + (i + 1))
                            act.activation(dst[:, g, bass.ds(n * 512, 512)], pq[i % 2][:], ACT.Copy).then_inc(s_qe, 1)


def tiles_of(size):
    out = []
    for i in range(size // 128):
        for lo in range(0, size, 512):
            out.append((i, lo, lo + 512))
    return out


def phase_attend(c):
    nc = c.nc
    QT = T // 128
    st = ExitStack()
    with st:
        qs = c.sb("q_staged", [128, T], f32, st)
        ks = c.sb("k_staged", [128, T], f32, st)
        qa = c.sb("q_with_max", [128, T], f32, st)
        vs = c.sb("v_staged", [128, QT, 4, 32], f32, st)
        pr = [c.sb(f"probs{i}", [128, 512], f32, st) for i in range(4)]
        ob = c.sb("o_unscaled", [128, T], f32, st)
        rc = c.sb("o_recip", [128, T], f32, st)
        big = [c.pb(f"scores{i}", st, 1024) for i in range(2)]
        pm = c.pb("max_in_rows", st, 1024)
        po = c.pb("o_sums", st, 1024)
        s_st, s_sf, s_s, s_m, s_r, s_q = (c.sem(n) for n in ("staged", "staging_free", "scores_q", "max_taken",
                                                             "max_turned", "q_ready"))
        s_t, s_e, s_pf, s_o, s_oc, s_d, s_dr = (c.sem(n) for n in ("scores_k", "exp_made", "probs_free", "o_summed",
                                                                   "o_copied", "den_spread", "den_recip"))
        s_dd = c.sem("o_scaled")
        kt = [(i, max(i * 128, lo), lo + 512) for i in range(QT) for lo in (0, 512) if lo + 512 > i * 128]
        NK = len(kt)
        with nc.Block() as block:
            @block.vector
            def _(v):
                v.tensor_copy(c.scratch[:, 0:2], c.ones[:, 0:2]).then_inc(s_m, 2)
                with v.Fori(0, B) as b:
                    with v.Fori(0, 4) as g:
                        u = b * 4 + g
                        qv = c.qT[:, bass.ds(g, 1), :].rearrange("p o (t b) -> p b (o t)", b=B)[:, bass.ds(b, 1), :]
                        kv = c.kT[:, bass.ds(g, 1), :].rearrange("p o (t b) -> p b (o t)", b=B)[:, bass.ds(b, 1), :]
                        v.tensor_copy(qs[:].rearrange("p (o t) -> p o t", o=1), qv).then_inc(s_st, 1)
                        v.tensor_scalar(ks[:].rearrange("p (o t) -> p o t", o=1), kv, c.diag[:, AD:AD + 1], None,
                                        ALU.add).then_inc(s_st, 1)
                        v.tensor_copy(vs[:], c.vt[:, bass.ds(b * QT, QT), bass.ds(g * 4, 4), :]).then_inc(s_st, 1)
                        for h in range(4):
                            for i in range(QT):
                                n = h * QT + i
                                v.wait_ge(s_s, u * (4 * QT) + (n + 1))
                                v.tensor_reduce(c.rowmax[:, i, h, AD:AD + 1], big[n % 2][:, 0:(i + 1) * 128], AX.X,
                                                ALU.max).then_inc(s_m, 1)
                        for half in range(2):
                            v.wait_ge(s_r, u * 2 + (half + 1))
                            v.tensor_tensor(blk(qa, half), blk(qs, half), blk(pm, half), ALU.subtract).then_inc(s_q, 1)
                        for half in range(2):
                            v.wait_ge(s_d, u * 2 + (half + 1))
                            v.reciprocal(blk(rc, half), blk(pm, half)).then_inc(s_dr, 1)
                        v.wait_ge(s_dr, u * 2 + 2)
                        dst = c.oT[:, bass.ds(g, 1), :].rearrange("p o (t b) -> p b (o t)", b=B)[:, bass.ds(b, 1), :]
                        v.tensor_tensor(dst, ob[:].rearrange("p (o t) -> p o t", o=1),
                                        rc[:].rearrange("p (o t) -> p o t", o=1), ALU.mult).then_inc(s_dd, 1)

            @block.tensor
            def _(pe):
                with pe.Fori(0, B) as b:
                    with pe.Fori(0, 4) as g:
                        u = b * 4 + g
                        pe.wait_ge(s_st, u * 3 + 3)
                        for h in range(4):
                            r = slice(32 * h, 32 * h + 32)
                            for i in range(QT):
                                n = h * QT + i
                                pe.wait_ge(s_m, u * (4 * QT) + (n + 1))
                                s = big[n % 2]
                                d = i * 128
                                for lo in range(0, d + 128, 512):
                                    hi = min(lo + 512, d + 128)
                                    here = hi == d + 128
                                    if here:
                                        pe.matmul(s[:, d:d + 128], c.ident16[:], c.mask_q[:], start=True, stop=True,
                                                  skip_group_check=True)
                                    mm = pe.matmul(s[:, lo:hi], qs[r, d:d + 128], ks[r, lo:hi], start=not here, stop=True,
                                                   skip_group_check=True)
                                mm.then_inc(s_s, 1)
                        pe.wait_ge(s_m, (u + 1) * (4 * QT) + 2)
                        for half in range(2):
                            for i in range(4 * half, 4 * half + 4):
                                mm = pe.matmul(pm[:, i * 128:(i + 1) * 128],
                                               c.rowmax[:, i].rearrange("p h r -> p (h r)"), c.ident[:],
                                               start=True, stop=True)
                            mm.then_inc(s_r, 1)
                        pe.wait_ge(s_q, u * 2 + 2)

                        def scores(m):
                            h, (i, lo, hi) = m // NK, kt[m % NK]
                            r = slice(32 * h, 32 * h + 32)
                            s = big[m % 4 // 2][:, m % 2 * 512:m % 2 * 512 + hi - lo]
                            if m >= 4:
                                pe.wait_ge(s_e, u * (4 * NK) + (m - 3))
                            diag = lo == i * 128
                            if diag:
                                pe.matmul(s[:, 0:128], c.ident16[:], c.mask_k[:], start=True, stop=True,
                                          skip_group_check=True)
                            pe.matmul(s, ks[r, i * 128:(i + 1) * 128], qa[r, lo:hi], start=not diag, stop=True,
                                      skip_group_check=True).then_inc(s_t, 1)

                        def sums(m):
                            h, (i, lo, hi) = m // NK, kt[m % NK]
                            pe.wait_ge(s_e, u * (4 * NK) + (m + 1))
                            last = (i == 3 and hi == 512) or i == 7
                            pe.matmul(po[32 * h:32 * h + 32, lo:hi], vs[:, i, h, :], pr[m % 4][:, 0:hi - lo],
                                      start=(i == 0), stop=last).then_inc(s_o, 1)

                        for m in range(4 * NK):
                            scores(m)
                            if m >= 2:
                                sums(m - 2)
                        sums(4 * NK - 2)
                        sums(4 * NK - 1)
                        for half in range(2):
                            pe.wait_ge(s_oc, u * 2 + (half + 1))
                            pe.matmul(blk(pm, half), c.dsel[:], blk(ob, half), start=True, stop=True).then_inc(s_d, 1)
                        pe.wait_ge(s_dr, u * 2 + 2)

            @block.scalar
            def _(act):
                with act.Fori(0, B) as b:
                    with act.Fori(0, 4) as g:
                        u = b * 4 + g
                        for m in range(4 * NK):
                            i, lo, hi = kt[m % NK]
                            act.wait_ge(s_t, u * (4 * NK) + (m + 1))
                            if m >= 4:
                                act.wait_ge(s_o, u * (4 * NK) + (m - 3))
                            act.activation(pr[m % 4][:, 0:hi - lo], big[m % 4 // 2][:, m % 2 * 512:m % 2 * 512 + hi - lo],
                                           ACT.Exp, scale=float(AD) ** -0.5).then_inc(s_e, 1)
                        act.wait_ge(s_o, (u + 1) * (4 * NK))
                        for half in range(2):
                            act.activation(blk(ob, half), blk(po, half), ACT.Copy).then_inc(s_oc, 1)


def phase_attn_out(c):
    nc, a = c.nc, c.a
    st = ExitStack()
    with st:
        wo = c.sb("w_o_padded", [128, 4, D], f32, st)
        px = [c.pb(f"attn_out_psum{i}", st) for i in range(2)]
        s_0, s_w, s_p, s_e = c.sem("w_o_zeroed"), c.sem("w_o_loaded"), c.sem("attn_out_made"), c.sem("attn_out_added")
        with nc.Block() as block:
            @block.gpsimd
            def _(pool):
                pool.memset(wo[:], 0.0).then_inc(s_0, 1)

            @block.sync
            def _(sp):
                sp.wait_ge(s_0, 1)
                for h in range(4):
                    sp.dma_start(wo[32 * h:32 * h + AD], a["L0_ffn_w_o"].rearrange("(g h d) n -> h d g n", h=4, d=AD)[h])\
                      .then_inc(s_w, 16)

            @block.tensor
            def _(pe):
                pe.wait_ge(s_w, 64)
                for n in range(NB):
                    for m in range(KT):
                        if n:
                            pe.wait_ge(s_e, (n - 1) * KT + m + 1)
                        for g in range(4):
                            mm = pe.matmul(px[m][:], wo[:, g, m * 128:(m + 1) * 128], blk(c.oT[:, g], n),
                                           start=(g == 0), stop=(g == 3))
                        mm.then_inc(s_p, 1)

            @block.vector
            def _(v):
                for n in range(NB):
                    for m in range(KT):
                        v.wait_ge(s_p, n * KT + m + 1)
                        x = blk(c.hT[:, m], n)
                        v.tensor_tensor(x, px[m][:], x, ALU.add).then_inc(s_e, 1)


def phase_layernorm(c, tag, other, out, gain, shift, residual):
    nc, a = c.nc, c.a
    st = ExitStack()
    with st:
        gb = c.sb(tag + "_gain_shift", [128, 2, KT], f32, st)
        mean_of = c.sb(tag + "_one_over_d", [128, 128], f32, st)
        r = c.sb(tag + "_sum", [128, KT, 512], f32, st)
        sq = c.sb(tag + "_squares", [128, KT, 512], f32, st)
        rt = c.sb(tag + "_root", [128, 512], f32, st)
        pm, pv = c.pb(tag + "_mean", st), c.pb(tag + "_var", st)
        s_w, s_k, s_r, s_m, s_c, s_v, s_e, s_rt, s_n = (c.sem(f"{tag}_{n}") for n in (
            "weights", "const", "summed", "mean_made", "squared", "var_made", "recip", "root_made", "normed"))
        with nc.Block() as block:
            @block.sync
            def _(sp):
                with nc.allow_non_contiguous_dma("small vectors"):
                    sp.dma_start(gb[:, 0], col(a[gain])).then_inc(s_w, 16)
                    sp.dma_start(gb[:, 1], col(a[shift])).then_inc(s_w, 16)

            @block.gpsimd
            def _(pool):
                pool.memset(mean_of[:], 1.0 / D).then_inc(s_k, 1)

            @block.tensor
            def _(pe):
                pe.wait_ge(s_k, 1)
                with pe.Fori(0, NB) as n:
                    for bank, src, ready, done in ((pm, r, s_r, s_m), (pv, sq, s_c, s_v)):
                        pe.wait_ge(ready, n + 1)
                        for k in range(KT):
                            mm = pe.matmul(bank[:], mean_of[:], src[:, k], start=(k == 0), stop=(k == KT - 1))
                        mm.then_inc(done, 1)

            @block.vector
            def _(v):
                v.wait_ge(s_w, 32)
                with v.Fori(0, NB) as n:
                    x = c.hT[:, :, bass.ds(n * 512, 512)]
                    if other is None:
                        v.tensor_copy(r[:], x).then_inc(s_r, 1)
                    else:
                        v.tensor_tensor(r[:], x, other[:, :, bass.ds(n * 512, 512)], ALU.add).then_inc(s_r, 1)
                    v.wait_ge(s_m, n + 1)
                    v.wait_ge(s_r, n + 1)
                    for k in range(KT):
                        v.tensor_tensor(r[:, k], r[:, k], pm[:], ALU.subtract).then_inc(s_n, 1)
                    v.wait_ge(s_n, n * 8 + 2)
                    v.tensor_tensor(sq[:], r[:], r[:], ALU.mult).then_inc(s_c, 1)
                    v.wait_ge(s_v, n + 1)
                    v.tensor_scalar(rt[:], pv[:], 1e-5, None, ALU.add).then_inc(s_n, 1)
                    v.wait_ge(s_n, n * 8 + 3)
                    v.reciprocal(rt[:], rt[:]).then_inc(s_e, 1)
                    v.wait_ge(s_rt, n + 1)
                    for k in range(KT):
                        v.scalar_tensor_tensor(sq[:, k], r[:, k], gb[:, 0, k:k + 1], rt[:], ALU.mult, ALU.mult)\
                         .then_inc(s_n, 1)
                    v.wait_ge(s_n, n * 8 + 5)
                    for k in range(KT):
                        dst = out[:, k, bass.ds(n * 512, 512)]
                        if residual:
                            v.scalar_tensor_tensor(dst, sq[:, k], gb[:, 1, k:k + 1], dst, ALU.add, ALU.add)\
                             .then_inc(s_n, 1)
                        else:
                            v.tensor_scalar(dst, sq[:, k], gb[:, 1, k:k + 1], None, ALU.add).then_inc(s_n, 1)
                    v.tensor_copy(c.scratch[:, 0:2], c.ones[:, 0:2]).then_inc(s_n, 1)
                    v.wait_ge(s_n, n * 8 + 8)

            @block.scalar
            def _(act):
                with act.Fori(0, NB) as n:
                    act.wait_ge(s_e, n + 1)
                    act.activation(rt[:], rt[:], ACT.Sqrt).then_inc(s_rt, 1)


def phase_router(c):
    nc, a = c.nc, c.a
    NT = TOK // 128
    st = ExitStack()
    with st:
        wg = c.sb("w_router", [128, KT, EX], f32, st)
        before = c.sb("expert_before", [128, EX, EX], f32, st)
        p = c.sb("expert_probs", [128, NT, EX], f32, st)
        mx = c.sb("expert_max", [128, NT], f32, st)
        sm = c.sb("expert_sum", [128, NT], f32, st)
        gt = c.sb("expert_greater", [128, NT, EX, EX], f32, st)
        eq = c.sb("expert_equal", [128, NT, EX, EX], f32, st)
        rank = c.sb("expert_rank", [128, NT, EX], f32, st)
        pl = c.pb("logits", st)
        pt = c.pb("weights_turned", st, 2048)
        s_w, s_b, s_l, s_d, s_x, s_t = (c.sem(n) for n in ("router_w", "router_const", "logits_made", "router_dve",
                                                           "router_exp", "weights_turned_s"))
        s_te = c.sem("weights_evacuated")
        with nc.Block() as block:
            @block.sync
            def _(sp):
                with nc.allow_non_contiguous_dma("narrow rows"):
                    sp.dma_start(wg[:], a["L0_ffn_wg"].rearrange("(k p) n -> p k n", p=128)).then_inc(s_w, 16)

            @block.gpsimd
            def _(pool):
                pool.memset(before[:], 1.0).then_inc(s_b, 1)
                pool.wait_ge(s_b, 1)
                pool.affine_select(out=before[:], in_=before[:], compare_op=ALU.is_ge, fill=0.0, base=-1,
                                   pattern=[[1, EX], [-1, EX]], channel_multiplier=0).then_inc(s_b, 1)

            @block.tensor
            def _(pe):
                pe.wait_ge(s_w, 16)
                for i in range(NT):
                    for k in range(KT):
                        mm = pe.matmul(pl[:, i * EX:(i + 1) * EX], c.hT[:, k, i * 128:(i + 1) * 128], wg[:, k, :],
                                       start=(k == 0), stop=(k == KT - 1))
                mm.then_inc(s_l, 1)
                pe.wait_ge(s_d, 13)
                for i in range(NT):
                    mm = pe.matmul(pt[0:EX, i * 128:(i + 1) * 128], p[:, i, :], c.ident[:], start=True, stop=True)
                mm.then_inc(s_t, 1)

            @block.scalar
            def _(act):
                act.wait_ge(s_d, 2)
                act.activation(p[:], p[:], ACT.Exp).then_inc(s_x, 1)
                act.wait_ge(s_t, 1)
                for n in range(NB):
                    act.activation(blk(c.wT, n), pt[0:EX, n * 512:(n + 1) * 512], ACT.Copy).then_inc(s_te, 1)

            @block.vector
            def _(v):
                steps = [0]

                def then(ins):
                    ins.then_inc(s_d, 1)
                    steps[0] += 1
                    v.wait_ge(s_d, steps[0])

                def over(t):
                    return t[:].rearrange("p (n o) -> p n o", o=1).to_broadcast([128, NT, EX])

                four = [128, NT, EX, EX]
                mine = p[:].rearrange("p n (e o) -> p n e o", o=1).to_broadcast(four)
                other = p[:].rearrange("p n (o e) -> p n o e", o=1).to_broadcast(four)
                logits = pl[:, 0:NT * EX].rearrange("p (n e) -> p n e", e=EX)
                v.wait_ge(s_l, 1)
                then(v.tensor_reduce(mx[:], logits, AX.X, ALU.max))
                then(v.tensor_tensor(p[:], logits, over(mx), ALU.subtract))
                v.wait_ge(s_x, 1)
                then(v.tensor_reduce(sm[:], p[:], AX.X, ALU.add))
                then(v.reciprocal(mx[:], sm[:]))
                then(v.tensor_tensor(p[:], p[:], over(mx), ALU.mult))
                then(v.tensor_tensor(gt[:], other, mine, ALU.is_gt))
                then(v.tensor_tensor(eq[:], other, mine, ALU.is_equal))
                v.wait_ge(s_b, 2)
                then(v.tensor_tensor(eq[:], eq[:], before[:].rearrange("p (o e) j -> p o e j", o=1).to_broadcast(four),
                                     ALU.mult))
                then(v.tensor_tensor(gt[:], gt[:], eq[:], ALU.add))
                then(v.tensor_reduce(rank[:], gt[:], AX.X, ALU.add))
                then(v.scalar_tensor_tensor(p[:], rank[:], 1.5, p[:], ALU.is_lt, ALU.mult))
                then(v.tensor_reduce(sm[:], p[:], AX.X, ALU.add))
                v.reciprocal(mx[:], sm[:]).then_inc(s_te, 1)
                v.wait_ge(s_te, 1)
                then(v.tensor_tensor(p[:], p[:], over(mx), ALU.mult))


def phase_experts(c):
    nc, a = c.nc, c.a
    st = ExitStack()
    with st:
        w1 = [c.sb(f"expert_w1_{i}", [128, KT, FF], f32, st) for i in range(2)]
        w2 = [c.sb(f"expert_w2_{i}", [128, FT, D], f32, st) for i in range(2)]
        b1 = [c.sb(f"expert_b1_{i}", [128, FT], f32, st) for i in range(2)]
        pick = [c.sb(f"expert_pick{i}", [EX, 128], f32, st) for i in range(2)]
        picks = c.sb("expert_picks", [EX, EX, 128], f32, st)
        b2 = c.sb("expert_b2", [EX, D], f32, st)
        g = [c.sb(f"gelu{i}", [128, 512], f32, st) for i in range(3)]
        gw = [c.sb(f"gelu_weighted{i}", [128, 512], f32, st) for i in range(3)]
        pu = [c.pb(f"up_psum{i}", st) for i in range(3)]
        py = [c.pb(f"down_psum{i}", st) for i in range(4)]
        pw = c.pb("weight_psum", st)
        wrow = [c.sb(f"weight_in_rows{i}", [128, 512], f32, st) for i in range(2)]
        s_b2, s_pk, s_pick = c.sem("b2_loaded"), c.sem("picks_made"), c.sem("pick_staged")
        s_w = [c.sem(f"expert_loaded{i}") for i in range(2)]
        s_i, s_ie = c.sem("y_start_made"), c.sem("y_started")
        s_wr, s_wre, s_up, s_g, s_gw, s_dn, s_y = (c.sem(n) for n in (
            "weight_spread", "weight_copied", "up_made", "gelu_made", "gelu_weighted_s", "down_made", "y_added"))
        with nc.Block() as block:
            def units(eng, body):
                with eng.Fori(0, EX // 2) as ei:
                    for je in range(2):
                        with eng.Fori(0, NB // 2) as ni:
                            for jn in range(2):
                                body(ei * 2 + je, je, ni * 2 + jn, jn, ei * (2 * NB) + ni * 2 + (je * NB + jn))

            @block.sync
            def _(sp):
                sp.dma_start(b2[:], a["L0_ffn_bb2"]).then_inc(s_b2, 16)
                with nc.allow_non_contiguous_dma("a column of biases"):
                    def load(e, je):
                        sp.dma_start(w1[je][:], a["L0_ffn_w1"][e].rearrange("o (k p) f -> p (o k) f", p=128)).then_inc(s_w[je], 16)
                        sp.dma_start(w2[je][:], a["L0_ffn_w2"][e].rearrange("o (f p) d -> p (o f) d", p=128)).then_inc(s_w[je], 16)
                        sp.dma_start(b1[je][:], a["L0_ffn_bb1"][e].rearrange("o (f p) -> p (o f)", p=128)).then_inc(s_w[je], 16)

                    for je in range(2):
                        load(slice(je, je + 1), je)
                    with sp.Fori(1, EX // 2) as ei:
                        for je in range(2):
                            sp.wait_ge(s_y, ei * (2 * NB * KT) + ((je - 1) * NB * KT + 6))
                            load(bass.ds(ei * 2 + je, 1), je)

            @block.gpsimd
            def _(pool):
                pool.memset(picks[:], 0.0).then_inc(s_pk, 1)
                pool.wait_ge(s_pk, 1)
                pool.affine_select(out=picks[:], in_=picks[:], compare_op=ALU.not_equal, fill=1.0, base=0,
                                   pattern=[[-1, EX], [0, 128]], channel_multiplier=1).then_inc(s_pk, 1)
                pool.wait_ge(s_pk, 2)
                for je in range(2):
                    pool.tensor_copy(pick[je][:], picks[:, je]).then_inc(s_pick, 1)
                with pool.Fori(1, EX // 2) as ei:
                    for je in range(2):
                        pool.wait_ge(s_y, ei * (2 * NB * KT) + ((je - 1) * NB * KT + 6))
                        pool.tensor_copy(pick[je][:].rearrange("p (o n) -> p o n", o=1),
                                         picks[:, bass.ds(ei * 2 + je, 1), :]).then_inc(s_pick, 1)

            @block.tensor
            def _(pe):
                pe.wait_ge(s_b2, 16)
                for n in range(NB):
                    for m in range(KT):
                        i = n * KT + m
                        if i >= 4:
                            pe.wait_ge(s_ie, i - 3)
                        pe.matmul(py[i % 4][:], b2[:, m * 128:(m + 1) * 128], blk(c.wT, n), start=True, stop=True)\
                          .then_inc(s_i, 1)
                pe.wait_ge(s_ie, NB * KT)

                def body(e, je, n, jn, u):
                    q = u * FT
                    h = [c.hT[:, k, bass.ds(n * 512, 512)] for k in range(KT)]
                    pe.wait_ge(s_pick, e + 1)
                    pe.wait_ge(s_wre, u + 1)
                    pe.matmul(pw[:], pick[je][:], c.wT[:, bass.ds(n * 512, 512)], start=True, stop=True).then_inc(s_wr, 1)
                    pe.wait_ge(s_w[je], (e - je) * 24 + 48)

                    def up(f):
                        if f >= 3:
                            pe.wait_ge(s_g, q + (f - 2))
                        for k in range(KT):
                            mm = pe.matmul(pu[f % 3][:], w1[je][:, k, f * 128:(f + 1) * 128], h[k],
                                           start=(k == 0), stop=(k == KT - 1))
                        mm.then_inc(s_up, 1)

                    def down(f):
                        pe.wait_ge(s_gw, q + (f + 1))
                        for m in range(KT):
                            mm = pe.matmul(py[jn * 2 + m][:], w2[je][:, f, m * 128:(m + 1) * 128], gw[f % 3][:],
                                           start=(f == 0), stop=(f == FT - 1))
                        mm.then_inc(s_dn, 1)
                        return mm

                    up(0)
                    up(1)
                    pe.wait_ge(s_y, u * KT + (KT + 2))
                    for f in range(FT):
                        if f + 2 < FT:
                            up(f + 2)
                        down(f)
                units(pe, body)

            @block.scalar
            def _(act):
                def body(e, je, n, jn, u):
                    q = u * FT
                    for f in range(FT):
                        act.wait_ge(s_up, q + (f + 1))
                        if f == 0:
                            act.wait_ge(s_w[je], (e - je) * 24 + 48)
                        if f >= 3:
                            act.wait_ge(s_gw, q + (f - 2))
                        act.activation(g[f % 3][:], pu[f % 3][:], ACT.Gelu_apprx_tanh, bias=b1[je][:, f:f + 1])\
                            .then_inc(s_g, 1)
                units(act, body)

            @block.vector
            def _(v):
                for n in range(NB):
                    for m in range(KT):
                        i = n * KT + m
                        v.wait_ge(s_i, i + 1)
                        v.tensor_copy(blk(c.y[:, m], n), py[i % 4][:]).then_inc(s_ie, 1)
                v.tensor_copy(c.scratch[:, 0:2], c.ones[:, 0:2]).then_inc(s_wre, 1)
                v.tensor_copy(c.scratch[:, 2:4], c.ones[:, 0:2]).then_inc(s_y, 6)

                def body(e, je, n, jn, u):
                    q = u * FT
                    v.wait_ge(s_wr, u + 1)
                    v.tensor_copy(wrow[jn][:], pw[:]).then_inc(s_wre, 1)
                    v.wait_ge(s_wre, u + 2)
                    for f in range(FT):
                        v.wait_ge(s_g, q + (f + 1))
                        if f >= 3:
                            v.wait_ge(s_dn, q + (f - 2))
                        v.tensor_tensor(gw[f % 3][:], g[f % 3][:], wrow[jn][:], ALU.mult).then_inc(s_gw, 1)
                    v.wait_ge(s_dn, q + FT)
                    for m in range(KT):
                        y = c.y[:, m, bass.ds(n * 512, 512)]
                        v.tensor_tensor(y, py[jn * 2 + m][:], y, ALU.add).then_inc(s_y, 1)
                units(v, body)


def phase_store(c, src):
    nc = c.nc
    st = ExitStack()
    with st:
        rows = c.sb("out_rows", [128, 2, T // 128, D], f32, st)
        pt = [c.pb(f"rows_turned{i}", st) for i in range(2)]
        s_t, s_e, s_out = c.sem("rows_turned_s"), c.sem("rows_evacuated"), c.sem("rows_stored")
        with nc.Block() as block:
            @block.tensor
            def _(pe):
                n = 0
                for b in range(B):
                    for i in range(T // 128):
                        if n >= 2:
                            pe.wait_ge(s_e, n - 1)
                        for k in range(KT):
                            s = src[:, k, :].rearrange("p (t b) -> p b t", b=B)[:, b, i * 128:(i + 1) * 128]
                            mm = pe.transpose(pt[n % 2][:, k * 128:(k + 1) * 128], s, c.ident[:])
                        mm.then_inc(s_t, 1)
                        n += 1

            @block.vector
            def _(v):
                for n in range(B * T // 128):
                    v.wait_ge(s_t, n + 1)
                    v.tensor_copy(rows[:, n // (T // 128), n % (T // 128)], pt[n % 2][:, 0:D]).then_inc(s_e, 1)

            @block.sync
            def _(sp):
                for b in range(B):
                    sp.wait_ge(s_e, (b + 1) * (T // 128))
                    sp.dma_start(c.a["out"][b].rearrange("(i p) c -> p i c", p=128), rows[:, b]).then_inc(s_out, 16)
                sp.wait_ge(s_out, 16 * B)


def program(nc, args):
    stack = ExitStack()
    with stack:
        c = Core(nc, args, stack)
        c.ident = c.sb("identity", [128, 128])
        c.headones = c.sb("ones_within_head", [128, 128])
        c.ones = c.sb("ones", [128, 128])
        c.unscale = c.sb("unscale", [128, 2])
        c.scratch = c.sb("scratch", [128, 4])
        c.diag = c.sb("diagonal", [128, RD])
        c.h0 = c.sb("h0", [128, KT, B])
        c.wh2 = c.sb("rnn_Wh", [128, KT, D])
        c.wa2 = c.sb("rnn_Wh_high", [128, KT, D], f16)
        c.wb2 = c.sb("rnn_Wh_low", [128, KT, D], f16)
        c.xT = c.sb("xT", [128, KT, TOK])
        c.hT = c.sb("hT", [128, KT, TOK])
        s1 = ExitStack()
        with s1:
            c.wh = c.sb("lstm_Wh", [128, KT, G4], f32, s1)
            c.wa = c.sb("lstm_Wh_high", [128, KT, G4], f16, s1)
            c.wb = c.sb("lstm_Wh_low", [128, KT, G4], f16, s1)
            c.xz = c.sb("lstm_xz", [128, T, G4 // 128, B], f32, s1)
            phase_load(c)
            phase_lstm(c)
        s2 = ExitStack()
        with s2:
            c.negones = c.sb("minus_ones_within_head", [128, 128], f32, s2)
            c.room = c.sb("o_rows", [128, T * 16], f32, s2)
            c.o = c.room[0:RD].rearrange("p (t x) -> p t x", x=16)
            s3 = ExitStack()
            with s3:
                c.kyk = c.sb("k_y_k", [128, T, 12], f32, s3)
                c.f, c.v, c.q = (c.sb(n, [128, T, 4], f32, s3) for n in ("decay_all", "v_all", "q_all"))
                phase_project(c)
                phase_delta(c)
            c.xw = c.sb("rnn_xw", [128, T, KT, B], f32, s2)
            phase_mix(c)
            phase_rnn(c)
        s5 = ExitStack()
        with s5:
            c.qT, c.kT, c.oT = (c.sb(n, [128, 4, TOK], f32, s5) for n in ("q_heads", "k_heads", "o_heads"))
            c.vt = c.sb("v_rows", [128, B * T // 128, AH, 32], f32, s5)
            c.rowmax = c.sb("score_max", [128, T // 128, 4, 32], f32, s5)
            c.mask_q, c.mask_k, c.ident16 = (c.sb(n, [128, 128], bf16, s5) for n in ("mask_q", "mask_k", "identity_bf16"))
            c.dsel = c.sb("sum_row_of_head", [128, 128], f32, s5)
            phase_heads(c)
            phase_attend(c)
            phase_attn_out(c)
        phase_layernorm(c, "norm1", None, c.hT, "L0_ffn_g1", "L0_ffn_b1", False)
        s6 = ExitStack()
        with s6:
            c.wT = c.sb("expert_weights", [EX, TOK], f32, s6)
            c.y = c.sb("expert_sum_y", [128, KT, TOK], f32, s6)
            phase_router(c)
            phase_experts(c)
            phase_layernorm(c, "norm2", c.y, c.xT, "L0_ffn_g2", "L0_ffn_b2", True)
        phase_store(c, c.xT)


_INS = ['x', 'cond_1024', 'L0_cond_Wx', 'L0_cond_Wh', 'L0_cond_b', 'L0_attn_Wq', 'L0_attn_Wk', 'L0_attn_Wv',
        'L0_attn_Wf1', 'L0_attn_Wf2', 'L0_attn_Wbeta', 'L0_attn_Wog1', 'L0_attn_Wog2', 'L0_attn_norm_w', 'L0_attn_Wo',
        'L0_cond2_Wx', 'L0_cond2_Wh', 'L0_cond2_b', 'L0_ffn_w_qkv', 'L0_ffn_w_o', 'L0_ffn_g1', 'L0_ffn_b1',
        'L0_ffn_wg', 'L0_ffn_w1', 'L0_ffn_bb1', 'L0_ffn_w2', 'L0_ffn_bb2', 'L0_ffn_g2', 'L0_ffn_b2']


def kernel(**inputs):
    import numpy as _np
    import concourse.bacc as _bacc
    from concourse import mybir as _mybir
    from concourse.bass_utils import run_bass_kernel_spmd as _run

    nc = _bacc.Bacc("TRN2", target_bir_lowering=False, num_devices=1)
    arrays, args = {}, {}
    for name in _INS:
        x = _np.ascontiguousarray(inputs[name])
        arrays[f"in_{name}_dram"] = x
        args[name] = nc.dram_tensor(f"in_{name}_dram", x.shape, _mybir.dt.from_np(x.dtype), kind="ExternalInput").ap()
    args["out"] = nc.dram_tensor("out_0_dram", (B, T, D), _mybir.dt.float32, kind="ExternalOutput").ap()
    program(nc, args)
    r = _run(nc, [arrays], core_ids=[0])
    return r.results[0]["out_0_dram"]
```

```python
import concourse.bass as bass
from concourse import mybir
from contextlib import ExitStack

f32 = mybir.dt.float32
f16 = mybir.dt.float16
bf16 = mybir.dt.bfloat16
i32 = mybir.dt.int32
ALU = mybir.AluOpType
ACT = mybir.ActivationFunctionType
AX = mybir.AxisListType

B, T, D = 2, 1024, 256
TOK = B * T
KT = D // 128
G4 = 4 * D
NB = TOK // 512
RH, RD = 8, 32
AH, AD = 16, 16
EX, FF = 8, 1024
FT = FF // 128
HS = 1024.0


class Core:

    def __init__(self, nc, args, stack):
        self.nc = nc
        self.a = args
        self.stack = stack

    def sb(self, name, shape, dt=f32, stack=None):
        return (stack or self.stack).enter_context(self.nc.sbuf_tensor(name, shape, dt))

    def pb(self, name, stack, n=512, dt=f32):
        return stack.enter_context(self.nc.psum_tensor(name, [128, n], dt))

    def sem(self, name):
        return self.stack.enter_context(self.nc.semaphore(name))


def col(v):
    return v.rearrange("(k p) -> p k", p=128)


def blk(t, n, size=512):
    return t[:, n * size:(n + 1) * size]


def phase_load(c):
    nc, a = c.nc, c.a
    st = ExitStack()
    with st:
        xin = c.sb("x_rows", [128, 2, T // 128, D], f32, st)
        wx = c.sb("lstm_Wx", [128, KT, G4], f32, st)
        wsc = c.sb("lstm_Wh_scaled", [128, KT, G4], f32, st)
        wbig = c.sb("wh_absmax", [128, 2], f32, st)
        wrow = c.sb("wh_absmax_row", [1, 2, 128], f32, st)
        wmax = c.sb("wh_scale_row", [1, 4], f32, st)
        scl = c.sb("wh_scale", [128, 2], f32, st)
        wr2 = c.sb("rnn_Wh_scaled", [128, KT, D], f32, st)
        bias = c.sb("lstm_b", [128, G4 // 128], f32, st)
        pt = [c.pb(f"x_turned{i}", st) for i in range(2)]
        pz = [c.pb(f"xz_psum{i}", st) for i in range(2)]
        pm = c.pb("absmax_turned", st)
        ps = c.pb("scale_spread", st)
        s_x, s_w, s_b = c.sem("x_loaded"), c.sem("weights_loaded"), c.sem("bias_loaded")
        s_c, s_t, s_e = c.sem("constants_made"), c.sem("x_turned"), c.sem("x_evacuated")
        s_m, s_mt, s_md = c.sem("absmax_made"), c.sem("absmax_turned_s"), c.sem("scale_row_made")
        s_sp, s_sd, s_z, s_ze = c.sem("scale_spread_s"), c.sem("split_step"), c.sem("xz_made"), c.sem("xz_evacuated")
        s_g = c.sem("pool_step")
        s_h0, s_xw0 = c.sem("h0_products"), c.sem("h0_added")
        xz = c.xz
        with nc.Block() as block:
            @block.sync
            def _(sp):
                for b in range(B):
                    sp.dma_start(xin[:, b], a["x"][b].rearrange("(i p) c -> p i c", p=128)).then_inc(s_x, 16)
                sp.dma_start(wx[:], a["L0_cond_Wx"].rearrange("(k p) n -> p k n", p=128)).then_inc(s_w, 16)
                sp.dma_start(c.wh[:], a["L0_cond_Wh"].rearrange("(k p) n -> p k n", p=128)).then_inc(s_w, 16)
                sp.dma_start(c.wh2[:], a["L0_cond2_Wh"].rearrange("(k p) n -> p k n", p=128)).then_inc(s_w, 16)
                with nc.allow_non_contiguous_dma("small vectors"):
                    sp.dma_start(bias[:], col(a["L0_cond_b"])).then_inc(s_b, 16)
                    for k in range(KT):
                        sp.dma_start(c.h0[:, k, :], a["cond_1024"][:, k * 128:(k + 1) * 128].rearrange("b p -> p b"))\
                          .then_inc(s_b, 16)

            @block.gpsimd
            def _(pool):
                pool.memset(c.ident[:], 0.0).then_inc(s_g, 1)
                pool.memset(c.headones[:], 1.0).then_inc(s_g, 1)
                pool.memset(c.ones[:], 1.0).then_inc(s_c, 1)
                pool.wait_ge(s_g, 2)
                pool.affine_select(out=c.ident[:], in_=c.ident[:], compare_op=ALU.not_equal, fill=1.0, base=0,
                                   pattern=[[-1, 128]], channel_multiplier=1).then_inc(s_c, 1)
                hv = c.headones[:].rearrange("p (h q) -> p h q", q=32)
                pool.affine_select(out=hv, in_=hv, compare_op=ALU.is_ge, fill=0.0, base=0,
                                   pattern=[[-32, 4], [0, 32]], channel_multiplier=1).then_inc(s_g, 1)
                pool.wait_ge(s_g, 3)
                pool.affine_select(out=hv, in_=hv, compare_op=ALU.is_ge, fill=0.0, base=31,
                                   pattern=[[32, 4], [0, 32]], channel_multiplier=-1).then_inc(s_c, 1)

            @block.tensor
            def _(pe):
                pe.wait_ge(s_c, 3)
                pe.wait_ge(s_x, 16 * B)
                n = 0
                for b in range(B):
                    for k in range(KT):
                        for half in range(2):
                            if n >= 2:
                                pe.wait_ge(s_e, n - 1)
                            for j in range(4):
                                mm = pe.transpose(pt[n % 2][:, j * 128:(j + 1) * 128],
                                                  xin[:, b, half * 4 + j, k * 128:(k + 1) * 128], c.ident[:])
                            mm.then_inc(s_t, 1)
                            n += 1
                pe.wait_ge(s_m, 2)
                for w in range(2):
                    mm = pe.transpose(pm[0:1, w * 128:(w + 1) * 128], wbig[:, w:w + 1], c.ident[:])
                mm.then_inc(s_mt, 1)
                pe.wait_ge(s_md, 5)
                pe.matmul(ps[:, 0:4], c.ones[0:1, :], wmax[0:1, :], start=True, stop=True).then_inc(s_sp, 1)
                pe.wait_ge(s_w, 48)
                pe.wait_ge(s_e, 8)
                for q in range(G4 // 128):
                    for n in range(NB):
                        u = q * NB + n
                        if u >= 2:
                            pe.wait_ge(s_ze, u - 1)
                        for k in range(KT):
                            mm = pe.matmul(pz[u % 2][:], wx[:, k, q * 128:(q + 1) * 128], blk(c.xT[:, k], n),
                                           start=(k == 0), stop=(k == KT - 1))
                        mm.then_inc(s_z, 1)
                pe.wait_ge(s_b, 48)
                pe.wait_ge(s_sd, 1)
                pe.wait_ge(s_sd, 2)
                for q in range(G4 // 128):
                    place = (q + 2) % 8
                    for k in range(KT):
                        pe.matmul(ps[:, 2 * place:2 * place + 2], c.wh[:, k, q * 128:(q + 1) * 128], c.h0[:, k, :],
                                  start=(k == 0), stop=(k == KT - 1))
                for m in range(KT):
                    for k in range(KT):
                        mm = pe.matmul(ps[:, 16 + 2 * m:18 + 2 * m], c.wh2[:, k, m * 128:(m + 1) * 128], c.h0[:, k, :],
                                       start=(k == 0), stop=(k == KT - 1))
                mm.then_inc(s_h0, 1)

            @block.vector
            def _(v):
                n = 0
                for b in range(B):
                    for k in range(KT):
                        for half in range(2):
                            v.wait_ge(s_t, n + 1)
                            dst = c.xT[:, k, :].rearrange("p (t b) -> p b t", b=B)[:, b, half * 512:(half + 1) * 512]
                            v.tensor_copy(dst, pt[n % 2][:]).then_inc(s_e, 1)
                            n += 1
                v.wait_ge(s_w, 48)
                for w, t in enumerate((c.wh, c.wh2)):
                    v.tensor_reduce(wbig[:, w:w + 1], t[:], AX.XY, ALU.max, apply_absolute_value=True).then_inc(s_m, 1)
                v.wait_ge(s_mt, 1)
                v.tensor_copy(wrow[0:1].rearrange("p a b -> p (a b)"), pm[0:1, 0:256]).then_inc(s_md, 1)
                v.wait_ge(s_md, 1)
                v.tensor_reduce(wmax[0:1, 0:2], wrow[0:1], AX.X, ALU.max).then_inc(s_md, 1)
                v.wait_ge(s_md, 2)
                v.tensor_scalar(wmax[0:1, 2:4], wmax[0:1, 0:2], 1e-30, None, ALU.max).then_inc(s_md, 1)
                v.wait_ge(s_md, 3)
                v.tensor_scalar(wmax[0:1, 0:2].bitcast(i32), wmax[0:1, 2:4].bitcast(i32), 0x7F800000, None,
                                ALU.bitwise_and).then_inc(s_md, 1)
                v.wait_ge(s_md, 4)
                v.reciprocal(wmax[0:1, 2:4], wmax[0:1, 0:2]).then_inc(s_md, 1)
                v.wait_ge(s_sp, 1)
                v.tensor_scalar(scl[:], ps[:, 2:4], 2.0 ** 14, None, ALU.mult).then_inc(s_sd, 1)
                v.tensor_scalar(c.unscale[:], ps[:, 0:2], 2.0 ** -14 / HS, None, ALU.mult).then_inc(s_sd, 1)
                v.wait_ge(s_sd, 2)
                for w, (src, big, wa, wb) in enumerate(((c.wh, wsc, c.wa, c.wb), (c.wh2, wr2, c.wa2, c.wb2))):
                    v.tensor_scalar(big[:], src[:], scl[:, w:w + 1], None, ALU.mult).then_inc(s_sd, 1)
                    v.wait_ge(s_sd, 3 + 3 * w)
                    v.tensor_copy(wa[:], big[:]).then_inc(s_sd, 1)
                    v.wait_ge(s_sd, 4 + 3 * w)
                    v.tensor_tensor(wb[:], big[:], wa[:], ALU.subtract).then_inc(s_sd, 1)
                v.wait_ge(s_h0, 1)
                v.wait_ge(s_ze, NB * G4 // 128)
                first = xz[:, 0].rearrange("p m b -> p (m b)")
                v.tensor_tensor(first, ps[:, 0:16], first, ALU.add)
                v.tensor_copy(c.r0[:].rearrange("p m b -> p (m b)"), ps[:, 16:20])

            @block.scalar
            def _(act):
                act.wait_ge(s_b, 48)
                order = {3: 0, 0: 1, 1: 2, 2: 3}
                for q in range(G4 // 128):
                    for n in range(NB):
                        u = q * NB + n
                        act.wait_ge(s_z, u + 1)
                        m = order[q // 2] * 2 + q % 2
                        dst = xz[:, n * 256:(n + 1) * 256, m, :]
                        act.activation(dst, pz[u % 2][:].rearrange("p (t b) -> p t b", b=B), ACT.Identity,
                                       bias=bias[:, q:q + 1]).then_inc(s_ze, 1)


CH = 128
CT = CH * B
NC = T // CH


def phase_start(c):
    with c.nc.Block() as block:
        @block.vector
        def _(v):
            for t, sem in ((c.hab[:, :, 0], c.s_ha), (c.hab[:, :, 1], c.s_hb), (c.rab[:, :, 0], c.s_ra),
                           (c.rab[:, :, 1], c.s_rb), (c.S[0][:], c.s_S)):
                v.memset(t, 0.0).then_inc(sem, 1)
            v.memset(c.cell[:], 0.0)
            v.memset(c.scratch[:, 0:1], 0.0).then_inc(c.s_p2, 2)
            v.memset(c.scratch[:, 1:2], 0.0).then_inc(c.s_u, 2)
            v.memset(c.scratch[:, 2:3], 0.0).then_inc(c.s_om, 2)
            v.memset(c.scratch[:, 3:4], 0.0).then_inc(c.s_oe, 2)
            v.memset(c.scratch[:, 4:5], 0.0).then_inc(c.s_hst, 1)
            v.memset(c.scratch[:, 5:6], 0.0).then_inc(c.s_py, 1)
            v.tensor_reduce(c.diag[:], c.ident[:].rearrange("p (h v) -> p v h", v=32), AX.X, ALU.add)


def recurrences(c, ci, lstm, delta, rnn):
    nc = c.nc
    xz = c.xz
    gates = [("g", 3, 0), ("i", 0, 1), ("f", 1, 2), ("o", 2, 3)]
    shape = [128, 4, RD]

    def pairs(body):
        def run(eng):
            with eng.Fori(0, CH // 2 - 1) as i:
                for j in range(2):
                    body(i * 2 + j, j, False)
            for j in range(2):
                body(CH - 2 + j, j, j == 1)
        return run

    def at(tt, n=1):
        return slice(tt, tt + n) if isinstance(tt, int) else bass.ds(tt, n)

    def tl(tt):
        return ci * CH + tt

    def td(tt):
        return (ci - 1) * CH + tt

    def tr(tt):
        return (ci - 2) * CH + tt

    with nc.Block() as block:
        @block.tensor
        def _(pe):
            def products(bank, tiles, high, low, state, sem_high, sem_low, t, done):
                pe.wait_ge(sem_high, t + 1)
                for n, at_w in enumerate(tiles):
                    for k in range(KT):
                        pe.matmul(bank[:, 4 * n:4 * n + B], low[:, k, at_w:at_w + 128], state[:, k, 0, :],
                                  start=(n == 0 and k == 0), stop=False, skip_group_check=True)
                pe.wait_ge(sem_low, t + 1)
                for n, at_w in enumerate(tiles):
                    for k in range(KT):
                        mm = pe.matmul(bank[:, 4 * n:4 * n + 2 * B], high[:, k, at_w:at_w + 128],
                                       state[:, k].rearrange("p a b -> p (a b)"), start=False, stop=True,
                                       skip_group_check=True)
                mm.then_inc(done, 1)

            gif = [(2 * q + m) * 128 for _, q, place in gates[:3] for m in range(2)]
            o = [(2 * gates[3][1] + m) * 128 for m in range(2)]

            def lstm_step(t):
                products(c.p_gif, gif, c.wa, c.wb, c.hab, c.s_ha, c.s_hb, t, c.s_gif)
                products(c.p_o, o, c.wa, c.wb, c.hab, c.s_ha, c.s_hb, t, c.s_o)

            def rnn_step(t):
                products(c.p_r, [m * 128 for m in range(KT)], c.wa2, c.wb2, c.rab, c.s_ra, c.s_rb, t, c.s_r)

            def project_state(t, j):
                pe.wait_ge(c.s_p2, t + 1)
                pe.wait_ge(c.s_prod, t + 1)
                pe.wait_ge(c.s_py, t + 2)
                pe.matmul(c.p_u[j][:, 0:256], c.headones[:], c.prod[:].rearrange("p a g v -> p (a g v)"),
                          start=True, stop=True).then_inc(c.s_u, 1)

            def read_state(t, j):
                pe.wait_ge(c.s_q, t + 1)
                pe.wait_ge(c.s_oe, t + 1)
                pe.wait_ge(c.s_S, t + 2)
                for g in range(4):
                    mm = pe.matmul(c.p_od[j][0:RD, g * 4:(g + 1) * 4], c.S[1 - j][:, g, :], c.qs[j][:, g, :],
                                   start=(g == 0), stop=(g == 3))
                mm.then_inc(c.s_om, 1)

            def step(tt, j, last):
                if lstm:
                    lstm_step(tl(tt))
                if rnn:
                    rnn_step(tr(tt))
                if delta:
                    read_state(td(tt), j)
                    if not last:
                        project_state(td(tt + 1), 1 - j)

            if delta:
                project_state(td(0), 0)
            pairs(step)(pe)

        @block.scalar
        def _(act):
            act.activation(c.scratch[:, 0:2], c.ones[:, 0:2], ACT.Sigmoid)

            def step(tt, j, last):
                if lstm:
                    t = tl(tt)
                    act.wait_ge(c.s_z, t + 1)
                    act.activation(c.sif[:], c.z[:, 2:6].rearrange("p m b -> p (m b)"), ACT.Sigmoid).then_inc(c.s_if, 1)
                    act.activation(c.tg[:], c.z[:, 0:2].rearrange("p m b -> p (m b)"), ACT.Tanh).then_inc(c.s_g, 1)
                    act.wait_ge(c.s_zo, t + 1)
                    act.wait_ge(c.s_hst, t + 1)
                    act.activation(c.so[:], c.z[:, 6:8].rearrange("p m b -> p (m b)"), ACT.Sigmoid).then_inc(c.s_so, 1)
                    act.wait_ge(c.s_c, t + 1)
                    act.activation(c.tc[:], c.cell[:], ACT.Tanh).then_inc(c.s_tc, 1)
                if rnn:
                    t = tr(tt)
                    act.wait_ge(c.s_rz, t + 1)
                    act.activation(c.rT[:, :, bass.ds(t * B, B)] if not isinstance(t, int) else
                                   c.rT[:, :, t * B:t * B + B], c.rz[:], ACT.Tanh).then_inc(c.s_rh, 1)
                if delta:
                    act.wait_ge(c.s_om, td(tt) + 3)
                    act.activation(c.o[:, at(tt), :], c.p_od[j][0:RD, 0:16].rearrange("p (o x) -> p o x", o=1), ACT.Copy)\
                        .then_inc(c.s_oe, 1)

            pairs(step)(act)

        @block.vector
        def _(v):
            def multiply_state(tt, t, j):
                v.wait_ge(c.s_S, t + 1)
                v.tensor_tensor(c.prod[:, 0], c.S[j][:],
                                c.kyk[:, at(tt), 0:4].rearrange("p o g -> p g o").to_broadcast(shape), ALU.mult)\
                 .then_inc(c.s_prod, 1)

            def two_parts(z, lo, n, bank, w, add, mid, done, t):
                p = bank[:, 0:4 * n].rearrange("p (n a b) -> p n a b", a=2, b=B)
                v.scalar_tensor_tensor(c.zh[:, lo:lo + n], p[:, :, 0], c.unscale[:, w:w + 1], add, ALU.mult, ALU.add)\
                 .then_inc(mid, 1)
                v.wait_ge(mid, t + 1)
                v.scalar_tensor_tensor(z, p[:, :, 1], c.unscale[:, w:w + 1], c.zh[:, lo:lo + n], ALU.mult, ALU.add)\
                 .then_inc(done, 1)

            def update_state(tt, t, j):
                v.wait_ge(c.s_u, t + 3)
                v.tensor_tensor(c.p2[:].rearrange("p a g v -> p (a g) v"),
                                c.p_u[j][:, 0:256].rearrange("p (g v) -> p g v", v=RD),
                                c.kyk[:, at(tt), 4:12].rearrange("p o g -> p g o").to_broadcast([128, 8, RD]),
                                ALU.mult).then_inc(c.s_p2, 1)
                v.wait_ge(c.s_p2, t + 3)
                v.wait_ge(c.s_ds, t + 1)
                v.tensor_tensor(c.s1[:], c.ds[:], c.p2[:, 0], ALU.subtract).then_inc(c.s_s1, 1)
                v.wait_ge(c.s_s1, t + 1)
                v.wait_ge(c.s_om, t + 1)
                v.tensor_tensor(c.S[1 - j][:], c.s1[:], c.p2[:, 1], ALU.subtract).then_inc(c.s_S, 1)

            def step(tt, j, last):
                if delta:
                    update_state(tt, td(tt), j)
                if lstm:
                    t = tl(tt)
                    x = xz[:, at(t), :, :].rearrange("p o m b -> p (o m) b")
                    v.wait_ge(c.s_gif, t + 1)
                    two_parts(c.z[:, 0:6], 0, 6, c.p_gif, 0, x[:, 0:6], c.s_zh, c.s_z, t)
                    v.wait_ge(c.s_o, t + 1)
                    two_parts(c.z[:, 6:8], 6, 2, c.p_o, 0, x[:, 6:8], c.s_zoh, c.s_zo, t)
                if delta and not last:
                    multiply_state(tt + 1, td(tt + 1), 1 - j)
                if lstm:
                    v.wait_ge(c.s_if, t + 1)
                    v.tensor_tensor(c.fc[:], c.sif[:, 4:8], c.cell[:], ALU.mult).then_inc(c.s_fc, 1)
                    v.wait_ge(c.s_g, t + 1)
                    v.tensor_tensor(c.ig[:], c.sif[:, 0:4], c.tg[:], ALU.mult).then_inc(c.s_fc, 1)
                    v.wait_ge(c.s_fc, t * 2 + 2)
                    v.tensor_tensor(c.cell[:], c.fc[:], c.ig[:], ALU.add).then_inc(c.s_c, 1)
                if rnn:
                    r = tr(tt)
                    v.wait_ge(c.s_r, r + 1)
                    two_parts(c.rz[:], 8, KT, c.p_r, 1, c.xw[:, at(tt)].rearrange("p o m b -> p (o m) b"),
                              c.s_rzh, c.s_rz, r)
                if lstm:
                    so, tc = (x[:].rearrange("p (k b) -> p k b", b=B) for x in (c.so, c.tc))
                    v.wait_ge(c.s_tc, t + 1)
                    v.scalar_tensor_tensor(c.hab[:, :, 0], so, HS, tc, ALU.mult, ALU.mult).then_inc(c.s_ha, 1)
                    v.scalar_tensor_tensor(c.hf[:], so, HS, tc, ALU.mult, ALU.mult).then_inc(c.s_hf, 1)
                    v.wait_ge(c.s_hf, t + 1)
                    v.tensor_tensor(c.hab[:, :, 1], c.hf[:], c.hab[:, :, 0], ALU.subtract).then_inc(c.s_hb, 1)
                if rnn:
                    h = c.rT[:, :, r * B:r * B + B] if isinstance(r, int) else c.rT[:, :, bass.ds(r * B, B)]
                    v.wait_ge(c.s_rh, r + 1)
                    v.tensor_scalar(c.rab[:, :, 0], h, HS, None, ALU.mult).then_inc(c.s_ra, 1)
                    v.wait_ge(c.s_ra, r + 2)
                    v.scalar_tensor_tensor(c.rab[:, :, 1], h, HS, c.rab[:, :, 0], ALU.mult, ALU.subtract)\
                     .then_inc(c.s_rb, 1)

            if delta:
                multiply_state(0, td(0), 0)
            pairs(step)(v)

        @block.gpsimd
        def _(pool):
            def over_v(t, tt, j=0):
                return t[:, at(tt), j * 4:(j + 1) * 4].rearrange("p o g -> p g o").to_broadcast(shape)

            def before_products(tt, t, j):
                pool.wait_ge(c.s_py, t + 1)
                pool.tensor_tensor(c.vd[:], over_v(c.v, tt), c.diag[:].rearrange("p (o v) -> p o v", o=1).to_broadcast(shape),
                                   ALU.mult).then_inc(c.s_vd, 1)
                pool.wait_ge(c.s_S, t + 1)
                pool.tensor_tensor(c.ys[:], c.S[j][:], over_v(c.kyk, tt, 1), ALU.mult).then_inc(c.s_ys, 1)
                pool.wait_ge(c.s_vd, t + 1)
                pool.wait_ge(c.s_ys, t + 1)
                pool.tensor_tensor(c.prod[:, 1], c.ys[:], c.vd[:], ALU.subtract).then_inc(c.s_py, 1)
                pool.tensor_tensor(c.ds[:], c.S[j][:], over_v(c.f, tt), ALU.mult).then_inc(c.s_ds, 1)

            def lay_out_q(tt, t, j):
                pool.wait_ge(c.s_om, t + 1)
                pool.tensor_tensor(c.qs[j][:], c.q[:, at(tt), :].rearrange("p o g -> p g o").to_broadcast([128, 4, 4]),
                                   c.headones[:, 0:128:32].rearrange("p (o h) -> p o h", o=1)
                                   .to_broadcast([128, 4, 4]), ALU.mult).then_inc(c.s_q, 1)

            def step(tt, j, last):
                if delta and not last:
                    before_products(tt + 1, td(tt + 1), 1 - j)
                    lay_out_q(tt + 1, td(tt + 1), 1 - j)
                if lstm:
                    t = tl(tt)
                    pool.wait_ge(c.s_tc, t + 1)
                    dst = c.hT[:, :, t * B:t * B + B] if isinstance(t, int) else c.hT[:, :, bass.ds(t * B, B)]
                    pool.tensor_tensor(dst, c.so[:].rearrange("p (k b) -> p k b", b=B),
                                       c.tc[:].rearrange("p (k b) -> p k b", b=B), ALU.mult).then_inc(c.s_hst, 1)

            if delta:
                before_products(0, td(0), 0)
                lay_out_q(0, td(0), 0)
            if lstm or delta:
                pairs(step)(pool)


def project_and_mix(c, ci, project, mix, first_mix=False):
    nc = c.nc
    n_p, n_m = ci, ci - 1

    def tokens(t, k, i):
        return t[:, k, i * CT:(i + 1) * CT] if isinstance(i, int) else t[:, k, bass.ds(i * CT, CT)]

    def both(t):
        return t.rearrange("p (m t b) -> p m t b", m=KT, b=B)

    def by_time(t, j=0):
        return t[:, :, j * 4:(j + 1) * 4].rearrange("p t (m b) -> p m t b", b=B)

    R = c.room
    sk, sv, sq, sbt, fd, kk, t1, t2, kn, w, o4, sg, y, y2 = (R[:, i * 512:(i + 1) * 512] for i in range(14))
    f1 = R[0:RD, 14 * 512:14 * 512 + CT]
    g1 = R[0:RD, 14 * 512 + CT:15 * 512]
    pk, pv, pq, pf, pb, ps, pin = c.banks[:7]
    pgate, pms, px = c.banks[0], c.banks[1], c.banks[2:4]
    px2 = c.banks[4]
    with nc.Block() as block:
        @block.tensor
        def _(pe):
            if project:
                rows = [tokens(c.hT, k, ci) for k in range(KT)]
                for k in range(KT):
                    mm = pe.matmul(pin[0:RD, 0:CT], c.wf1[:, k, :], rows[k], start=(k == 0), stop=(k == KT - 1))
                mm.then_inc(c.q_f1, 1)
                for bank, wt, done in ((pk, c.wk, c.q_p), (pb, c.wbs, c.q_p), (pv, c.wv, c.q_p), (pq, c.wq, c.q_p)):
                    for m in range(KT):
                        for k in range(KT):
                            mm = pe.matmul(bank[:, m * CT:(m + 1) * CT], wt[:, k, m * 128:(m + 1) * 128], rows[k],
                                           start=(k == 0), stop=(k == KT - 1))
                    mm.then_inc(done, 1)
                pe.wait_ge(c.q_f1e, n_p + 1)
                for m in range(KT):
                    mm = pe.matmul(pf[:, m * CT:(m + 1) * CT], c.wf2[:, m * 128:(m + 1) * 128], f1, start=True, stop=True)
                mm.then_inc(c.q_p, 1)
            if mix:
                rows = [tokens(c.hT, k, ci - 1) for k in range(KT)]
                for k in range(KT):
                    mm = pe.matmul(pin[0:RD, 0:CT], c.wg1[:, k, :], rows[k], start=(k == 0), stop=(k == KT - 1))
                mm.then_inc(c.m_g1, 1)
                pe.wait_ge(c.m_g1e, n_m + 1)
                if project:
                    pe.wait_ge(c.q_kk, n_p + 1)
                for m in range(KT):
                    mm = pe.matmul(pgate[:, m * CT:(m + 1) * CT], c.wg2[:, m * 128:(m + 1) * 128], g1, start=True, stop=True)
                mm.then_inc(c.m_g, 1)
            if project:
                pe.wait_ge(c.q_k2, n_p + 1)
                pe.matmul(ps[:], c.headones[:], t1, start=True, stop=True).then_inc(c.q_ss, 1)
                pe.wait_ge(c.q_kw, n_p + 1)
                pe.matmul(ps[:], c.headones[:], t1, start=True, stop=True).then_inc(c.q_gm, 1)
            if mix:
                pe.wait_ge(c.m_y2, n_m + 1)
                pe.matmul(pms[:], c.headones[:], y2, start=True, stop=True).then_inc(c.m_ms, 1)
                pe.wait_ge(c.m_yn, n_m * 2 + 2)
                for m in range(KT):
                    for k in range(KT):
                        mm = pe.matmul(px[m][:, 0:CT], c.wo[:, k, m * 128:(m + 1) * 128], y[:, k * CT:(k + 1) * CT],
                                       start=(k == 0), stop=(k == KT - 1))
                    mm.then_inc(c.m_x, 1)
                pe.wait_ge(c.m_x1, n_m * KT + KT)
                for m in range(KT):
                    for k in range(KT):
                        mm = pe.matmul(px2[:, m * CT:(m + 1) * CT], c.wx2[:, k, m * 128:(m + 1) * 128],
                                       tokens(c.xT, k, ci - 1), start=(k == 0), stop=(k == KT - 1))
                    mm.then_inc(c.m_xw, 1)

        @block.scalar
        def _(act):
            if project:
                act.wait_ge(c.q_f1, n_p + 1)
                act.activation(f1, pin[0:RD, 0:CT], ACT.Copy).then_inc(c.q_f1e, 1)
                for i, (dst, src) in enumerate(((sk, pk), (sbt, pb), (sv, pv), (sq, pq), (fd, pf))):
                    act.wait_ge(c.q_p, n_p * 5 + (i + 1))
                    act.activation(dst, src[:], ACT.Sigmoid).then_inc(c.q_sig, 1)
            if mix:
                act.wait_ge(c.m_g1, n_m + 1)
                act.activation(g1, pin[0:RD, 0:CT], ACT.Copy).then_inc(c.m_g1e, 1)
                act.wait_ge(c.m_g, n_m + 1)
                act.activation(sg, pgate[:], ACT.Sigmoid).then_inc(c.m_sg, 1)
            if project:
                act.wait_ge(c.q_r, n_p + 1)
                act.activation(t1, t2, ACT.Sqrt).then_inc(c.q_rt, 1)
            if mix:
                act.wait_ge(c.m_r, n_m + 1)
                act.activation(y2, sg, ACT.Sqrt).then_inc(c.m_rt, 1)
                for m in range(KT):
                    act.wait_ge(c.m_xw, n_m * KT + KT)
                    act.activation(c.xw[:, :, m, :], px2[:, m * CT:(m + 1) * CT].rearrange("p (t b) -> p t b", b=B),
                                   ACT.Identity, bias=c.b2[:, m:m + 1]).then_inc(c.m_xwe, 1)

        @block.vector
        def _(v):
            if project:
                sig = n_p * 5
                v.wait_ge(c.q_sig, sig + 1)
                v.tensor_tensor(kk, pk[:], sk, ALU.mult).then_inc(c.q_kk, 1)
                v.wait_ge(c.q_kk, n_p + 1)
                v.tensor_tensor(t1, kk, kk, ALU.mult).then_inc(c.q_k2, 1)
                v.wait_ge(c.q_sig, sig + 3)
                v.tensor_tensor(by_time(c.v), both(pv[:]), both(sv), ALU.mult)
                v.wait_ge(c.q_sig, sig + 4)
                v.tensor_tensor(by_time(c.q), both(pq[:]), both(sq), ALU.mult).then_inc(c.q_q, 1)
                v.wait_ge(c.q_ss, n_p + 1)
                v.tensor_scalar(w, ps[:], 1e-6, None, ALU.add).then_inc(c.q_e, 1)
                v.wait_ge(c.q_e, n_p + 1)
                v.reciprocal(t2, w).then_inc(c.q_r, 1)
            if project:
                v.wait_ge(c.q_rt, n_p + 1)
                v.tensor_tensor(kn, kk, t1, ALU.mult).then_inc(c.q_kn, 1)
                v.wait_ge(c.q_sig, sig + 5)
                v.wait_ge(c.q_kn, n_p + 1)
                v.tensor_tensor(w, fd, kn, ALU.mult).then_inc(c.q_w, 1)
                v.wait_ge(c.q_w, n_p + 1)
                v.tensor_tensor(t1, kn, w, ALU.mult).then_inc(c.q_kw, 1)
                v.tensor_copy(by_time(c.kyk, 0), both(kn))
                v.tensor_copy(by_time(c.kyk, 2), both(kn))
                v.tensor_copy(by_time(c.f), both(fd))
                v.tensor_tensor(sk, sbt, kn, ALU.mult).then_inc(c.q_bk, 1)
                v.scalar_tensor_tensor(sv, sbt, 2.0, w, ALU.mult, ALU.mult)
                v.wait_ge(c.q_bk, n_p + 1)
                v.tensor_tensor(sq, sk, sbt, ALU.mult).then_inc(c.q_bbk, 1)
                v.wait_ge(c.q_gm, n_p + 1)
                v.wait_ge(c.q_bbk, n_p + 1)
                v.scalar_tensor_tensor(t2, ps[:], 2.0, sq, ALU.mult, ALU.mult).then_inc(c.q_y, 1)
                v.wait_ge(c.q_y, n_p + 1)
                v.tensor_tensor(by_time(c.kyk, 1), both(sv), both(t2), ALU.subtract).then_inc(c.q_done, 1)
            if mix:
                for h in range(4):
                    src = c.o.rearrange("p t (m b h) -> p m t b h", m=KT, b=B)[:, :, :, :, h]
                    last = v.tensor_copy(both(o4[32 * h:32 * h + 32]), src)
                last.then_inc(c.m_o, 1)
                v.wait_ge(c.m_o, n_m + 1)
                v.wait_ge(c.m_sg, n_m + 1)
                v.tensor_tensor(y, o4, sg, ALU.mult).then_inc(c.m_y, 1)
                v.wait_ge(c.m_y, n_m + 1)
                v.tensor_tensor(y2, y, y, ALU.mult).then_inc(c.m_y2, 1)
                v.wait_ge(c.m_ms, n_m + 1)
                v.tensor_scalar(o4, pms[:], 1.0 / RD, 1e-6, ALU.mult, ALU.add).then_inc(c.m_e, 1)
                v.wait_ge(c.m_e, n_m + 1)
                v.reciprocal(sg, o4).then_inc(c.m_r, 1)
                v.wait_ge(c.m_rt, n_m + 1)
                for k in range(KT):
                    s = slice(k * CT, (k + 1) * CT)
                    v.scalar_tensor_tensor(y[:, s], y[:, s], c.nw[:, k:k + 1], y2[:, s], ALU.mult, ALU.mult)\
                     .then_inc(c.m_yn, 1)
                for m in range(KT):
                    v.wait_ge(c.m_x, n_m * KT + (m + 1))
                    x1 = tokens(c.xT, m, ci - 1)
                    v.tensor_tensor(x1, px[m][:, 0:CT], x1, ALU.add).then_inc(c.m_x1, 1)
                if first_mix:
                    v.wait_ge(c.m_xwe, KT)
                    v.tensor_tensor(c.xw[:, 0], c.xw[:, 0], c.r0[:], ALU.add)


def phase_weights(c):
    nc, a = c.nc, c.a
    s_w, s_s = c.sem("delta_weights"), c.sem("beta_spread")
    with nc.Block() as block:
        @block.sync
        def _(sp):
            for t, n in ((c.wq, "attn_Wq"), (c.wk, "attn_Wk"), (c.wv, "attn_Wv"), (c.wf1, "attn_Wf1"),
                         (c.wb0, "attn_Wbeta"), (c.wg1, "attn_Wog1"), (c.wo, "attn_Wo"), (c.wx2, "cond2_Wx")):
                sp.dma_start(t[:], a["L0_" + n].rearrange("(k p) n -> p k n", p=128)).then_inc(s_w, 16)
            sp.dma_start(c.wf2[:], a["L0_attn_Wf2"]).then_inc(s_w, 16)
            sp.dma_start(c.wg2[:], a["L0_attn_Wog2"]).then_inc(s_w, 16)
            with nc.allow_non_contiguous_dma("small vectors"):
                sp.dma_start(c.nw[:], col(a["L0_attn_norm_w"])).then_inc(s_w, 16)
                sp.dma_start(c.b2[:], col(a["L0_cond2_b"])).then_inc(s_w, 16)

        @block.gpsimd
        def _(pool):
            pool.wait_ge(s_w, 192)
            pool.tensor_copy(c.wbs[:].rearrange("p k (h r) -> p k h r", r=RD),
                             c.wb0[:].rearrange("p k (h o) -> p k h o", o=1).to_broadcast([128, KT, RH, RD]))


def phases_recurrent(c):
    nc = c.nc
    st = ExitStack()
    with st:
        c.hab = c.sb("h_parts", [128, KT, 2, B], f16, st)
        c.hf = c.sb("h_scaled", [128, KT, B], f32, st)
        c.z = c.sb("z", [128, 8, B], f32, st)
        c.zh = c.sb("z_part", [128, 10, B], f32, st)
        c.sif = c.sb("sig_if", [128, 8], f32, st)
        c.tg, c.so, c.cell, c.fc, c.ig, c.tc = (c.sb(n, [128, 4], f32, st) for n in
                                                ("tanh_g", "sig_o", "cell", "f_cell", "i_g", "tanh_cell"))
        c.S = [c.sb(f"state{i}", [128, 4, RD], f32, st) for i in range(2)]
        c.prod, c.p2 = (c.sb(n, [128, 2, 4, RD], f32, st) for n in ("k_and_y_times_state", "updates"))
        c.ds, c.s1 = (c.sb(n, [128, 4, RD], f32, st) for n in ("decayed_state", "half_updated"))
        c.vd, c.ys = (c.sb(n, [128, 4, RD], f32, st) for n in ("v_on_diagonal", "y_times_state"))
        c.qs = [c.sb(f"q_per_head{i}", [128, 4, 4], f32, st) for i in range(2)]
        c.kyk = c.sb("k_y_k", [128, CH, 12], f32, st)
        c.f, c.q, c.v = (c.sb(n, [128, CH, 4], f32, st) for n in ("decay", "q", "v"))
        c.o = c.sb("o_rows", [RD, CH, 16], f32, st)
        c.rab = c.sb("r_parts", [128, KT, 2, B], f16, st)
        c.rz = c.sb("r_z", [128, KT, B], f32, st)
        c.xw = c.sb("rnn_xw", [128, CH, KT, B], f32, st)
        c.wq, c.wk, c.wv, c.wo, c.wx2, c.wbs = (c.sb(n, [128, KT, D], f32, st) for n in (
            "delta_Wq", "delta_Wk", "delta_Wv", "mix_Wo", "rnn_Wx", "delta_Wbeta_spread"))
        c.wf1, c.wg1 = (c.sb(n, [128, KT, RD], f32, st) for n in ("delta_Wf1", "gate_W1"))
        c.wf2, c.wg2 = (c.sb(n, [RD, D], f32, st) for n in ("delta_Wf2", "gate_W2"))
        c.wb0 = c.sb("delta_Wbeta", [128, KT, RH], f32, st)
        c.nw, c.b2 = (c.sb(n, [128, KT], f32, st) for n in ("norm_w", "rnn_b"))
        c.room = c.sb("chunk_temporaries", [128, 15 * 512], f32, st)
        c.banks = [c.pb(f"bank{i}", st) for i in range(8)]
        c.p_gif, c.p_o, c.p_r = c.banks[0:3]
        c.p_u, c.p_od = c.banks[3:5], c.banks[5:7]
        (c.s_gif, c.s_o, c.s_z, c.s_zo, c.s_if, c.s_g, c.s_so, c.s_fc, c.s_c, c.s_tc, c.s_ha, c.s_hf, c.s_hb,
         c.s_hst, c.s_zh, c.s_zoh) = (c.sem("lstm_" + n) for n in (
             "gif_products", "o_products", "z_gif", "z_o", "sig_if", "tanh_g", "sig_o", "cell_parts", "cell",
             "tanh_cell", "h_high", "h_scaled", "h_low", "h_stored", "z_gif_part", "z_o_part"))
        (c.s_S, c.s_prod, c.s_ds, c.s_p2, c.s_s1, c.s_u, c.s_vd, c.s_q, c.s_om, c.s_oe, c.s_ys, c.s_py) = (
            c.sem("delta_" + n) for n in ("state", "prod", "decayed", "updates", "half_updated", "projections",
                                          "v_on_diagonal", "q_laid_out", "o_made", "o_stored", "y_times_state",
                                          "y_prod"))
        c.s_r, c.s_rz, c.s_rh, c.s_ra, c.s_rb, c.s_rzh = (c.sem("rnn_" + n) for n in
                                                          ("products", "z", "state", "high", "low", "z_part"))
        (c.q_f1, c.q_p, c.q_f1e, c.q_k2, c.q_ss, c.q_kw, c.q_gm, c.q_done, c.q_sig, c.q_r, c.q_rt, c.q_kk, c.q_q,
         c.q_e, c.q_kn, c.q_w, c.q_bk, c.q_bbk, c.q_y) = (c.sem("project_" + n) for n in (
             "f1", "products", "f1_stored", "k_squared", "sum_of_squares", "k_fk", "gamma", "done", "sigmoids",
             "reciprocal", "root", "silu_k", "q_made", "plus_eps", "k_unit", "fk", "bk", "bbk", "y_part"))
        (c.m_g1, c.m_g1e, c.m_g, c.m_y2, c.m_ms, c.m_yn, c.m_x, c.m_x1, c.m_xw, c.m_sg, c.m_r, c.m_rt, c.m_xwe,
         c.m_o, c.m_y, c.m_e) = (c.sem("mix_" + n) for n in (
             "g1", "g1_stored", "gate", "squares", "sum_of_squares", "normed", "products", "x1", "xw_products",
             "sigmoid", "reciprocal", "root", "xw", "o_turned", "gated", "plus_eps"))
        phase_weights(c)
        phase_start(c)
        recurrences(c, 0, True, False, False)
        project_and_mix(c, 0, True, False)
        recurrences(c, 1, True, True, False)
        project_and_mix(c, 1, True, True, first_mix=True)
        with nc.Fori(2, NC) as ci:
            recurrences(c, ci, True, True, True)
            project_and_mix(c, ci, True, True)
        recurrences(c, NC, False, True, True)
        project_and_mix(c, NC, False, True)
        recurrences(c, NC + 1, False, False, True)


def phase_heads(c):
    nc, a = c.nc, c.a
    st = ExitStack()
    with st:
        w = c.sb("w_qkv", [128, KT, 3 * D], f32, st)
        wp = c.sb("w_qk_padded", [128, KT, 2, 4, 128], f32, st)
        pq = [c.pb(f"qk_psum{i}", st) for i in range(2)]
        pv = [c.pb(f"v_psum{i}", st) for i in range(2)]
        s_w, s_0, s_pad = c.sem("qkv_weights"), c.sem("qk_zeroed"), c.sem("qk_padded")
        s_q, s_qe, s_v, s_ve, s_m = c.sem("qk_made"), c.sem("qk_evac"), c.sem("v_made"), c.sem("v_evac"), c.sem("masks")
        with nc.Block() as block:
            @block.sync
            def _(sp):
                sp.dma_start(w[:], a["L0_ffn_w_qkv"].rearrange("(k p) n -> p k n", p=128)).then_inc(s_w, 16)

            @block.gpsimd
            def _(pool):
                pool.memset(wp[:], 0.0).then_inc(s_0, 1)
                pool.memset(c.rowmax[:], 0.0).then_inc(s_0, 1)
                pool.memset(c.vt[:], 0.0).then_inc(s_0, 1)
                pool.memset(c.mask_q[:], 0.0).then_inc(s_0, 1)
                pool.memset(c.mask_k[:], 0.0).then_inc(s_0, 1)
                pool.wait_ge(s_0, 5)
                pool.affine_select(out=c.mask_q[:], in_=c.mask_q[:], compare_op=ALU.is_ge, fill=-1e30, base=0,
                                   pattern=[[-1, 128]], channel_multiplier=1).then_inc(s_m, 1)
                pool.affine_select(out=c.mask_k[:], in_=c.mask_k[:], compare_op=ALU.is_ge, fill=-1e30, base=0,
                                   pattern=[[1, 128]], channel_multiplier=-1).then_inc(s_m, 1)
                pool.memset(c.vt[:, :, :, AD:AD + 1], 1.0).then_inc(s_m, 1)

            @block.tensor
            def _(pe):
                pe.wait_ge(s_pad, 2 * KT)
                with pe.Fori(0, NB) as n:
                    for j in range(2):
                        for g in range(4):
                            i = j * 4 + g
                            pe.wait_ge(s_qe, n * 8 + (i + 1))
                            for k in range(KT):
                                mm = pe.matmul(pq[i % 2][:], wp[:, k, j, g, :], c.hT[:, k, bass.ds(n * 512, 512)],
                                               start=(k == 0), stop=(k == KT - 1))
                            mm.then_inc(s_q, 1)
                for b in range(B):
                    for i in range(T // 128):
                        u = b * (T // 128) + i
                        if u >= 2:
                            pe.wait_ge(s_ve, u - 1)
                        for k in range(KT):
                            rows = c.hT[:, k, :].rearrange("p (t b) -> p b t", b=B)[:, b, i * 128:(i + 1) * 128]
                            mm = pe.matmul(pv[u % 2][:, 0:D], rows, w[:, k, 2 * D:3 * D], start=(k == 0), stop=(k == KT - 1))
                        mm.then_inc(s_v, 1)

            @block.vector
            def _(v):
                v.wait_ge(s_0, 1)
                v.wait_ge(s_w, 16)
                for k in range(KT):
                    for j in range(2):
                        v.tensor_copy(wp[:, k, j].rearrange("p g (h r) -> p (g h) r", r=32)[:, :, 0:AD],
                                      w[:, k, j * D:(j + 1) * D].rearrange("p (h d) -> p h d", d=AD)).then_inc(s_pad, 1)
                v.tensor_copy(c.ident16[:], c.ident[:])
                v.tensor_scalar(c.dsel[:], c.headones[:], c.diag[:, AD:AD + 1], None, ALU.mult)
                v.wait_ge(s_m, 3)
                for b in range(B):
                    for i in range(T // 128):
                        u = b * (T // 128) + i
                        v.wait_ge(s_v, u + 1)
                        v.tensor_copy(c.vt[:, u, :, 0:AD], pv[u % 2][:, 0:D].rearrange("p (h d) -> p h d", d=AD))\
                         .then_inc(s_ve, 1)

            @block.scalar
            def _(act):
                act.activation(c.scratch[:, 0:2], c.ones[:, 0:2], ACT.Copy).then_inc(s_qe, 2)
                with act.Fori(0, NB) as n:
                    for j, dst in enumerate((c.qT, c.kT)):
                        for g in range(4):
                            i = j * 4 + g
                            act.wait_ge(s_q, n * 8 + (i + 1))
                            act.activation(dst[:, g, bass.ds(n * 512, 512)], pq[i % 2][:], ACT.Copy).then_inc(s_qe, 1)


def tiles_of(size):
    out = []
    for i in range(size // 128):
        for lo in range(0, size, 512):
            out.append((i, lo, lo + 512))
    return out


def phase_attend(c):
    nc = c.nc
    QT = T // 128
    st = ExitStack()
    with st:
        qs = c.sb("q_staged", [128, T], f32, st)
        ks = c.sb("k_staged", [128, T], f32, st)
        qa = c.sb("q_with_max", [128, T], f32, st)
        vs = c.sb("v_staged", [128, QT, 4, 32], f32, st)
        pr = [c.sb(f"probs{i}", [128, 512], f32, st) for i in range(4)]
        ob = c.sb("o_unscaled", [128, T], f32, st)
        rc = c.sb("o_recip", [128, T], f32, st)
        big = [c.pb(f"scores{i}", st, 1024) for i in range(2)]
        pm = c.pb("max_in_rows", st, 1024)
        po = c.pb("o_sums", st, 1024)
        s_st, s_sf, s_s, s_m, s_r, s_q = (c.sem(n) for n in ("staged", "staging_free", "scores_q", "max_taken",
                                                             "max_turned", "q_ready"))
        s_t, s_e, s_pf, s_o, s_oc, s_d, s_dr = (c.sem(n) for n in ("scores_k", "exp_made", "probs_free", "o_summed",
                                                                   "o_copied", "den_spread", "den_recip"))
        s_dd = c.sem("o_scaled")
        kt = [(i, max(i * 128, lo), lo + 512) for i in range(QT) for lo in (0, 512) if lo + 512 > i * 128]
        NK = len(kt)
        with nc.Block() as block:
            @block.vector
            def _(v):
                v.tensor_copy(c.scratch[:, 0:2], c.ones[:, 0:2]).then_inc(s_m, 2)
                with v.Fori(0, B) as b:
                    with v.Fori(0, 4) as g:
                        u = b * 4 + g
                        qv = c.qT[:, bass.ds(g, 1), :].rearrange("p o (t b) -> p b (o t)", b=B)[:, bass.ds(b, 1), :]
                        kv = c.kT[:, bass.ds(g, 1), :].rearrange("p o (t b) -> p b (o t)", b=B)[:, bass.ds(b, 1), :]
                        v.tensor_copy(qs[:].rearrange("p (o t) -> p o t", o=1), qv).then_inc(s_st, 1)
                        v.tensor_scalar(ks[:].rearrange("p (o t) -> p o t", o=1), kv, c.diag[:, AD:AD + 1], None,
                                        ALU.add).then_inc(s_st, 1)
                        v.tensor_copy(vs[:], c.vt[:, bass.ds(b * QT, QT), bass.ds(g * 4, 4), :]).then_inc(s_st, 1)
                        for h in range(4):
                            for i in range(QT):
                                n = h * QT + i
                                v.wait_ge(s_s, u * (4 * QT) + (n + 1))
                                v.tensor_reduce(c.rowmax[:, i, h, AD:AD + 1], big[n % 2][:, 0:(i + 1) * 128], AX.X,
                                                ALU.max).then_inc(s_m, 1)
                        for half in range(2):
                            v.wait_ge(s_r, u * 2 + (half + 1))
                            v.tensor_tensor(blk(qa, half), blk(qs, half), blk(pm, half), ALU.subtract).then_inc(s_q, 1)
                        for half in range(2):
                            v.wait_ge(s_d, u * 2 + (half + 1))
                            v.reciprocal(blk(rc, half), blk(pm, half)).then_inc(s_dr, 1)
                        v.wait_ge(s_dr, u * 2 + 2)
                        dst = c.oT[:, bass.ds(g, 1), :].rearrange("p o (t b) -> p b (o t)", b=B)[:, bass.ds(b, 1), :]
                        v.tensor_tensor(dst, ob[:].rearrange("p (o t) -> p o t", o=1),
                                        rc[:].rearrange("p (o t) -> p o t", o=1), ALU.mult).then_inc(s_dd, 1)

            @block.tensor
            def _(pe):
                with pe.Fori(0, B) as b:
                    with pe.Fori(0, 4) as g:
                        u = b * 4 + g
                        pe.wait_ge(s_st, u * 3 + 3)
                        for h in range(4):
                            r = slice(32 * h, 32 * h + 32)
                            for i in range(QT):
                                n = h * QT + i
                                pe.wait_ge(s_m, u * (4 * QT) + (n + 1))
                                s = big[n % 2]
                                d = i * 128
                                for lo in range(0, d + 128, 512):
                                    hi = min(lo + 512, d + 128)
                                    here = hi == d + 128
                                    if here:
                                        pe.matmul(s[:, d:d + 128], c.ident16[:], c.mask_q[:], start=True, stop=True,
                                                  skip_group_check=True)
                                    mm = pe.matmul(s[:, lo:hi], qs[r, d:d + 128], ks[r, lo:hi], start=not here, stop=True,
                                                   skip_group_check=True)
                                mm.then_inc(s_s, 1)
                        pe.wait_ge(s_m, (u + 1) * (4 * QT) + 2)
                        for half in range(2):
                            for i in range(4 * half, 4 * half + 4):
                                mm = pe.matmul(pm[:, i * 128:(i + 1) * 128],
                                               c.rowmax[:, i].rearrange("p h r -> p (h r)"), c.ident[:],
                                               start=True, stop=True)
                            mm.then_inc(s_r, 1)
                        pe.wait_ge(s_q, u * 2 + 2)

                        def scores(m):
                            h, (i, lo, hi) = m // NK, kt[m % NK]
                            r = slice(32 * h, 32 * h + 32)
                            s = big[m % 4 // 2][:, m % 2 * 512:m % 2 * 512 + hi - lo]
                            if m >= 4:
                                pe.wait_ge(s_e, u * (4 * NK) + (m - 3))
                            diag = lo == i * 128
                            if diag:
                                pe.matmul(s[:, 0:128], c.ident16[:], c.mask_k[:], start=True, stop=True,
                                          skip_group_check=True)
                            pe.matmul(s, ks[r, i * 128:(i + 1) * 128], qa[r, lo:hi], start=not diag, stop=True,
                                      skip_group_check=True).then_inc(s_t, 1)

                        def sums(m):
                            h, (i, lo, hi) = m // NK, kt[m % NK]
                            pe.wait_ge(s_e, u * (4 * NK) + (m + 1))
                            last = (i == 3 and hi == 512) or i == 7
                            pe.matmul(po[32 * h:32 * h + 32, lo:hi], vs[:, i, h, :], pr[m % 4][:, 0:hi - lo],
                                      start=(i == 0), stop=last).then_inc(s_o, 1)

                        for m in range(4 * NK):
                            scores(m)
                            if m >= 2:
                                sums(m - 2)
                        sums(4 * NK - 2)
                        sums(4 * NK - 1)
                        for half in range(2):
                            pe.wait_ge(s_oc, u * 2 + (half + 1))
                            pe.matmul(blk(pm, half), c.dsel[:], blk(ob, half), start=True, stop=True).then_inc(s_d, 1)
                        pe.wait_ge(s_dr, u * 2 + 2)

            @block.scalar
            def _(act):
                with act.Fori(0, B) as b:
                    with act.Fori(0, 4) as g:
                        u = b * 4 + g
                        for m in range(4 * NK):
                            i, lo, hi = kt[m % NK]
                            act.wait_ge(s_t, u * (4 * NK) + (m + 1))
                            if m >= 4:
                                act.wait_ge(s_o, u * (4 * NK) + (m - 3))
                            act.activation(pr[m % 4][:, 0:hi - lo], big[m % 4 // 2][:, m % 2 * 512:m % 2 * 512 + hi - lo],
                                           ACT.Exp, scale=float(AD) ** -0.5).then_inc(s_e, 1)
                        act.wait_ge(s_o, (u + 1) * (4 * NK))
                        for half in range(2):
                            act.activation(blk(ob, half), blk(po, half), ACT.Copy).then_inc(s_oc, 1)


def phase_attn_out(c):
    nc, a = c.nc, c.a
    st = ExitStack()
    with st:
        wo = c.sb("w_o_padded", [128, 4, D], f32, st)
        px = [c.pb(f"attn_out_psum{i}", st) for i in range(2)]
        s_0, s_w, s_p, s_e = c.sem("w_o_zeroed"), c.sem("w_o_loaded"), c.sem("attn_out_made"), c.sem("attn_out_added")
        with nc.Block() as block:
            @block.gpsimd
            def _(pool):
                pool.memset(wo[:], 0.0).then_inc(s_0, 1)

            @block.sync
            def _(sp):
                sp.wait_ge(s_0, 1)
                for h in range(4):
                    sp.dma_start(wo[32 * h:32 * h + AD], a["L0_ffn_w_o"].rearrange("(g h d) n -> h d g n", h=4, d=AD)[h])\
                      .then_inc(s_w, 16)

            @block.tensor
            def _(pe):
                pe.wait_ge(s_w, 64)
                for n in range(NB):
                    for m in range(KT):
                        if n:
                            pe.wait_ge(s_e, (n - 1) * KT + m + 1)
                        for g in range(4):
                            mm = pe.matmul(px[m][:], wo[:, g, m * 128:(m + 1) * 128], blk(c.oT[:, g], n),
                                           start=(g == 0), stop=(g == 3))
                        mm.then_inc(s_p, 1)

            @block.vector
            def _(v):
                for n in range(NB):
                    for m in range(KT):
                        v.wait_ge(s_p, n * KT + m + 1)
                        x = blk(c.hT[:, m], n)
                        v.tensor_tensor(x, px[m][:], x, ALU.add).then_inc(s_e, 1)


def phase_layernorm(c, tag, other, out, gain, shift, residual):
    nc, a = c.nc, c.a
    st = ExitStack()
    with st:
        gb = c.sb(tag + "_gain_shift", [128, 2, KT], f32, st)
        mean_of = c.sb(tag + "_one_over_d", [128, 128], f32, st)
        r = c.sb(tag + "_sum", [128, KT, 512], f32, st)
        sq = c.sb(tag + "_squares", [128, KT, 512], f32, st)
        rt = c.sb(tag + "_root", [128, 512], f32, st)
        pm, pv = c.pb(tag + "_mean", st), c.pb(tag + "_var", st)
        s_w, s_k, s_r, s_m, s_c, s_v, s_e, s_rt, s_n = (c.sem(f"{tag}_{n}") for n in (
            "weights", "const", "summed", "mean_made", "squared", "var_made", "recip", "root_made", "normed"))
        with nc.Block() as block:
            @block.sync
            def _(sp):
                with nc.allow_non_contiguous_dma("small vectors"):
                    sp.dma_start(gb[:, 0], col(a[gain])).then_inc(s_w, 16)
                    sp.dma_start(gb[:, 1], col(a[shift])).then_inc(s_w, 16)

            @block.gpsimd
            def _(pool):
                pool.memset(mean_of[:], 1.0 / D).then_inc(s_k, 1)

            @block.tensor
            def _(pe):
                pe.wait_ge(s_k, 1)
                with pe.Fori(0, NB) as n:
                    for bank, src, ready, done in ((pm, r, s_r, s_m), (pv, sq, s_c, s_v)):
                        pe.wait_ge(ready, n + 1)
                        for k in range(KT):
                            mm = pe.matmul(bank[:], mean_of[:], src[:, k], start=(k == 0), stop=(k == KT - 1))
                        mm.then_inc(done, 1)

            @block.vector
            def _(v):
                v.wait_ge(s_w, 32)
                with v.Fori(0, NB) as n:
                    x = c.hT[:, :, bass.ds(n * 512, 512)]
                    if other is None:
                        v.tensor_copy(r[:], x).then_inc(s_r, 1)
                    else:
                        v.tensor_tensor(r[:], x, other[:, :, bass.ds(n * 512, 512)], ALU.add).then_inc(s_r, 1)
                    v.wait_ge(s_m, n + 1)
                    v.wait_ge(s_r, n + 1)
                    for k in range(KT):
                        v.tensor_tensor(r[:, k], r[:, k], pm[:], ALU.subtract).then_inc(s_n, 1)
                    v.wait_ge(s_n, n * 8 + 2)
                    v.tensor_tensor(sq[:], r[:], r[:], ALU.mult).then_inc(s_c, 1)
                    v.wait_ge(s_v, n + 1)
                    v.tensor_scalar(rt[:], pv[:], 1e-5, None, ALU.add).then_inc(s_n, 1)
                    v.wait_ge(s_n, n * 8 + 3)
                    v.reciprocal(rt[:], rt[:]).then_inc(s_e, 1)
                    v.wait_ge(s_rt, n + 1)
                    for k in range(KT):
                        v.scalar_tensor_tensor(sq[:, k], r[:, k], gb[:, 0, k:k + 1], rt[:], ALU.mult, ALU.mult)\
                         .then_inc(s_n, 1)
                    v.wait_ge(s_n, n * 8 + 5)
                    for k in range(KT):
                        dst = out[:, k, bass.ds(n * 512, 512)]
                        if residual:
                            v.scalar_tensor_tensor(dst, sq[:, k], gb[:, 1, k:k + 1], dst, ALU.add, ALU.add)\
                             .then_inc(s_n, 1)
                        else:
                            v.tensor_scalar(dst, sq[:, k], gb[:, 1, k:k + 1], None, ALU.add).then_inc(s_n, 1)
                    v.tensor_copy(c.scratch[:, 0:2], c.ones[:, 0:2]).then_inc(s_n, 1)
                    v.wait_ge(s_n, n * 8 + 8)

            @block.scalar
            def _(act):
                with act.Fori(0, NB) as n:
                    act.wait_ge(s_e, n + 1)
                    act.activation(rt[:], rt[:], ACT.Sqrt).then_inc(s_rt, 1)


def phase_router(c):
    nc, a = c.nc, c.a
    NT = TOK // 128
    st = ExitStack()
    with st:
        wg = c.sb("w_router", [128, KT, EX], f32, st)
        before = c.sb("expert_before", [128, EX, EX], f32, st)
        p = c.sb("expert_probs", [128, NT, EX], f32, st)
        mx = c.sb("expert_max", [128, NT], f32, st)
        sm = c.sb("expert_sum", [128, NT], f32, st)
        gt = c.sb("expert_greater", [128, NT, EX, EX], f32, st)
        eq = c.sb("expert_equal", [128, NT, EX, EX], f32, st)
        rank = c.sb("expert_rank", [128, NT, EX], f32, st)
        pl = c.pb("logits", st)
        pt = c.pb("weights_turned", st, 2048)
        s_w, s_b, s_l, s_d, s_x, s_t = (c.sem(n) for n in ("router_w", "router_const", "logits_made", "router_dve",
                                                           "router_exp", "weights_turned_s"))
        s_te = c.sem("weights_evacuated")
        with nc.Block() as block:
            @block.sync
            def _(sp):
                with nc.allow_non_contiguous_dma("narrow rows"):
                    sp.dma_start(wg[:], a["L0_ffn_wg"].rearrange("(k p) n -> p k n", p=128)).then_inc(s_w, 16)

            @block.gpsimd
            def _(pool):
                pool.memset(before[:], 1.0).then_inc(s_b, 1)
                pool.wait_ge(s_b, 1)
                pool.affine_select(out=before[:], in_=before[:], compare_op=ALU.is_ge, fill=0.0, base=-1,
                                   pattern=[[1, EX], [-1, EX]], channel_multiplier=0).then_inc(s_b, 1)

            @block.tensor
            def _(pe):
                pe.wait_ge(s_w, 16)
                for i in range(NT):
                    for k in range(KT):
                        mm = pe.matmul(pl[:, i * EX:(i + 1) * EX], c.hT[:, k, i * 128:(i + 1) * 128], wg[:, k, :],
                                       start=(k == 0), stop=(k == KT - 1))
                mm.then_inc(s_l, 1)
                pe.wait_ge(s_d, 13)
                for i in range(NT):
                    mm = pe.matmul(pt[0:EX, i * 128:(i + 1) * 128], p[:, i, :], c.ident[:], start=True, stop=True)
                mm.then_inc(s_t, 1)

            @block.scalar
            def _(act):
                act.wait_ge(s_d, 2)
                act.activation(p[:], p[:], ACT.Exp).then_inc(s_x, 1)
                act.wait_ge(s_t, 1)
                for n in range(NB):
                    act.activation(blk(c.wT, n), pt[0:EX, n * 512:(n + 1) * 512], ACT.Copy).then_inc(s_te, 1)

            @block.vector
            def _(v):
                steps = [0]

                def then(ins):
                    ins.then_inc(s_d, 1)
                    steps[0] += 1
                    v.wait_ge(s_d, steps[0])

                def over(t):
                    return t[:].rearrange("p (n o) -> p n o", o=1).to_broadcast([128, NT, EX])

                four = [128, NT, EX, EX]
                mine = p[:].rearrange("p n (e o) -> p n e o", o=1).to_broadcast(four)
                other = p[:].rearrange("p n (o e) -> p n o e", o=1).to_broadcast(four)
                logits = pl[:, 0:NT * EX].rearrange("p (n e) -> p n e", e=EX)
                v.wait_ge(s_l, 1)
                then(v.tensor_reduce(mx[:], logits, AX.X, ALU.max))
                then(v.tensor_tensor(p[:], logits, over(mx), ALU.subtract))
                v.wait_ge(s_x, 1)
                then(v.tensor_reduce(sm[:], p[:], AX.X, ALU.add))
                then(v.reciprocal(mx[:], sm[:]))
                then(v.tensor_tensor(p[:], p[:], over(mx), ALU.mult))
                then(v.tensor_tensor(gt[:], other, mine, ALU.is_gt))
                then(v.tensor_tensor(eq[:], other, mine, ALU.is_equal))
                v.wait_ge(s_b, 2)
                then(v.tensor_tensor(eq[:], eq[:], before[:].rearrange("p (o e) j -> p o e j", o=1).to_broadcast(four),
                                     ALU.mult))
                then(v.tensor_tensor(gt[:], gt[:], eq[:], ALU.add))
                then(v.tensor_reduce(rank[:], gt[:], AX.X, ALU.add))
                then(v.scalar_tensor_tensor(p[:], rank[:], 1.5, p[:], ALU.is_lt, ALU.mult))
                then(v.tensor_reduce(sm[:], p[:], AX.X, ALU.add))
                v.reciprocal(mx[:], sm[:]).then_inc(s_te, 1)
                v.wait_ge(s_te, 1)
                then(v.tensor_tensor(p[:], p[:], over(mx), ALU.mult))


def phase_experts(c):
    nc, a = c.nc, c.a
    st = ExitStack()
    with st:
        w1 = [c.sb(f"expert_w1_{i}", [128, KT, FF], f32, st) for i in range(2)]
        w2 = [c.sb(f"expert_w2_{i}", [128, FT, D], f32, st) for i in range(2)]
        b1 = [c.sb(f"expert_b1_{i}", [128, FT], f32, st) for i in range(2)]
        pick = [c.sb(f"expert_pick{i}", [EX, 128], f32, st) for i in range(2)]
        picks = c.sb("expert_picks", [EX, EX, 128], f32, st)
        b2 = c.sb("expert_b2", [EX, D], f32, st)
        g = [c.sb(f"gelu{i}", [128, 512], f32, st) for i in range(3)]
        gw = [c.sb(f"gelu_weighted{i}", [128, 512], f32, st) for i in range(3)]
        pu = [c.pb(f"up_psum{i}", st) for i in range(3)]
        py = [c.pb(f"down_psum{i}", st) for i in range(4)]
        pw = c.pb("weight_psum", st)
        wrow = [c.sb(f"weight_in_rows{i}", [128, 512], f32, st) for i in range(2)]
        s_b2, s_pk, s_pick = c.sem("b2_loaded"), c.sem("picks_made"), c.sem("pick_staged")
        s_w = [c.sem(f"expert_loaded{i}") for i in range(2)]
        s_i, s_ie = c.sem("y_start_made"), c.sem("y_started")
        s_wr, s_wre, s_up, s_g, s_gw, s_dn, s_y = (c.sem(n) for n in (
            "weight_spread", "weight_copied", "up_made", "gelu_made", "gelu_weighted_s", "down_made", "y_added"))
        with nc.Block() as block:
            def units(eng, body):
                with eng.Fori(0, EX // 2) as ei:
                    for je in range(2):
                        with eng.Fori(0, NB // 2) as ni:
                            for jn in range(2):
                                body(ei * 2 + je, je, ni * 2 + jn, jn, ei * (2 * NB) + ni * 2 + (je * NB + jn))

            @block.sync
            def _(sp):
                sp.dma_start(b2[:], a["L0_ffn_bb2"]).then_inc(s_b2, 16)
                with nc.allow_non_contiguous_dma("a column of biases"):
                    def load(e, je):
                        sp.dma_start(w1[je][:], a["L0_ffn_w1"][e].rearrange("o (k p) f -> p (o k) f", p=128)).then_inc(s_w[je], 16)
                        sp.dma_start(w2[je][:], a["L0_ffn_w2"][e].rearrange("o (f p) d -> p (o f) d", p=128)).then_inc(s_w[je], 16)
                        sp.dma_start(b1[je][:], a["L0_ffn_bb1"][e].rearrange("o (f p) -> p (o f)", p=128)).then_inc(s_w[je], 16)

                    for je in range(2):
                        load(slice(je, je + 1), je)
                    with sp.Fori(1, EX // 2) as ei:
                        for je in range(2):
                            sp.wait_ge(s_y, ei * (2 * NB * KT) + ((je - 1) * NB * KT + 6))
                            load(bass.ds(ei * 2 + je, 1), je)

            @block.gpsimd
            def _(pool):
                pool.memset(picks[:], 0.0).then_inc(s_pk, 1)
                pool.wait_ge(s_pk, 1)
                pool.affine_select(out=picks[:], in_=picks[:], compare_op=ALU.not_equal, fill=1.0, base=0,
                                   pattern=[[-1, EX], [0, 128]], channel_multiplier=1).then_inc(s_pk, 1)
                pool.wait_ge(s_pk, 2)
                for je in range(2):
                    pool.tensor_copy(pick[je][:], picks[:, je]).then_inc(s_pick, 1)
                with pool.Fori(1, EX // 2) as ei:
                    for je in range(2):
                        pool.wait_ge(s_y, ei * (2 * NB * KT) + ((je - 1) * NB * KT + 6))
                        pool.tensor_copy(pick[je][:].rearrange("p (o n) -> p o n", o=1),
                                         picks[:, bass.ds(ei * 2 + je, 1), :]).then_inc(s_pick, 1)

            @block.tensor
            def _(pe):
                pe.wait_ge(s_b2, 16)
                for n in range(NB):
                    for m in range(KT):
                        i = n * KT + m
                        if i >= 4:
                            pe.wait_ge(s_ie, i - 3)
                        pe.matmul(py[i % 4][:], b2[:, m * 128:(m + 1) * 128], blk(c.wT, n), start=True, stop=True)\
                          .then_inc(s_i, 1)
                pe.wait_ge(s_ie, NB * KT)

                def body(e, je, n, jn, u):
                    q = u * FT
                    h = [c.hT[:, k, bass.ds(n * 512, 512)] for k in range(KT)]
                    pe.wait_ge(s_pick, e + 1)
                    pe.wait_ge(s_wre, u + 1)
                    pe.matmul(pw[:], pick[je][:], c.wT[:, bass.ds(n * 512, 512)], start=True, stop=True).then_inc(s_wr, 1)
                    pe.wait_ge(s_w[je], (e - je) * 24 + 48)

                    def up(f):
                        if f >= 3:
                            pe.wait_ge(s_g, q + (f - 2))
                        for k in range(KT):
                            mm = pe.matmul(pu[f % 3][:], w1[je][:, k, f * 128:(f + 1) * 128], h[k],
                                           start=(k == 0), stop=(k == KT - 1))
                        mm.then_inc(s_up, 1)

                    def down(f):
                        pe.wait_ge(s_gw, q + (f + 1))
                        for m in range(KT):
                            mm = pe.matmul(py[jn * 2 + m][:], w2[je][:, f, m * 128:(m + 1) * 128], gw[f % 3][:],
                                           start=(f == 0), stop=(f == FT - 1))
                        mm.then_inc(s_dn, 1)
                        return mm

                    up(0)
                    up(1)
                    pe.wait_ge(s_y, u * KT + (KT + 2))
                    for f in range(FT):
                        if f + 2 < FT:
                            up(f + 2)
                        down(f)
                units(pe, body)

            @block.scalar
            def _(act):
                def body(e, je, n, jn, u):
                    q = u * FT
                    for f in range(FT):
                        act.wait_ge(s_up, q + (f + 1))
                        if f == 0:
                            act.wait_ge(s_w[je], (e - je) * 24 + 48)
                        if f >= 3:
                            act.wait_ge(s_gw, q + (f - 2))
                        act.activation(g[f % 3][:], pu[f % 3][:], ACT.Gelu_apprx_tanh, bias=b1[je][:, f:f + 1])\
                            .then_inc(s_g, 1)
                units(act, body)

            @block.vector
            def _(v):
                for n in range(NB):
                    for m in range(KT):
                        i = n * KT + m
                        v.wait_ge(s_i, i + 1)
                        v.tensor_copy(blk(c.y[:, m], n), py[i % 4][:]).then_inc(s_ie, 1)
                v.tensor_copy(c.scratch[:, 0:2], c.ones[:, 0:2]).then_inc(s_wre, 1)
                v.tensor_copy(c.scratch[:, 2:4], c.ones[:, 0:2]).then_inc(s_y, 6)

                def body(e, je, n, jn, u):
                    q = u * FT
                    v.wait_ge(s_wr, u + 1)
                    v.tensor_copy(wrow[jn][:], pw[:]).then_inc(s_wre, 1)
                    v.wait_ge(s_wre, u + 2)
                    for f in range(FT):
                        v.wait_ge(s_g, q + (f + 1))
                        if f >= 3:
                            v.wait_ge(s_dn, q + (f - 2))
                        v.tensor_tensor(gw[f % 3][:], g[f % 3][:], wrow[jn][:], ALU.mult).then_inc(s_gw, 1)
                    v.wait_ge(s_dn, q + FT)
                    for m in range(KT):
                        y = c.y[:, m, bass.ds(n * 512, 512)]
                        v.tensor_tensor(y, py[jn * 2 + m][:], y, ALU.add).then_inc(s_y, 1)
                units(v, body)


def phase_store(c, src):
    nc = c.nc
    st = ExitStack()
    with st:
        rows = c.sb("out_rows", [128, 2, T // 128, D], f32, st)
        pt = [c.pb(f"rows_turned{i}", st) for i in range(2)]
        s_t, s_e, s_out = c.sem("rows_turned_s"), c.sem("rows_evacuated"), c.sem("rows_stored")
        with nc.Block() as block:
            @block.tensor
            def _(pe):
                n = 0
                for b in range(B):
                    for i in range(T // 128):
                        if n >= 2:
                            pe.wait_ge(s_e, n - 1)
                        for k in range(KT):
                            s = src[:, k, :].rearrange("p (t b) -> p b t", b=B)[:, b, i * 128:(i + 1) * 128]
                            mm = pe.transpose(pt[n % 2][:, k * 128:(k + 1) * 128], s, c.ident[:])
                        mm.then_inc(s_t, 1)
                        n += 1

            @block.vector
            def _(v):
                for n in range(B * T // 128):
                    v.wait_ge(s_t, n + 1)
                    v.tensor_copy(rows[:, n // (T // 128), n % (T // 128)], pt[n % 2][:, 0:D]).then_inc(s_e, 1)

            @block.sync
            def _(sp):
                for b in range(B):
                    sp.wait_ge(s_e, (b + 1) * (T // 128))
                    sp.dma_start(c.a["out"][b].rearrange("(i p) c -> p i c", p=128), rows[:, b]).then_inc(s_out, 16)
                sp.wait_ge(s_out, 16 * B)


def program(nc, args):
    stack = ExitStack()
    with stack:
        c = Core(nc, args, stack)
        c.ident = c.sb("identity", [128, 128])
        c.headones = c.sb("ones_within_head", [128, 128])
        c.ones = c.sb("ones", [128, 128])
        c.unscale = c.sb("unscale", [128, 2])
        c.scratch = c.sb("scratch", [128, 8])
        c.diag = c.sb("diagonal", [128, RD])
        c.h0 = c.sb("h0", [128, KT, B])
        c.wh2 = c.sb("rnn_Wh", [128, KT, D])
        c.wa2 = c.sb("rnn_Wh_high", [128, KT, D], f16)
        c.wb2 = c.sb("rnn_Wh_low", [128, KT, D], f16)
        c.xT = c.sb("xT", [128, KT, TOK])
        c.rT = c.sb("rT", [128, KT, TOK])
        c.r0 = c.sb("r0_products", [128, KT, B])
        s1 = ExitStack()
        with s1:
            c.wh = c.sb("lstm_Wh", [128, KT, G4], f32, s1)
            c.wa = c.sb("lstm_Wh_high", [128, KT, G4], f16, s1)
            c.wb = c.sb("lstm_Wh_low", [128, KT, G4], f16, s1)
            c.xz = c.sb("lstm_xz", [128, T, G4 // 128, B], f32, s1)
            c.hT = c.sb("hT", [128, KT, TOK], f32, s1)
            phase_load(c)
            phases_recurrent(c)
        c.hT = c.rT
        s5 = ExitStack()
        with s5:
            c.qT, c.kT, c.oT = (c.sb(n, [128, 4, TOK], f32, s5) for n in ("q_heads", "k_heads", "o_heads"))
            c.vt = c.sb("v_rows", [128, B * T // 128, AH, 32], f32, s5)
            c.rowmax = c.sb("score_max", [128, T // 128, 4, 32], f32, s5)
            c.mask_q, c.mask_k, c.ident16 = (c.sb(n, [128, 128], bf16, s5) for n in ("mask_q", "mask_k", "identity_bf16"))
            c.dsel = c.sb("sum_row_of_head", [128, 128], f32, s5)
            phase_heads(c)
            phase_attend(c)
            phase_attn_out(c)
        phase_layernorm(c, "norm1", None, c.hT, "L0_ffn_g1", "L0_ffn_b1", False)
        s6 = ExitStack()
        with s6:
            c.wT = c.sb("expert_weights", [EX, TOK], f32, s6)
            c.y = c.sb("expert_sum_y", [128, KT, TOK], f32, s6)
            phase_router(c)
            phase_experts(c)
            phase_layernorm(c, "norm2", c.y, c.xT, "L0_ffn_g2", "L0_ffn_b2", True)
        phase_store(c, c.xT)


_INS = ['x', 'cond_1024', 'L0_cond_Wx', 'L0_cond_Wh', 'L0_cond_b', 'L0_attn_Wq', 'L0_attn_Wk', 'L0_attn_Wv',
        'L0_attn_Wf1', 'L0_attn_Wf2', 'L0_attn_Wbeta', 'L0_attn_Wog1', 'L0_attn_Wog2', 'L0_attn_norm_w', 'L0_attn_Wo',
        'L0_cond2_Wx', 'L0_cond2_Wh', 'L0_cond2_b', 'L0_ffn_w_qkv', 'L0_ffn_w_o', 'L0_ffn_g1', 'L0_ffn_b1',
        'L0_ffn_wg', 'L0_ffn_w1', 'L0_ffn_bb1', 'L0_ffn_w2', 'L0_ffn_bb2', 'L0_ffn_g2', 'L0_ffn_b2']


def kernel(**inputs):
    import numpy as _np
    import concourse.bacc as _bacc
    from concourse import mybir as _mybir
    from concourse.bass_utils import run_bass_kernel_spmd as _run

    nc = _bacc.Bacc("TRN2", target_bir_lowering=False, num_devices=1)
    arrays, args = {}, {}
    for name in _INS:
        x = _np.ascontiguousarray(inputs[name])
        arrays[f"in_{name}_dram"] = x
        args[name] = nc.dram_tensor(f"in_{name}_dram", x.shape, _mybir.dt.from_np(x.dtype), kind="ExternalInput").ap()
    args["out"] = nc.dram_tensor("out_0_dram", (B, T, D), _mybir.dt.float32, kind="ExternalOutput").ap()
    program(nc, args)
    r = _run(nc, [arrays], core_ids=[0])
    return r.results[0]["out_0_dram"]
```

```python
import concourse.bass as bass
from concourse import mybir
from contextlib import ExitStack

f32 = mybir.dt.float32
f16 = mybir.dt.float16
bf16 = mybir.dt.bfloat16
i32 = mybir.dt.int32
ALU = mybir.AluOpType
ACT = mybir.ActivationFunctionType
AX = mybir.AxisListType

B, T, D = 2, 1024, 256
TOK = B * T
KT = D // 128
G4 = 4 * D
NB = TOK // 512
RH, RD = 8, 32
AH, AD = 16, 16
EX, FF = 8, 1024
FT = FF // 128
HS = 1024.0


class Core:

    def __init__(self, nc, args, stack):
        self.nc = nc
        self.a = args
        self.stack = stack

    def sb(self, name, shape, dt=f32, stack=None):
        return (stack or self.stack).enter_context(self.nc.sbuf_tensor(name, shape, dt))

    def pb(self, name, stack, n=512, dt=f32):
        return stack.enter_context(self.nc.psum_tensor(name, [128, n], dt))

    def sem(self, name):
        return self.stack.enter_context(self.nc.semaphore(name))


def col(v):
    return v.rearrange("(k p) -> p k", p=128)


def blk(t, n, size=512):
    return t[:, n * size:(n + 1) * size]


def blk3(t, n, size=512):
    return t[:, :, n * size:(n + 1) * size]


def phase_load(c):
    nc, a = c.nc, c.a
    st = ExitStack()
    with st:
        xin = c.sb("x_rows", [128, 2, T // 128, D], f32, st)
        wx = c.sb("lstm_Wx", [128, KT, G4], f32, st)
        wsc = c.sb("lstm_Wh_scaled", [128, KT, G4], f32, st)
        wbig = c.sb("wh_absmax", [128, 2], f32, st)
        wrow = c.sb("wh_absmax_row", [1, 2, 128], f32, st)
        wmax = c.sb("wh_scale_row", [1, 4], f32, st)
        scl = c.sb("wh_scale", [128, 2], f32, st)
        wr2 = c.sb("rnn_Wh_scaled", [128, KT, D], f32, st)
        bias = c.sb("lstm_b", [128, G4 // 128], f32, st)
        pt = [c.pb(f"x_turned{i}", st) for i in range(2)]
        pz = [c.pb(f"xz_psum{i}", st) for i in range(2)]
        pm = c.pb("absmax_turned", st)
        ps = c.pb("scale_spread", st)
        s_x, s_w, s_b = c.sem("x_loaded"), c.sem("weights_loaded"), c.sem("bias_loaded")
        s_c, s_t, s_e = c.sem("constants_made"), c.sem("x_turned"), c.sem("x_evacuated")
        s_m, s_mt, s_md = c.sem("absmax_made"), c.sem("absmax_turned_s"), c.sem("scale_row_made")
        s_sp, s_sd, s_z, s_ze = c.sem("scale_spread_s"), c.sem("split_step"), c.sem("xz_made"), c.sem("xz_evacuated")
        s_g = c.sem("pool_step")
        s_h0 = c.sem("h0_products")
        xz = c.xz
        with nc.Block() as block:
            @block.sync
            def _(sp):
                for b in range(B):
                    sp.dma_start(xin[:, b], a["x"][b].rearrange("(i p) c -> p i c", p=128)).then_inc(s_x, 16)
                sp.dma_start(wx[:], a["L0_cond_Wx"].rearrange("(k p) n -> p k n", p=128)).then_inc(s_w, 16)
                sp.dma_start(c.wh[:], a["L0_cond_Wh"].rearrange("(k p) n -> p k n", p=128)).then_inc(s_w, 16)
                sp.dma_start(c.wh2[:], a["L0_cond2_Wh"].rearrange("(k p) n -> p k n", p=128)).then_inc(s_w, 16)
                with nc.allow_non_contiguous_dma("small vectors"):
                    sp.dma_start(bias[:], col(a["L0_cond_b"])).then_inc(s_b, 16)
                    for k in range(KT):
                        sp.dma_start(c.h0[:, k, :], a["cond_1024"][:, k * 128:(k + 1) * 128].rearrange("b p -> p b"))\
                          .then_inc(s_b, 16)

            @block.gpsimd
            def _(pool):
                pool.memset(c.ident[:], 0.0).then_inc(s_g, 1)
                pool.memset(c.headones[:], 1.0).then_inc(s_g, 1)
                pool.memset(c.ones[:], 1.0).then_inc(s_c, 1)
                pool.wait_ge(s_g, 2)
                pool.affine_select(out=c.ident[:], in_=c.ident[:], compare_op=ALU.not_equal, fill=1.0, base=0,
                                   pattern=[[-1, 128]], channel_multiplier=1).then_inc(s_c, 1)
                hv = c.headones[:].rearrange("p (h q) -> p h q", q=32)
                pool.affine_select(out=hv, in_=hv, compare_op=ALU.is_ge, fill=0.0, base=0,
                                   pattern=[[-32, 4], [0, 32]], channel_multiplier=1).then_inc(s_g, 1)
                pool.wait_ge(s_g, 3)
                pool.affine_select(out=hv, in_=hv, compare_op=ALU.is_ge, fill=0.0, base=31,
                                   pattern=[[32, 4], [0, 32]], channel_multiplier=-1).then_inc(s_c, 1)

            @block.tensor
            def _(pe):
                pe.wait_ge(s_c, 3)
                pe.wait_ge(s_x, 16 * B)
                n = 0
                for b in range(B):
                    for k in range(KT):
                        for half in range(2):
                            if n >= 2:
                                pe.wait_ge(s_e, n - 1)
                            for j in range(4):
                                mm = pe.transpose(pt[n % 2][:, j * 128:(j + 1) * 128],
                                                  xin[:, b, half * 4 + j, k * 128:(k + 1) * 128], c.ident[:])
                            mm.then_inc(s_t, 1)
                            n += 1
                pe.wait_ge(s_m, 2)
                for w in range(2):
                    mm = pe.transpose(pm[0:1, w * 128:(w + 1) * 128], wbig[:, w:w + 1], c.ident[:])
                mm.then_inc(s_mt, 1)
                pe.wait_ge(s_md, 5)
                pe.matmul(ps[:, 0:4], c.ones[0:1, :], wmax[0:1, :], start=True, stop=True).then_inc(s_sp, 1)
                pe.wait_ge(s_w, 48)
                pe.wait_ge(s_e, 8)
                for q in range(G4 // 128):
                    for n in range(NB):
                        u = q * NB + n
                        if u >= 2:
                            pe.wait_ge(s_ze, u - 1)
                        for k in range(KT):
                            mm = pe.matmul(pz[u % 2][:], wx[:, k, q * 128:(q + 1) * 128], blk(c.xT[:, k], n),
                                           start=(k == 0), stop=(k == KT - 1))
                        mm.then_inc(s_z, 1)
                pe.wait_ge(s_b, 48)
                pe.wait_ge(s_sd, 1)
                pe.wait_ge(s_sd, 2)
                for q in range(G4 // 128):
                    place = (q + 2) % 8
                    for k in range(KT):
                        pe.matmul(ps[:, 2 * place:2 * place + 2], c.wh[:, k, q * 128:(q + 1) * 128], c.h0[:, k, :],
                                  start=(k == 0), stop=(k == KT - 1))
                for m in range(KT):
                    for k in range(KT):
                        mm = pe.matmul(ps[:, 16 + 2 * m:18 + 2 * m], c.wh2[:, k, m * 128:(m + 1) * 128], c.h0[:, k, :],
                                       start=(k == 0), stop=(k == KT - 1))
                mm.then_inc(s_h0, 1)

            @block.vector
            def _(v):
                n = 0
                for b in range(B):
                    for k in range(KT):
                        for half in range(2):
                            v.wait_ge(s_t, n + 1)
                            dst = c.xT[:, k, :].rearrange("p (t b) -> p b t", b=B)[:, b, half * 512:(half + 1) * 512]
                            v.tensor_copy(dst, pt[n % 2][:]).then_inc(s_e, 1)
                            n += 1
                v.wait_ge(s_w, 48)
                for w, t in enumerate((c.wh, c.wh2)):
                    v.tensor_reduce(wbig[:, w:w + 1], t[:], AX.XY, ALU.max, apply_absolute_value=True).then_inc(s_m, 1)
                v.wait_ge(s_mt, 1)
                v.tensor_copy(wrow[0:1].rearrange("p a b -> p (a b)"), pm[0:1, 0:256]).then_inc(s_md, 1)
                v.wait_ge(s_md, 1)
                v.tensor_reduce(wmax[0:1, 0:2], wrow[0:1], AX.X, ALU.max).then_inc(s_md, 1)
                v.wait_ge(s_md, 2)
                v.tensor_scalar(wmax[0:1, 2:4], wmax[0:1, 0:2], 1e-30, None, ALU.max).then_inc(s_md, 1)
                v.wait_ge(s_md, 3)
                v.tensor_scalar(wmax[0:1, 0:2].bitcast(i32), wmax[0:1, 2:4].bitcast(i32), 0x7F800000, None,
                                ALU.bitwise_and).then_inc(s_md, 1)
                v.wait_ge(s_md, 4)
                v.reciprocal(wmax[0:1, 2:4], wmax[0:1, 0:2]).then_inc(s_md, 1)
                v.wait_ge(s_sp, 1)
                v.tensor_scalar(scl[:], ps[:, 2:4], 2.0 ** 14, None, ALU.mult).then_inc(s_sd, 1)
                v.tensor_scalar(c.unscale[:], ps[:, 0:2], 2.0 ** -14 / HS, None, ALU.mult).then_inc(s_sd, 1)
                v.wait_ge(s_sd, 2)
                for w, (src, big, wa, wb) in enumerate(((c.wh, wsc, c.wa, c.wb), (c.wh2, wr2, c.wa2, c.wb2))):
                    v.tensor_scalar(big[:], src[:], scl[:, w:w + 1], None, ALU.mult).then_inc(s_sd, 1)
                    v.wait_ge(s_sd, 3 + 3 * w)
                    v.tensor_copy(wa[:], big[:]).then_inc(s_sd, 1)
                    v.wait_ge(s_sd, 4 + 3 * w)
                    v.tensor_tensor(wb[:], big[:], wa[:], ALU.subtract).then_inc(s_sd, 1)
                v.wait_ge(s_h0, 1)
                v.wait_ge(s_ze, NB * G4 // 128)
                first = xz[:, 0].rearrange("p m b -> p (m b)")
                v.tensor_tensor(first, ps[:, 0:16], first, ALU.add)
                v.tensor_copy(c.r0[:].rearrange("p m b -> p (m b)"), ps[:, 16:20])

            @block.scalar
            def _(act):
                act.wait_ge(s_b, 48)
                order = {3: 0, 0: 1, 1: 2, 2: 3}
                for q in range(G4 // 128):
                    for n in range(NB):
                        u = q * NB + n
                        act.wait_ge(s_z, u + 1)
                        m = order[q // 2] * 2 + q % 2
                        dst = xz[:, n * 256:(n + 1) * 256, m, :]
                        act.activation(dst, pz[u % 2][:].rearrange("p (t b) -> p t b", b=B), ACT.Identity,
                                       bias=bias[:, q:q + 1]).then_inc(s_ze, 1)


UNROLL = 8
CH = 64
CT = CH * B
CW = KT * CT
NC = T // CH


def phase_start(c):
    with c.nc.Block() as block:
        @block.vector
        def _(v):
            v.memset(c.hab[:, :, 0], 0.0).then_inc(c.s_ha, 1)
            v.memset(c.hab[:, :, 1], 0.0).then_inc(c.s_hb, 1)
            v.memset(c.rab[:, :, 0], 0.0).then_inc(c.s_ra, 2 * CH + 1)
            v.memset(c.rh[:], 0.0)
            v.memset(c.S[0][:], 0.0).then_inc(c.s_S, CH)
            v.memset(c.cell[:], 0.0)
            credits = [(c.s_prod, CH - 1), (c.s_py, CH - 1), (c.s_vd, CH - 1),
                       (c.s_u, CH), (c.s_ds, CH), (c.s_q, CH), (c.s_p2, CH), (c.s_s1, CH), (c.s_om, CH),
                       (c.s_oe, CH + 2),
                       (c.s_r, 2 * CH), (c.s_rzh, 2 * CH), (c.s_rz, 2 * CH), (c.s_rh, 2 * CH), (c.s_rb, 2 * CH)]
            for i, (sem, n) in enumerate(credits):
                v.memset(c.scratch[:, i:i + 1], 0.0).then_inc(sem, n)
            v.tensor_reduce(c.diag[:], c.ident[:].rearrange("p (h v) -> p v h", v=32), AX.X, ALU.add)


def recurrences(c, ci, lstm, delta, rnn):
    nc = c.nc
    xz = c.xz
    gates = [("g", 3), ("i", 0), ("f", 1), ("o", 2)]
    shape = [128, 4, RD]
    before = ci * CH

    def steps(body):
        def run(eng):
            with eng.Fori(0, CH // UNROLL - 1) as i:
                for j in range(UNROLL):
                    body(i * UNROLL + j, j % 2, False)
            for j in range(UNROLL):
                body(CH - UNROLL + j, j % 2, j == UNROLL - 1)
        return run

    def at(tt, n=1):
        return slice(tt, tt + n) if isinstance(tt, int) else bass.ds(tt, n)

    def of_step(row, t):
        return row[:, :, t * B:t * B + B] if isinstance(t, int) else row[:, :, bass.ds(t * B, B)]

    with nc.Block() as block:
        @block.tensor
        def _(pe):
            def products(bank, tiles, high, low, state, sem_high, sem_low, now, done):
                pe.wait_ge(sem_high, now)
                for n, at_w in enumerate(tiles):
                    for k in range(KT):
                        pe.matmul(bank[:, 4 * n:4 * n + B], low[:, k, at_w:at_w + 128], state[:, k, 0, :],
                                  start=(n == 0 and k == 0), stop=False, skip_group_check=True)
                pe.wait_ge(sem_low, now)
                for n, at_w in enumerate(tiles):
                    for k in range(KT):
                        mm = pe.matmul(bank[:, 4 * n:4 * n + 2 * B], high[:, k, at_w:at_w + 128],
                                       state[:, k].rearrange("p a b -> p (a b)"), start=False, stop=True,
                                       skip_group_check=True)
                mm.then_inc(done, 1)

            gif = [(2 * q + m) * 128 for _, q in gates[:3] for m in range(2)]
            o = [(2 * gates[3][1] + m) * 128 for m in range(2)]

            def project_state(now, j):
                pe.wait_ge(c.s_py, now)
                pe.matmul(c.p_u[j][:, 0:256], c.headones[:], c.prod[:].rearrange("p a g v -> p (a g v)"),
                          start=True, stop=True).then_inc(c.s_u, 1)

            def step(tt, j, last):
                now = before + tt + 1
                if lstm:
                    products(c.p_gif, gif, c.wa, c.wb, c.hab, c.s_ha, c.s_hb, now, c.s_gif)
                    products(c.p_o, o, c.wa, c.wb, c.hab, c.s_ha, c.s_hb, now, c.s_o)
                if rnn:
                    products(c.p_r, [m * 128 for m in range(KT)], c.wa2, c.wb2, c.rab, c.s_ra, c.s_rb, now, c.s_r)
                if delta:
                    pe.wait_ge(c.s_S, now)
                    pe.wait_ge(c.s_q, now)
                    pe.wait_ge(c.s_oe, now)
                    for g in range(4):
                        mm = pe.matmul(c.p_od[j][0:RD, g * 4:(g + 1) * 4], c.S[1 - j][:, g, :], c.qs[j][:, g, :],
                                       start=(g == 0), stop=(g == 3))
                    mm.then_inc(c.s_om, 1)
                    if not last:
                        project_state(now, 1 - j)

            if delta:
                project_state(before, 0)
            steps(step)(pe)

        @block.scalar
        def _(act):
            act.activation(c.scratch[:, 0:2], c.ones[:, 0:2], ACT.Sigmoid)

            def step(tt, j, last):
                now = before + tt + 1
                if lstm:
                    act.wait_ge(c.s_z, now)
                    act.activation(c.sif[:], c.z[:, 2:6].rearrange("p m b -> p (m b)"), ACT.Sigmoid).then_inc(c.s_if, 1)
                    act.activation(c.tg[:], c.z[:, 0:2].rearrange("p m b -> p (m b)"), ACT.Tanh).then_inc(c.s_g, 1)
                    act.wait_ge(c.s_zo, now)
                    act.activation(c.so[:], c.z[:, 6:8].rearrange("p m b -> p (m b)"), ACT.Sigmoid).then_inc(c.s_so, 1)
                    act.wait_ge(c.s_c, now)
                    act.activation(c.tc[:], c.cell[:], ACT.Tanh).then_inc(c.s_tc, 1)
                if rnn:
                    act.wait_ge(c.s_rz, now)
                    act.activation(c.rh[:], c.rz[:], ACT.Tanh).then_inc(c.s_rh, 1)
                    act.activation(of_step(c.rT, (ci - 2) * CH + tt), c.rz[:], ACT.Tanh)
                    act.wait_ge(c.s_rh, now)
                    act.activation(c.rab[:, :, 0], c.rh[:], ACT.Copy, scale=HS).then_inc(c.s_ra, 1)
                if delta:
                    act.wait_ge(c.s_om, now)
                    act.activation(c.o[:, at(tt), :], c.p_od[j][0:RD, 0:16].rearrange("p (o x) -> p o x", o=1), ACT.Copy)\
                        .then_inc(c.s_oe, 1)

            steps(step)(act)

        @block.vector
        def _(v):
            def multiply_state(now, j):
                v.wait_ge(c.s_S, now)
                v.wait_ge(c.s_vd, now)
                v.tensor_tensor(c.prod[:], c.S[j][:].rearrange("p (o g) v -> p o g v", o=1).to_broadcast([128, 2, 4, RD]),
                                c.row[j][:, 0:8].rearrange("p (a g o) -> p a g o", a=2, o=1)
                                .to_broadcast([128, 2, 4, RD]), ALU.mult).then_inc(c.s_prod, 1)

            def less_v(now, j):
                v.wait_ge(c.s_prod, now)
                v.tensor_tensor(c.prod[:, 1], c.prod[:, 1], c.vd[j][:], ALU.subtract).then_inc(c.s_py, 1)

            def first_part(lo, n, bank, w, add, mid):
                p = bank[:, 0:4 * n].rearrange("p (n a b) -> p n a b", a=2, b=B)
                v.scalar_tensor_tensor(c.zh[:, lo:lo + n], p[:, :, 0], c.unscale[:, w:w + 1], add, ALU.mult, ALU.add)\
                 .then_inc(mid, 1)

            def second_part(z, lo, n, bank, w, mid, done, now):
                p = bank[:, 0:4 * n].rearrange("p (n a b) -> p n a b", a=2, b=B)
                v.wait_ge(mid, now)
                v.scalar_tensor_tensor(z, p[:, :, 1], c.unscale[:, w:w + 1], c.zh[:, lo:lo + n], ALU.mult, ALU.add)\
                 .then_inc(done, 1)

            def step(tt, j, last):
                now = before + tt + 1
                if delta:
                    v.wait_ge(c.s_u, now)
                    v.tensor_tensor(c.p2[:].rearrange("p a g v -> p (a g) v"),
                                    c.p_u[j][:, 0:256].rearrange("p (g v) -> p g v", v=RD),
                                    c.row[j][:, 4:12].rearrange("p (g o) -> p g o", o=1).to_broadcast([128, 8, RD]),
                                    ALU.mult).then_inc(c.s_p2, 1)
                if rnn:
                    v.wait_ge(c.s_ra, now)
                    v.scalar_tensor_tensor(c.rab[:, :, 1], c.rh[:], HS, c.rab[:, :, 0], ALU.mult, ALU.subtract)\
                     .then_inc(c.s_rb, 1)
                if delta:
                    v.wait_ge(c.s_p2, now)
                    v.wait_ge(c.s_ds, now)
                    v.tensor_tensor(c.s1[:], c.ds[:], c.p2[:, 0], ALU.subtract).then_inc(c.s_s1, 1)
                if lstm:
                    v.wait_ge(c.s_gif, now)
                    v.wait_ge(c.s_x, now)
                    first_part(0, 6, c.p_gif, 0, c.xrow[j][:, 0:6], c.s_zh)
                if delta:
                    v.wait_ge(c.s_s1, now)
                    v.tensor_tensor(c.S[1 - j][:], c.s1[:], c.p2[:, 1], ALU.subtract).then_inc(c.s_S, 1)
                if lstm:
                    v.wait_ge(c.s_o, now)
                    first_part(6, 2, c.p_o, 0, c.xrow[j][:, 6:8], c.s_zoh)
                if delta and not last:
                    multiply_state(now, 1 - j)
                if lstm:
                    second_part(c.z[:, 0:6], 0, 6, c.p_gif, 0, c.s_zh, c.s_z, now)
                if delta and not last:
                    less_v(now, 1 - j)
                if lstm:
                    second_part(c.z[:, 6:8], 6, 2, c.p_o, 0, c.s_zoh, c.s_zo, now)
                    v.wait_ge(c.s_if, now)
                    v.tensor_tensor(c.fc[:], c.sif[:, 4:8], c.cell[:], ALU.mult)
                    v.wait_ge(c.s_g, now)
                    v.tensor_tensor(c.ig[:], c.sif[:, 0:4], c.tg[:], ALU.mult).then_inc(c.s_fc, 1)
                if rnn:
                    v.wait_ge(c.s_r, now)
                    if not lstm:
                        v.wait_ge(c.s_x, now)
                    first_part(8, KT, c.p_r, 1, c.xwrow[j][:], c.s_rzh)
                if lstm:
                    v.wait_ge(c.s_fc, now)
                    v.tensor_tensor(c.cell[:], c.fc[:], c.ig[:], ALU.add).then_inc(c.s_c, 1)
                if rnn:
                    second_part(c.rz[:], 8, KT, c.p_r, 1, c.s_rzh, c.s_rz, now)
                if lstm:
                    so, tc = (x[:].rearrange("p (k b) -> p k b", b=B) for x in (c.so, c.tc))
                    h = of_step(c.hT, before + tt)
                    v.wait_ge(c.s_tc, now)
                    v.scalar_tensor_tensor(c.hab[:, :, 0], so, HS, tc, ALU.mult, ALU.mult).then_inc(c.s_ha, 1)
                    v.tensor_tensor(h, so, tc, ALU.mult).then_inc(c.s_hf, 1)
                    v.wait_ge(c.s_hf, now)
                    v.scalar_tensor_tensor(c.hab[:, :, 1], h, HS, c.hab[:, :, 0], ALU.mult, ALU.subtract)\
                     .then_inc(c.s_hb, 1)

            if delta:
                multiply_state(before, 0)
                less_v(before, 0)
            steps(step)(v)

        @block.gpsimd
        def _(pool):
            def over_v(t, tt):
                return t[:, at(tt)].rearrange("p o g -> p g o").to_broadcast(shape)

            def lay_out_v(tt, j):
                pool.tensor_copy(c.row[j][:].rearrange("p (o x) -> p o x", o=1), c.kyk[:, at(tt), :])
                pool.tensor_tensor(c.vd[j][:], over_v(c.v, tt),
                                   c.diag[:].rearrange("p (o v) -> p o v", o=1).to_broadcast(shape),
                                   ALU.mult).then_inc(c.s_vd, 1)

            def decay_state(tt, now, j):
                pool.wait_ge(c.s_S, now)
                pool.tensor_tensor(c.ds[:], c.S[j][:], over_v(c.f, tt), ALU.mult).then_inc(c.s_ds, 1)
                pool.tensor_tensor(c.qs[j][:], c.q[:, at(tt), :].rearrange("p o g -> p g o").to_broadcast([128, 4, 4]),
                                   c.headones[:, 0:128:32].rearrange("p (o h) -> p o h", o=1)
                                   .to_broadcast([128, 4, 4]), ALU.mult).then_inc(c.s_q, 1)

            def lay_out_x(tt, j):
                if lstm:
                    last = pool.tensor_copy(c.xrow[j][:].rearrange("p (o m) b -> p o m b", o=1), xz[:, at(before + tt)])
                if rnn:
                    last = pool.tensor_copy(c.xwrow[j][:].rearrange("p (o m) b -> p o m b", o=1), c.xw[:, at(tt)])
                last.then_inc(c.s_x, 1)

            def step(tt, j, last):
                now = before + tt + 1
                soon = not isinstance(tt, int) or tt < CH - 2
                if delta and not last:
                    decay_state(tt + 1, now, 1 - j)
                    if soon:
                        lay_out_v(tt + 2, j)
                if (lstm or rnn) and soon:
                    if lstm:
                        pool.wait_ge(c.s_zoh, now)
                    if rnn:
                        pool.wait_ge(c.s_rzh, now)
                    lay_out_x(tt + 2, j)

            if lstm or rnn:
                lay_out_x(0, 0)
                lay_out_x(1, 1)
            if delta:
                decay_state(0, before, 0)
                lay_out_v(0, 0)
                lay_out_v(1, 1)
            steps(step)(pool)


def project_and_mix(c, ci, project, mix, first_mix=False):
    nc = c.nc
    n_p, n_m = ci, ci - 1

    def tokens(t, k, i):
        return t[:, k, i * CT:(i + 1) * CT] if isinstance(i, int) else t[:, k, bass.ds(i * CT, CT)]

    def both(t):
        return t.rearrange("p (m t b) -> p m t b", m=KT, b=B)

    def by_time(t, j=0):
        return t[:, :, j * 4:(j + 1) * 4].rearrange("p t (m b) -> p m t b", b=B)

    R = c.room
    sk, sv, sq, sbt, fd, kk, t1, t2, kn, w, o4, sg, y, y2 = (blk(R, i, CW) for i in range(14))
    f1 = R[0:RD, 14 * CW:14 * CW + CT]
    g1 = R[0:RD, 14 * CW + CT:15 * CW]
    pk, pv, pq, pf, pb, ps, pin = (bank[:, 0:CW] for bank in c.banks[:7])
    pgate, pms = (bank[:, 0:CW] for bank in c.banks[0:2])
    px, px2 = c.banks[2:4], c.banks[4]
    with nc.Block() as block:
        @block.tensor
        def _(pe):
            if project:
                rows = [tokens(c.hT, k, ci) for k in range(KT)]
                for k in range(KT):
                    mm = pe.matmul(pin[0:RD, 0:CT], c.wf1[:, k, :], rows[k], start=(k == 0), stop=(k == KT - 1))
                mm.then_inc(c.q_f1, 1)
                for bank, wt, done in ((pk, c.wk, c.q_p), (pb, c.wbs, c.q_p), (pv, c.wv, c.q_p), (pq, c.wq, c.q_p)):
                    for m in range(KT):
                        for k in range(KT):
                            mm = pe.matmul(bank[:, m * CT:(m + 1) * CT], wt[:, k, m * 128:(m + 1) * 128], rows[k],
                                           start=(k == 0), stop=(k == KT - 1))
                    mm.then_inc(done, 1)
                pe.wait_ge(c.q_f1e, n_p + 1)
                for m in range(KT):
                    mm = pe.matmul(pf[:, m * CT:(m + 1) * CT], c.wf2[:, m * 128:(m + 1) * 128], f1, start=True, stop=True)
                mm.then_inc(c.q_p, 1)
            if mix:
                rows = [tokens(c.hT, k, ci - 1) for k in range(KT)]
                for k in range(KT):
                    mm = pe.matmul(pin[0:RD, 0:CT], c.wg1[:, k, :], rows[k], start=(k == 0), stop=(k == KT - 1))
                mm.then_inc(c.m_g1, 1)
                pe.wait_ge(c.m_g1e, n_m + 1)
                if project:
                    pe.wait_ge(c.q_kk, n_p + 1)
                for m in range(KT):
                    mm = pe.matmul(pgate[:, m * CT:(m + 1) * CT], c.wg2[:, m * 128:(m + 1) * 128], g1, start=True, stop=True)
                mm.then_inc(c.m_g, 1)
            if project:
                pe.wait_ge(c.q_k2, n_p + 1)
                pe.matmul(ps[:], c.headones[:], t1, start=True, stop=True).then_inc(c.q_ss, 1)
                pe.wait_ge(c.q_kw, n_p + 1)
                pe.matmul(ps[:], c.headones[:], t1, start=True, stop=True).then_inc(c.q_gm, 1)
            if mix:
                pe.wait_ge(c.m_y2, n_m + 1)
                pe.matmul(pms[:], c.headones[:], y2, start=True, stop=True).then_inc(c.m_ms, 1)
                pe.wait_ge(c.m_yn, n_m * 2 + 2)
                for m in range(KT):
                    for k in range(KT):
                        mm = pe.matmul(px[m][:, 0:CT], c.wo[:, k, m * 128:(m + 1) * 128], y[:, k * CT:(k + 1) * CT],
                                       start=(k == 0), stop=(k == KT - 1))
                    mm.then_inc(c.m_x, 1)
                pe.wait_ge(c.m_x1, n_m * KT + KT)
                for m in range(KT):
                    for k in range(KT):
                        mm = pe.matmul(px2[:, m * CT:(m + 1) * CT], c.wx2[:, k, m * 128:(m + 1) * 128],
                                       tokens(c.xT, k, ci - 1), start=(k == 0), stop=(k == KT - 1))
                    mm.then_inc(c.m_xw, 1)

        @block.scalar
        def _(act):
            if project:
                act.wait_ge(c.q_f1, n_p + 1)
                act.activation(f1, pin[0:RD, 0:CT], ACT.Copy).then_inc(c.q_f1e, 1)
                for i, (dst, src) in enumerate(((sk, pk), (sbt, pb), (sv, pv), (sq, pq), (fd, pf))):
                    act.wait_ge(c.q_p, n_p * 5 + (i + 1))
                    act.activation(dst, src[:], ACT.Sigmoid).then_inc(c.q_sig, 1)
            if mix:
                act.wait_ge(c.m_g1, n_m + 1)
                act.activation(g1, pin[0:RD, 0:CT], ACT.Copy).then_inc(c.m_g1e, 1)
                act.wait_ge(c.m_g, n_m + 1)
                act.activation(sg, pgate[:], ACT.Sigmoid).then_inc(c.m_sg, 1)
            if project:
                act.wait_ge(c.q_r, n_p + 1)
                act.activation(t1, t2, ACT.Sqrt).then_inc(c.q_rt, 1)
            if mix:
                act.wait_ge(c.m_r, n_m + 1)
                act.activation(y2, sg, ACT.Sqrt).then_inc(c.m_rt, 1)
                for m in range(KT):
                    act.wait_ge(c.m_xw, n_m * KT + KT)
                    act.activation(c.xw[:, :, m, :], px2[:, m * CT:(m + 1) * CT].rearrange("p (t b) -> p t b", b=B),
                                   ACT.Identity, bias=c.b2[:, m:m + 1]).then_inc(c.m_xwe, 1)

        @block.vector
        def _(v):
            if project:
                sig = n_p * 5
                v.wait_ge(c.q_sig, sig + 1)
                v.tensor_tensor(kk, pk[:], sk, ALU.mult).then_inc(c.q_kk, 1)
                v.wait_ge(c.q_kk, n_p + 1)
                v.tensor_tensor(t1, kk, kk, ALU.mult).then_inc(c.q_k2, 1)
                v.wait_ge(c.q_sig, sig + 3)
                v.tensor_tensor(by_time(c.v), both(pv[:]), both(sv), ALU.mult)
                v.wait_ge(c.q_sig, sig + 4)
                v.tensor_tensor(by_time(c.q), both(pq[:]), both(sq), ALU.mult).then_inc(c.q_q, 1)
                v.wait_ge(c.q_ss, n_p + 1)
                v.tensor_scalar(w, ps[:], 1e-6, None, ALU.add).then_inc(c.q_e, 1)
                v.wait_ge(c.q_e, n_p + 1)
                v.reciprocal(t2, w).then_inc(c.q_r, 1)
            if project:
                v.wait_ge(c.q_rt, n_p + 1)
                v.tensor_tensor(kn, kk, t1, ALU.mult).then_inc(c.q_kn, 1)
                v.wait_ge(c.q_sig, sig + 5)
                v.wait_ge(c.q_kn, n_p + 1)
                v.tensor_tensor(w, fd, kn, ALU.mult).then_inc(c.q_w, 1)
                v.wait_ge(c.q_w, n_p + 1)
                v.tensor_tensor(t1, kn, w, ALU.mult).then_inc(c.q_kw, 1)
                v.tensor_copy(by_time(c.kyk, 0), both(kn))
                v.tensor_copy(by_time(c.kyk, 2), both(kn))
                v.tensor_copy(by_time(c.f), both(fd))
                v.tensor_tensor(sk, sbt, kn, ALU.mult).then_inc(c.q_bk, 1)
                v.scalar_tensor_tensor(sv, sbt, 2.0, w, ALU.mult, ALU.mult)
                v.wait_ge(c.q_bk, n_p + 1)
                v.tensor_tensor(sq, sk, sbt, ALU.mult).then_inc(c.q_bbk, 1)
                v.wait_ge(c.q_gm, n_p + 1)
                v.wait_ge(c.q_bbk, n_p + 1)
                v.scalar_tensor_tensor(t2, ps[:], 2.0, sq, ALU.mult, ALU.mult).then_inc(c.q_y, 1)
                v.wait_ge(c.q_y, n_p + 1)
                v.tensor_tensor(by_time(c.kyk, 1), both(sv), both(t2), ALU.subtract).then_inc(c.q_done, 1)
            if mix:
                for h in range(4):
                    src = c.o.rearrange("p t (m b h) -> p m t b h", m=KT, b=B)[:, :, :, :, h]
                    last = v.tensor_copy(both(o4[32 * h:32 * h + 32]), src)
                last.then_inc(c.m_o, 1)
                v.wait_ge(c.m_o, n_m + 1)
                v.wait_ge(c.m_sg, n_m + 1)
                v.tensor_tensor(y, o4, sg, ALU.mult).then_inc(c.m_y, 1)
                v.wait_ge(c.m_y, n_m + 1)
                v.tensor_tensor(y2, y, y, ALU.mult).then_inc(c.m_y2, 1)
                v.wait_ge(c.m_ms, n_m + 1)
                v.tensor_scalar(o4, pms[:], 1.0 / RD, 1e-6, ALU.mult, ALU.add).then_inc(c.m_e, 1)
                v.wait_ge(c.m_e, n_m + 1)
                v.reciprocal(sg, o4).then_inc(c.m_r, 1)
                v.wait_ge(c.m_rt, n_m + 1)
                for k in range(KT):
                    s = slice(k * CT, (k + 1) * CT)
                    v.scalar_tensor_tensor(y[:, s], y[:, s], c.nw[:, k:k + 1], y2[:, s], ALU.mult, ALU.mult)\
                     .then_inc(c.m_yn, 1)
                for m in range(KT):
                    v.wait_ge(c.m_x, n_m * KT + (m + 1))
                    x1 = tokens(c.xT, m, ci - 1)
                    v.tensor_tensor(x1, px[m][:, 0:CT], x1, ALU.add).then_inc(c.m_x1, 1)
                if first_mix:
                    v.wait_ge(c.m_xwe, KT)
                    v.tensor_tensor(c.xw[:, 0], c.xw[:, 0], c.r0[:], ALU.add)


def phase_weights(c):
    nc, a = c.nc, c.a
    s_w = c.sem("delta_weights")
    with nc.Block() as block:
        @block.sync
        def _(sp):
            for t, n in ((c.wq, "attn_Wq"), (c.wk, "attn_Wk"), (c.wv, "attn_Wv"), (c.wf1, "attn_Wf1"),
                         (c.wbeta, "attn_Wbeta"), (c.wg1, "attn_Wog1"), (c.wo, "attn_Wo"), (c.wx2, "cond2_Wx")):
                sp.dma_start(t[:], a["L0_" + n].rearrange("(k p) n -> p k n", p=128)).then_inc(s_w, 16)
            sp.dma_start(c.wf2[:], a["L0_attn_Wf2"]).then_inc(s_w, 16)
            sp.dma_start(c.wg2[:], a["L0_attn_Wog2"]).then_inc(s_w, 16)
            with nc.allow_non_contiguous_dma("small vectors"):
                sp.dma_start(c.nw[:], col(a["L0_attn_norm_w"])).then_inc(s_w, 16)
                sp.dma_start(c.b2[:], col(a["L0_cond2_b"])).then_inc(s_w, 16)

        @block.gpsimd
        def _(pool):
            pool.wait_ge(s_w, 192)
            pool.tensor_copy(c.wbs[:].rearrange("p k (h r) -> p k h r", r=RD),
                             c.wbeta[:].rearrange("p k (h o) -> p k h o", o=1).to_broadcast([128, KT, RH, RD]))


def phases_recurrent(c):
    nc = c.nc
    st = ExitStack()
    with st:
        c.hab = c.sb("h_parts", [128, KT, 2, B], f16, st)
        c.z = c.sb("z", [128, 8, B], f32, st)
        c.zh = c.sb("z_part", [128, 10, B], f32, st)
        c.sif = c.sb("sig_if", [128, 8], f32, st)
        c.tg, c.so, c.cell, c.fc, c.ig, c.tc = (c.sb(n, [128, 4], f32, st) for n in
                                                ("tanh_g", "sig_o", "cell", "f_cell", "i_g", "tanh_cell"))
        c.S = [c.sb(f"state{i}", [128, 4, RD], f32, st) for i in range(2)]
        c.prod, c.p2 = (c.sb(n, [128, 2, 4, RD], f32, st) for n in ("k_and_y_times_state", "updates"))
        c.ds, c.s1 = (c.sb(n, [128, 4, RD], f32, st) for n in ("decayed_state", "half_updated"))
        c.vd = [c.sb(f"v_on_diagonal{i}", [128, 4, RD], f32, st) for i in range(2)]
        c.row = [c.sb(f"k_y_k_of_step{i}", [128, 12], f32, st) for i in range(2)]
        c.qs = [c.sb(f"q_per_head{i}", [128, 4, 4], f32, st) for i in range(2)]
        c.kyk = c.sb("k_y_k", [128, CH, 12], f32, st)
        c.f, c.q, c.v = (c.sb(n, [128, CH, 4], f32, st) for n in ("decay", "q", "v"))
        c.o = c.sb("o_rows", [RD, CH, 16], f32, st)
        c.rab = c.sb("r_parts", [128, KT, 2, B], f16, st)
        c.xrow, c.xwrow = ([c.sb(f"{n}{i}", [128, m, B], f32, st) for i in range(2)]
                           for n, m in (("lstm_x_of_step", 8), ("rnn_x_of_step", KT)))
        c.rz, c.rh = (c.sb(n, [128, KT, B], f32, st) for n in ("r_z", "r_state"))
        c.xw = c.sb("rnn_xw", [128, CH, KT, B], f32, st)
        c.wq, c.wk, c.wv, c.wo, c.wx2, c.wbs = (c.sb(n, [128, KT, D], f32, st) for n in (
            "delta_Wq", "delta_Wk", "delta_Wv", "mix_Wo", "rnn_Wx", "delta_Wbeta_spread"))
        c.wf1, c.wg1 = (c.sb(n, [128, KT, RD], f32, st) for n in ("delta_Wf1", "gate_W1"))
        c.wf2, c.wg2 = (c.sb(n, [RD, D], f32, st) for n in ("delta_Wf2", "gate_W2"))
        c.wbeta = c.sb("delta_Wbeta", [128, KT, RH], f32, st)
        c.nw, c.b2 = (c.sb(n, [128, KT], f32, st) for n in ("norm_w", "rnn_b"))
        c.room = c.sb("chunk_temporaries", [128, 15 * CW], f32, st)
        c.banks = [c.pb(f"bank{i}", st) for i in range(8)]
        c.p_gif, c.p_o, c.p_r = c.banks[0:3]
        c.p_u, c.p_od = c.banks[3:5], c.banks[5:7]
        (c.s_gif, c.s_o, c.s_z, c.s_zo, c.s_if, c.s_g, c.s_so, c.s_fc, c.s_c, c.s_tc, c.s_ha, c.s_hf, c.s_hb,
         c.s_zh, c.s_zoh) = (c.sem("lstm_" + n) for n in (
             "gif_products", "o_products", "z_gif", "z_o", "sig_if", "tanh_g", "sig_o", "cell_parts", "cell",
             "tanh_cell", "h_high", "h", "h_low", "z_gif_part", "z_o_part"))
        (c.s_S, c.s_prod, c.s_ds, c.s_p2, c.s_s1, c.s_u, c.s_vd, c.s_q, c.s_om, c.s_oe, c.s_py) = (
            c.sem("delta_" + n) for n in ("state", "prod", "decayed", "updates", "half_updated", "projections",
                                          "v_on_diagonal", "q_laid_out", "o_made", "o_stored", "y_prod"))
        c.s_r, c.s_rz, c.s_rh, c.s_ra, c.s_rb, c.s_rzh = (c.sem("rnn_" + n) for n in
                                                          ("products", "z", "state", "high", "low", "z_part"))
        (c.q_f1, c.q_p, c.q_f1e, c.q_k2, c.q_ss, c.q_kw, c.q_gm, c.q_done, c.q_sig, c.q_r, c.q_rt, c.q_kk, c.q_q,
         c.q_e, c.q_kn, c.q_w, c.q_bk, c.q_bbk, c.q_y) = (c.sem("project_" + n) for n in (
             "f1", "products", "f1_stored", "k_squared", "sum_of_squares", "k_fk", "gamma", "done", "sigmoids",
             "reciprocal", "root", "silu_k", "q_made", "plus_eps", "k_unit", "fk", "bk", "bbk", "y_part"))
        (c.m_g1, c.m_g1e, c.m_g, c.m_y2, c.m_ms, c.m_yn, c.m_x, c.m_x1, c.m_xw, c.m_sg, c.m_r, c.m_rt, c.m_xwe,
         c.m_o, c.m_y, c.m_e) = (c.sem("mix_" + n) for n in (
             "g1", "g1_stored", "gate", "squares", "sum_of_squares", "normed", "products", "x1", "xw_products",
             "sigmoid", "reciprocal", "root", "xw", "o_turned", "gated", "plus_eps"))
        c.s_x = c.sem("x_rows_laid_out")
        phase_weights(c)
        phase_start(c)
        recurrences(c, 0, True, False, False)
        project_and_mix(c, 0, True, False)
        recurrences(c, 1, True, True, False)
        project_and_mix(c, 1, True, True, first_mix=True)
        with nc.Fori(2, NC) as ci:
            recurrences(c, ci, True, True, True)
            project_and_mix(c, ci, True, True)
        recurrences(c, NC, False, True, True)
        project_and_mix(c, NC, False, True)
        recurrences(c, NC + 1, False, False, True)


def phase_heads(c):
    nc, a = c.nc, c.a
    st = ExitStack()
    with st:
        w = c.sb("w_qkv", [128, KT, 3 * D], f32, st)
        wp = c.sb("w_qk_padded", [128, KT, 2, 4, 128], f32, st)
        pq = [c.pb(f"qk_psum{i}", st) for i in range(2)]
        pv = [c.pb(f"v_psum{i}", st) for i in range(2)]
        s_w, s_0, s_pad = c.sem("qkv_weights"), c.sem("qk_zeroed"), c.sem("qk_padded")
        s_q, s_qe, s_v, s_ve, s_m = c.sem("qk_made"), c.sem("qk_evac"), c.sem("v_made"), c.sem("v_evac"), c.sem("masks")
        with nc.Block() as block:
            @block.sync
            def _(sp):
                sp.dma_start(w[:], a["L0_ffn_w_qkv"].rearrange("(k p) n -> p k n", p=128)).then_inc(s_w, 16)

            @block.gpsimd
            def _(pool):
                pool.memset(wp[:], 0.0).then_inc(s_0, 1)
                pool.memset(c.rowmax[:], 0.0).then_inc(s_0, 1)
                pool.memset(c.vt[:], 0.0).then_inc(s_0, 1)
                pool.memset(c.mask_q[:], 0.0).then_inc(s_0, 1)
                pool.memset(c.mask_k[:], 0.0).then_inc(s_0, 1)
                pool.wait_ge(s_0, 5)
                pool.affine_select(out=c.mask_q[:], in_=c.mask_q[:], compare_op=ALU.is_ge, fill=-1e30, base=0,
                                   pattern=[[-1, 128]], channel_multiplier=1).then_inc(s_m, 1)
                pool.affine_select(out=c.mask_k[:], in_=c.mask_k[:], compare_op=ALU.is_ge, fill=-1e30, base=0,
                                   pattern=[[1, 128]], channel_multiplier=-1).then_inc(s_m, 1)
                pool.memset(c.vt[:, :, :, AD:AD + 1], 1.0).then_inc(s_m, 1)

            @block.tensor
            def _(pe):
                pe.wait_ge(s_pad, 2 * KT)
                with pe.Fori(0, NB) as n:
                    for j in range(2):
                        for g in range(4):
                            i = j * 4 + g
                            pe.wait_ge(s_qe, n * 8 + (i + 1))
                            for k in range(KT):
                                mm = pe.matmul(pq[i % 2][:], wp[:, k, j, g, :], c.hT[:, k, bass.ds(n * 512, 512)],
                                               start=(k == 0), stop=(k == KT - 1))
                            mm.then_inc(s_q, 1)
                for b in range(B):
                    for i in range(T // 128):
                        u = b * (T // 128) + i
                        if u >= 2:
                            pe.wait_ge(s_ve, u - 1)
                        for k in range(KT):
                            rows = c.hT[:, k, :].rearrange("p (t b) -> p b t", b=B)[:, b, i * 128:(i + 1) * 128]
                            mm = pe.matmul(pv[u % 2][:, 0:D], rows, w[:, k, 2 * D:3 * D], start=(k == 0), stop=(k == KT - 1))
                        mm.then_inc(s_v, 1)

            @block.vector
            def _(v):
                v.wait_ge(s_0, 1)
                v.wait_ge(s_w, 16)
                for k in range(KT):
                    for j in range(2):
                        v.tensor_copy(wp[:, k, j].rearrange("p g (h r) -> p (g h) r", r=32)[:, :, 0:AD],
                                      w[:, k, j * D:(j + 1) * D].rearrange("p (h d) -> p h d", d=AD)).then_inc(s_pad, 1)
                v.tensor_copy(c.ident16[:], c.ident[:])
                v.tensor_scalar(c.dsel[:], c.headones[:], c.diag[:, AD:AD + 1], None, ALU.mult)
                v.wait_ge(s_m, 3)
                for b in range(B):
                    for i in range(T // 128):
                        u = b * (T // 128) + i
                        v.wait_ge(s_v, u + 1)
                        v.tensor_copy(c.vt[:, u, :, 0:AD], pv[u % 2][:, 0:D].rearrange("p (h d) -> p h d", d=AD))\
                         .then_inc(s_ve, 1)

            @block.scalar
            def _(act):
                act.activation(c.scratch[:, 0:2], c.ones[:, 0:2], ACT.Copy).then_inc(s_qe, 2)
                with act.Fori(0, NB) as n:
                    for j, dst in enumerate((c.qT, c.kT)):
                        for g in range(4):
                            i = j * 4 + g
                            act.wait_ge(s_q, n * 8 + (i + 1))
                            act.activation(dst[:, g, bass.ds(n * 512, 512)], pq[i % 2][:], ACT.Copy).then_inc(s_qe, 1)


def tiles_of(size):
    out = []
    for i in range(size // 128):
        for lo in range(0, size, 512):
            out.append((i, lo, lo + 512))
    return out


def phase_attend(c):
    nc = c.nc
    QT = T // 128
    st = ExitStack()
    with st:
        qh2 = [c.sb(f"q_of_head{i}", [128, 4, T], f32, st) for i in range(2)]
        nm = c.sb("minus_head_rows", [128, 4], f32, st)
        ks2 = [c.sb(f"k_staged{i}", [128, T], f32, st) for i in range(2)]
        vs2 = [c.sb(f"v_staged{i}", [128, QT, 4, 32], f32, st) for i in range(2)]
        pr = [c.sb(f"probs{i}", [128, 512], f32, st) for i in range(8)]
        ob = c.sb("o_unscaled", [128, T], f32, st)
        big = [c.pb(f"scores{i}", st, 1024) for i in range(2)]
        pm = c.pb("max_in_rows", st, 1024)
        po = c.pb("o_sums", st, 1024)
        s_st, s_s, s_m, s_r, s_q = (c.sem(n) for n in ("staged", "scores_q", "max_taken", "max_turned", "q_ready"))
        s_t, s_e, s_o, s_oc, s_d, s_dr = (c.sem(n) for n in ("scores_k", "exp_made", "o_summed", "o_copied",
                                                             "den_spread", "den_recip"))
        s_dd, s_nm = c.sem("o_scaled"), c.sem("head_rows_made")
        kt = [(i, max(i * 128, lo), lo + 512) for i in range(QT) for lo in (0, 512) if lo + 512 > i * 128]
        NK = len(kt)
        with nc.Block() as block:
            @block.vector
            def _(v):
                v.tensor_copy(c.scratch[:, 0:2], c.ones[:, 0:2]).then_inc(s_m, 2)
                v.tensor_scalar(nm[:], c.headones[:, 0:128:32], -1.0, None, ALU.mult).then_inc(s_nm, 1)
                v.wait_ge(s_nm, 1)
                v.tensor_copy(c.scratch[:, 2:4], c.ones[:, 0:2]).then_inc(s_dr, 2)

                def of_unit(t, g, b):
                    t = t[:, g:g + 1, :] if isinstance(g, int) else t[:, bass.ds(g, 1), :]
                    return t.rearrange("p o (t b) -> p b (o t)", b=B)[:, b:b + 1, :]

                def stage(g, b):
                    for h in range(4):
                        v.tensor_scalar(qh2[b][:, h:h + 1, :], of_unit(c.qT, g, b), c.headones[:, 32 * h:32 * h + 1],
                                        None, ALU.mult).then_inc(s_st, 1)
                    v.tensor_scalar(ks2[b][:].rearrange("p (o t) -> p o t", o=1), of_unit(c.kT, g, b),
                                    c.diag[:, AD:AD + 1], None, ALU.add).then_inc(s_st, 1)
                    heads = slice(g * 4, g * 4 + 4) if isinstance(g, int) else bass.ds(g * 4, 4)
                    v.tensor_copy(vs2[b][:], c.vt[:, b * QT:(b + 1) * QT, heads, :]).then_inc(s_st, 1)

                def unit(g, b, following):
                    u = g * B + b
                    qh = qh2[b]
                    for h in range(4):
                        for i in range(QT):
                            n = h * QT + i
                            v.wait_ge(s_s, u * (4 * QT) + (n + 1))
                            v.tensor_reduce(c.rowmax[:, i, h, AD:AD + 1], big[n % 2][:, 0:(i + 1) * 128], AX.X,
                                            ALU.max).then_inc(s_m, 1)
                    for half in range(2):
                        v.wait_ge(s_r, u * 2 + (half + 1))
                        for h in range(4):
                            v.scalar_tensor_tensor(blk(qh[:, h], half), blk(pm, half), nm[:, h:h + 1],
                                                   blk(qh[:, h], half), ALU.mult, ALU.add).then_inc(s_q, 1)
                    if following is not None:
                        stage(*following)
                    for half in range(2):
                        v.wait_ge(s_d, u * 2 + (half + 1))
                        v.reciprocal(pr[half][:], blk(pm, half)).then_inc(s_dr, 1)
                    for half in range(2):
                        v.wait_ge(s_dr, u * 2 + (half + 3))
                        v.tensor_tensor(blk3(of_unit(c.oT, g, b), half), blk(ob, half).rearrange("p (o t) -> p o t", o=1),
                                        pr[half][:].rearrange("p (o t) -> p o t", o=1), ALU.mult).then_inc(s_dd, 1)

                stage(0, 0)
                with v.Fori(0, 3) as g:
                    unit(g, 0, (g, 1))
                    unit(g, 1, (g + 1, 0))
                unit(3, 0, (3, 1))
                unit(3, 1, None)

            @block.tensor
            def _(pe):
                with pe.Fori(0, 4) as g:
                    for b in range(B):
                        u = g * B + b
                        qh, ks, vs = qh2[b], ks2[b], vs2[b]
                        pe.wait_ge(s_st, u * 6 + 6)
                        for h in range(4):
                            for i in range(QT):
                                n = h * QT + i
                                pe.wait_ge(s_m, u * (4 * QT) + (n + 1))
                                s = big[n % 2]
                                d = i * 128
                                for lo in range(0, d + 128, 512):
                                    hi = min(lo + 512, d + 128)
                                    here = hi == d + 128
                                    if here:
                                        pe.matmul(s[:, d:d + 128], c.ident16[:], c.mask_q[:], start=True, stop=True,
                                                  skip_group_check=True)
                                    mm = pe.matmul(s[:, lo:hi], qh[:, h, d:d + 128], ks[:, lo:hi], start=not here, stop=True,
                                                   skip_group_check=True)
                                mm.then_inc(s_s, 1)
                        pe.wait_ge(s_m, (u + 1) * (4 * QT) + 2)
                        pe.wait_ge(s_dr, u * 2 + 2)
                        for half in range(2):
                            for i in range(4 * half, 4 * half + 4):
                                mm = pe.matmul(pm[:, i * 128:(i + 1) * 128],
                                               c.rowmax[:, i].rearrange("p h r -> p (h r)"), c.ident[:],
                                               start=True, stop=True)
                            mm.then_inc(s_r, 1)
                        pe.wait_ge(s_q, u * 8 + 4)

                        def scores(m):
                            h, (i, lo, hi) = m % 4, kt[m // 4]
                            s = big[m % 4 // 2][:, m % 2 * 512:m % 2 * 512 + hi - lo]
                            if m >= 4:
                                pe.wait_ge(s_e, u * (4 * NK) + (m - 3))
                            diag = lo == i * 128
                            if diag:
                                pe.matmul(s[:, 0:128], c.ident16[:], c.mask_k[:], start=True, stop=True,
                                          skip_group_check=True)
                            pe.matmul(s, ks[:, i * 128:(i + 1) * 128], qh[:, h, lo:hi], start=not diag, stop=True,
                                      skip_group_check=True).then_inc(s_t, 1)

                        def sums(m):
                            h, (i, lo, hi) = m % 4, kt[m // 4]
                            pe.wait_ge(s_e, u * (4 * NK) + (m + 1))
                            last = (i == 3 and hi == 512) or i == 7
                            pe.matmul(po[32 * h:32 * h + 32, lo:hi], vs[:, i, h, :], pr[m % 8][:, 0:hi - lo],
                                      start=(i == 0), stop=last).then_inc(s_o, 1)

                        for x in range(NK + 1):
                            if x == 1:
                                pe.wait_ge(s_q, u * 8 + 8)
                            for h in range(4):
                                if x < NK:
                                    scores(4 * x + h)
                            for h in range(4):
                                if x > 0:
                                    sums(4 * (x - 1) + h)
                        for half in range(2):
                            pe.wait_ge(s_oc, u * 2 + (half + 1))
                            pe.matmul(blk(pm, half), c.dsel[:], blk(ob, half), start=True, stop=True).then_inc(s_d, 1)

            @block.scalar
            def _(act):
                with act.Fori(0, 4) as g:
                    for b in range(B):
                        u = g * B + b
                        for m in range(4 * NK):
                            i, lo, hi = kt[m // 4]
                            act.wait_ge(s_t, u * (4 * NK) + (m + 1))
                            if m >= 8:
                                act.wait_ge(s_o, u * (4 * NK) + (m - 7))
                            act.activation(pr[m % 8][:, 0:hi - lo], big[m % 4 // 2][:, m % 2 * 512:m % 2 * 512 + hi - lo],
                                           ACT.Exp, scale=float(AD) ** -0.5).then_inc(s_e, 1)
                        act.wait_ge(s_o, (u + 1) * (4 * NK))
                        for half in range(2):
                            act.activation(blk(ob, half), blk(po, half), ACT.Copy).then_inc(s_oc, 1)


def phase_attn_out(c):
    nc, a = c.nc, c.a
    st = ExitStack()
    with st:
        wo = c.sb("w_o_padded", [128, 4, D], f32, st)
        px = [c.pb(f"attn_out_psum{i}", st) for i in range(2)]
        s_0, s_w, s_p, s_e = c.sem("w_o_zeroed"), c.sem("w_o_loaded"), c.sem("attn_out_made"), c.sem("attn_out_added")
        with nc.Block() as block:
            @block.gpsimd
            def _(pool):
                pool.memset(wo[:], 0.0).then_inc(s_0, 1)

            @block.sync
            def _(sp):
                sp.wait_ge(s_0, 1)
                for h in range(4):
                    sp.dma_start(wo[32 * h:32 * h + AD], a["L0_ffn_w_o"].rearrange("(g h d) n -> h d g n", h=4, d=AD)[h])\
                      .then_inc(s_w, 16)

            @block.tensor
            def _(pe):
                pe.wait_ge(s_w, 64)
                for n in range(NB):
                    for m in range(KT):
                        if n:
                            pe.wait_ge(s_e, (n - 1) * KT + m + 1)
                        for g in range(4):
                            mm = pe.matmul(px[m][:], wo[:, g, m * 128:(m + 1) * 128], blk(c.oT[:, g], n),
                                           start=(g == 0), stop=(g == 3))
                        mm.then_inc(s_p, 1)

            @block.vector
            def _(v):
                for n in range(NB):
                    for m in range(KT):
                        v.wait_ge(s_p, n * KT + m + 1)
                        x = blk(c.hT[:, m], n)
                        v.tensor_tensor(x, px[m][:], x, ALU.add).then_inc(s_e, 1)


def phase_layernorm(c, tag, other, out, gain, shift, residual):
    nc, a = c.nc, c.a
    st = ExitStack()
    with st:
        gb = c.sb(tag + "_gain_shift", [128, 2, KT], f32, st)
        mean_of = c.sb(tag + "_one_over_d", [128, 128], f32, st)
        r = c.sb(tag + "_sum", [128, KT, 512], f32, st)
        sq = c.sb(tag + "_squares", [128, KT, 512], f32, st)
        rt = c.sb(tag + "_root", [128, 512], f32, st)
        pm, pv = c.pb(tag + "_mean", st), c.pb(tag + "_var", st)
        s_w, s_k, s_r, s_m, s_c, s_v, s_e, s_rt, s_n = (c.sem(f"{tag}_{n}") for n in (
            "weights", "const", "summed", "mean_made", "squared", "var_made", "recip", "root_made", "normed"))
        with nc.Block() as block:
            @block.sync
            def _(sp):
                with nc.allow_non_contiguous_dma("small vectors"):
                    sp.dma_start(gb[:, 0], col(a[gain])).then_inc(s_w, 16)
                    sp.dma_start(gb[:, 1], col(a[shift])).then_inc(s_w, 16)

            @block.gpsimd
            def _(pool):
                pool.memset(mean_of[:], 1.0 / D).then_inc(s_k, 1)

            @block.tensor
            def _(pe):
                pe.wait_ge(s_k, 1)
                with pe.Fori(0, NB) as n:
                    for bank, src, ready, done in ((pm, r, s_r, s_m), (pv, sq, s_c, s_v)):
                        pe.wait_ge(ready, n + 1)
                        for k in range(KT):
                            mm = pe.matmul(bank[:], mean_of[:], src[:, k], start=(k == 0), stop=(k == KT - 1))
                        mm.then_inc(done, 1)

            @block.vector
            def _(v):
                v.wait_ge(s_w, 32)
                with v.Fori(0, NB) as n:
                    x = c.hT[:, :, bass.ds(n * 512, 512)]
                    if other is None:
                        v.tensor_copy(r[:], x).then_inc(s_r, 1)
                    else:
                        v.tensor_tensor(r[:], x, other[:, :, bass.ds(n * 512, 512)], ALU.add).then_inc(s_r, 1)
                    v.wait_ge(s_m, n + 1)
                    v.wait_ge(s_r, n + 1)
                    for k in range(KT):
                        v.tensor_tensor(r[:, k], r[:, k], pm[:], ALU.subtract).then_inc(s_n, 1)
                    v.wait_ge(s_n, n * 8 + 2)
                    v.tensor_tensor(sq[:], r[:], r[:], ALU.mult).then_inc(s_c, 1)
                    v.wait_ge(s_v, n + 1)
                    v.tensor_scalar(rt[:], pv[:], 1e-5, None, ALU.add).then_inc(s_n, 1)
                    v.wait_ge(s_n, n * 8 + 3)
                    v.reciprocal(rt[:], rt[:]).then_inc(s_e, 1)
                    v.wait_ge(s_rt, n + 1)
                    for k in range(KT):
                        v.scalar_tensor_tensor(sq[:, k], r[:, k], gb[:, 0, k:k + 1], rt[:], ALU.mult, ALU.mult)\
                         .then_inc(s_n, 1)
                    v.wait_ge(s_n, n * 8 + 5)
                    for k in range(KT):
                        dst = out[:, k, bass.ds(n * 512, 512)]
                        if residual:
                            v.scalar_tensor_tensor(dst, sq[:, k], gb[:, 1, k:k + 1], dst, ALU.add, ALU.add)\
                             .then_inc(s_n, 1)
                        else:
                            v.tensor_scalar(dst, sq[:, k], gb[:, 1, k:k + 1], None, ALU.add).then_inc(s_n, 1)
                    v.tensor_copy(c.scratch[:, 0:2], c.ones[:, 0:2]).then_inc(s_n, 1)
                    v.wait_ge(s_n, n * 8 + 8)

            @block.scalar
            def _(act):
                with act.Fori(0, NB) as n:
                    act.wait_ge(s_e, n + 1)
                    act.activation(rt[:], rt[:], ACT.Sqrt).then_inc(s_rt, 1)


def phase_router(c):
    nc, a = c.nc, c.a
    NT = TOK // 128
    st = ExitStack()
    with st:
        wg = c.sb("w_router", [128, KT, EX], f32, st)
        before = c.sb("expert_before", [128, EX, EX], f32, st)
        p = c.sb("expert_probs", [128, NT, EX], f32, st)
        mx = c.sb("expert_max", [128, NT], f32, st)
        sm = c.sb("expert_sum", [128, NT], f32, st)
        gt = c.sb("expert_greater", [128, NT, EX, EX], f32, st)
        eq = c.sb("expert_equal", [128, NT, EX, EX], f32, st)
        rank = c.sb("expert_rank", [128, NT, EX], f32, st)
        pl = c.pb("logits", st)
        pt = c.pb("weights_turned", st, 2048)
        s_w, s_b, s_l, s_d, s_x, s_t = (c.sem(n) for n in ("router_w", "router_const", "logits_made", "router_dve",
                                                           "router_exp", "weights_turned_s"))
        s_te = c.sem("weights_evacuated")
        with nc.Block() as block:
            @block.sync
            def _(sp):
                with nc.allow_non_contiguous_dma("narrow rows"):
                    sp.dma_start(wg[:], a["L0_ffn_wg"].rearrange("(k p) n -> p k n", p=128)).then_inc(s_w, 16)

            @block.gpsimd
            def _(pool):
                pool.memset(before[:], 1.0).then_inc(s_b, 1)
                pool.wait_ge(s_b, 1)
                pool.affine_select(out=before[:], in_=before[:], compare_op=ALU.is_ge, fill=0.0, base=-1,
                                   pattern=[[1, EX], [-1, EX]], channel_multiplier=0).then_inc(s_b, 1)

            @block.tensor
            def _(pe):
                pe.wait_ge(s_w, 16)
                for i in range(NT):
                    for k in range(KT):
                        mm = pe.matmul(pl[:, i * EX:(i + 1) * EX], c.hT[:, k, i * 128:(i + 1) * 128], wg[:, k, :],
                                       start=(k == 0), stop=(k == KT - 1))
                mm.then_inc(s_l, 1)
                pe.wait_ge(s_d, 13)
                for i in range(NT):
                    mm = pe.matmul(pt[0:EX, i * 128:(i + 1) * 128], p[:, i, :], c.ident[:], start=True, stop=True)
                mm.then_inc(s_t, 1)

            @block.scalar
            def _(act):
                act.wait_ge(s_d, 2)
                act.activation(p[:], p[:], ACT.Exp).then_inc(s_x, 1)
                act.wait_ge(s_t, 1)
                for n in range(NB):
                    act.activation(blk(c.wT, n), pt[0:EX, n * 512:(n + 1) * 512], ACT.Copy).then_inc(s_te, 1)

            @block.vector
            def _(v):
                steps = [0]

                def then(ins):
                    ins.then_inc(s_d, 1)
                    steps[0] += 1
                    v.wait_ge(s_d, steps[0])

                def over(t):
                    return t[:].rearrange("p (n o) -> p n o", o=1).to_broadcast([128, NT, EX])

                four = [128, NT, EX, EX]
                mine = p[:].rearrange("p n (e o) -> p n e o", o=1).to_broadcast(four)
                other = p[:].rearrange("p n (o e) -> p n o e", o=1).to_broadcast(four)
                logits = pl[:, 0:NT * EX].rearrange("p (n e) -> p n e", e=EX)
                v.wait_ge(s_l, 1)
                then(v.tensor_reduce(mx[:], logits, AX.X, ALU.max))
                then(v.tensor_tensor(p[:], logits, over(mx), ALU.subtract))
                v.wait_ge(s_x, 1)
                then(v.tensor_reduce(sm[:], p[:], AX.X, ALU.add))
                then(v.reciprocal(mx[:], sm[:]))
                then(v.tensor_tensor(p[:], p[:], over(mx), ALU.mult))
                then(v.tensor_tensor(gt[:], other, mine, ALU.is_gt))
                then(v.tensor_tensor(eq[:], other, mine, ALU.is_equal))
                v.wait_ge(s_b, 2)
                then(v.tensor_tensor(eq[:], eq[:], before[:].rearrange("p (o e) j -> p o e j", o=1).to_broadcast(four),
                                     ALU.mult))
                then(v.tensor_tensor(gt[:], gt[:], eq[:], ALU.add))
                then(v.tensor_reduce(rank[:], gt[:], AX.X, ALU.add))
                then(v.scalar_tensor_tensor(p[:], rank[:], 1.5, p[:], ALU.is_lt, ALU.mult))
                then(v.tensor_reduce(sm[:], p[:], AX.X, ALU.add))
                v.reciprocal(mx[:], sm[:]).then_inc(s_te, 1)
                v.wait_ge(s_te, 1)
                then(v.tensor_tensor(p[:], p[:], over(mx), ALU.mult))


def phase_experts(c):
    nc, a = c.nc, c.a
    st = ExitStack()
    with st:
        w1 = [c.sb(f"expert_w1_{i}", [128, KT, FF], f32, st) for i in range(2)]
        w2 = [c.sb(f"expert_w2_{i}", [128, FT, D], f32, st) for i in range(2)]
        b1 = [c.sb(f"expert_b1_{i}", [128, FT], f32, st) for i in range(2)]
        pick = [c.sb(f"expert_pick{i}", [EX, 128], f32, st) for i in range(2)]
        picks = c.sb("expert_picks", [EX, EX, 128], f32, st)
        b2 = c.sb("expert_b2", [EX, D], f32, st)
        g = [c.sb(f"gelu{i}", [128, 512], f32, st) for i in range(3)]
        gw = [c.sb(f"gelu_weighted{i}", [128, 512], f32, st) for i in range(3)]
        pu = [c.pb(f"up_psum{i}", st) for i in range(3)]
        py = [c.pb(f"down_psum{i}", st) for i in range(4)]
        pw = c.pb("weight_psum", st)
        wrow = [c.sb(f"weight_in_rows{i}", [128, 512], f32, st) for i in range(2)]
        s_b2, s_pk, s_pick = c.sem("b2_loaded"), c.sem("picks_made"), c.sem("pick_staged")
        s_w = [c.sem(f"expert_loaded{i}") for i in range(2)]
        s_i, s_ie = c.sem("y_start_made"), c.sem("y_started")
        s_wr, s_wre, s_up, s_g, s_gw, s_dn, s_y = (c.sem(n) for n in (
            "weight_spread", "weight_copied", "up_made", "gelu_made", "gelu_weighted_s", "down_made", "y_added"))
        with nc.Block() as block:
            def units(eng, body):
                with eng.Fori(0, EX // 2) as ei:
                    for je in range(2):
                        with eng.Fori(0, NB // 2) as ni:
                            for jn in range(2):
                                body(ei * 2 + je, je, ni * 2 + jn, jn, ei * (2 * NB) + ni * 2 + (je * NB + jn))

            @block.sync
            def _(sp):
                sp.dma_start(b2[:], a["L0_ffn_bb2"]).then_inc(s_b2, 16)
                with nc.allow_non_contiguous_dma("a column of biases"):
                    def load(e, je):
                        sp.dma_start(w1[je][:], a["L0_ffn_w1"][e].rearrange("o (k p) f -> p (o k) f", p=128)).then_inc(s_w[je], 16)
                        sp.dma_start(w2[je][:], a["L0_ffn_w2"][e].rearrange("o (f p) d -> p (o f) d", p=128)).then_inc(s_w[je], 16)
                        sp.dma_start(b1[je][:], a["L0_ffn_bb1"][e].rearrange("o (f p) -> p (o f)", p=128)).then_inc(s_w[je], 16)

                    for je in range(2):
                        load(slice(je, je + 1), je)
                    with sp.Fori(1, EX // 2) as ei:
                        for je in range(2):
                            sp.wait_ge(s_y, ei * (2 * NB * KT) + ((je - 1) * NB * KT + 6))
                            load(bass.ds(ei * 2 + je, 1), je)

            @block.gpsimd
            def _(pool):
                pool.memset(picks[:], 0.0).then_inc(s_pk, 1)
                pool.wait_ge(s_pk, 1)
                pool.affine_select(out=picks[:], in_=picks[:], compare_op=ALU.not_equal, fill=1.0, base=0,
                                   pattern=[[-1, EX], [0, 128]], channel_multiplier=1).then_inc(s_pk, 1)
                pool.wait_ge(s_pk, 2)
                for je in range(2):
                    pool.tensor_copy(pick[je][:], picks[:, je]).then_inc(s_pick, 1)
                with pool.Fori(1, EX // 2) as ei:
                    for je in range(2):
                        pool.wait_ge(s_y, ei * (2 * NB * KT) + ((je - 1) * NB * KT + 6))
                        pool.tensor_copy(pick[je][:].rearrange("p (o n) -> p o n", o=1),
                                         picks[:, bass.ds(ei * 2 + je, 1), :]).then_inc(s_pick, 1)

            @block.tensor
            def _(pe):
                pe.wait_ge(s_b2, 16)
                for n in range(NB):
                    for m in range(KT):
                        i = n * KT + m
                        if i >= 4:
                            pe.wait_ge(s_ie, i - 3)
                        pe.matmul(py[i % 4][:], b2[:, m * 128:(m + 1) * 128], blk(c.wT, n), start=True, stop=True)\
                          .then_inc(s_i, 1)
                pe.wait_ge(s_ie, NB * KT)

                def body(e, je, n, jn, u):
                    q = u * FT
                    h = [c.hT[:, k, bass.ds(n * 512, 512)] for k in range(KT)]
                    pe.wait_ge(s_pick, e + 1)
                    pe.wait_ge(s_wre, u + 1)
                    pe.matmul(pw[:], pick[je][:], c.wT[:, bass.ds(n * 512, 512)], start=True, stop=True).then_inc(s_wr, 1)
                    pe.wait_ge(s_w[je], (e - je) * 24 + 48)

                    def up(f):
                        if f >= 3:
                            pe.wait_ge(s_g, q + (f - 2))
                        for k in range(KT):
                            mm = pe.matmul(pu[f % 3][:], w1[je][:, k, f * 128:(f + 1) * 128], h[k],
                                           start=(k == 0), stop=(k == KT - 1))
                        mm.then_inc(s_up, 1)

                    def down(f):
                        pe.wait_ge(s_gw, q + (f + 1))
                        for m in range(KT):
                            mm = pe.matmul(py[jn * 2 + m][:], w2[je][:, f, m * 128:(m + 1) * 128], gw[f % 3][:],
                                           start=(f == 0), stop=(f == FT - 1))
                        mm.then_inc(s_dn, 1)
                        return mm

                    up(0)
                    up(1)
                    pe.wait_ge(s_y, u * KT + (KT + 2))
                    for f in range(FT):
                        if f + 2 < FT:
                            up(f + 2)
                        down(f)
                units(pe, body)

            @block.scalar
            def _(act):
                def body(e, je, n, jn, u):
                    q = u * FT
                    for f in range(FT):
                        act.wait_ge(s_up, q + (f + 1))
                        if f == 0:
                            act.wait_ge(s_w[je], (e - je) * 24 + 48)
                        if f >= 3:
                            act.wait_ge(s_gw, q + (f - 2))
                        act.activation(g[f % 3][:], pu[f % 3][:], ACT.Gelu_apprx_tanh, bias=b1[je][:, f:f + 1])\
                            .then_inc(s_g, 1)
                units(act, body)

            @block.vector
            def _(v):
                for n in range(NB):
                    for m in range(KT):
                        i = n * KT + m
                        v.wait_ge(s_i, i + 1)
                        v.tensor_copy(blk(c.y[:, m], n), py[i % 4][:]).then_inc(s_ie, 1)
                v.tensor_copy(c.scratch[:, 0:2], c.ones[:, 0:2]).then_inc(s_wre, 1)
                v.tensor_copy(c.scratch[:, 2:4], c.ones[:, 0:2]).then_inc(s_y, 6)

                def body(e, je, n, jn, u):
                    q = u * FT
                    v.wait_ge(s_wr, u + 1)
                    v.tensor_copy(wrow[jn][:], pw[:]).then_inc(s_wre, 1)
                    v.wait_ge(s_wre, u + 2)
                    for f in range(FT):
                        v.wait_ge(s_g, q + (f + 1))
                        if f >= 3:
                            v.wait_ge(s_dn, q + (f - 2))
                        v.tensor_tensor(gw[f % 3][:], g[f % 3][:], wrow[jn][:], ALU.mult).then_inc(s_gw, 1)
                    v.wait_ge(s_dn, q + FT)
                    for m in range(KT):
                        y = c.y[:, m, bass.ds(n * 512, 512)]
                        v.tensor_tensor(y, py[jn * 2 + m][:], y, ALU.add).then_inc(s_y, 1)
                units(v, body)


def phase_store(c, src):
    nc = c.nc
    st = ExitStack()
    with st:
        rows = c.sb("out_rows", [128, 2, T // 128, D], f32, st)
        pt = [c.pb(f"rows_turned{i}", st) for i in range(2)]
        s_t, s_e, s_out = c.sem("rows_turned_s"), c.sem("rows_evacuated"), c.sem("rows_stored")
        with nc.Block() as block:
            @block.tensor
            def _(pe):
                n = 0
                for b in range(B):
                    for i in range(T // 128):
                        if n >= 2:
                            pe.wait_ge(s_e, n - 1)
                        for k in range(KT):
                            s = src[:, k, :].rearrange("p (t b) -> p b t", b=B)[:, b, i * 128:(i + 1) * 128]
                            mm = pe.transpose(pt[n % 2][:, k * 128:(k + 1) * 128], s, c.ident[:])
                        mm.then_inc(s_t, 1)
                        n += 1

            @block.vector
            def _(v):
                for n in range(B * T // 128):
                    v.wait_ge(s_t, n + 1)
                    v.tensor_copy(rows[:, n // (T // 128), n % (T // 128)], pt[n % 2][:, 0:D]).then_inc(s_e, 1)

            @block.sync
            def _(sp):
                for b in range(B):
                    sp.wait_ge(s_e, (b + 1) * (T // 128))
                    sp.dma_start(c.a["out"][b].rearrange("(i p) c -> p i c", p=128), rows[:, b]).then_inc(s_out, 16)
                sp.wait_ge(s_out, 16 * B)


def program(nc, args):
    stack = ExitStack()
    with stack:
        c = Core(nc, args, stack)
        c.ident = c.sb("identity", [128, 128])
        c.headones = c.sb("ones_within_head", [128, 128])
        c.ones = c.sb("ones", [128, 128])
        c.unscale = c.sb("unscale", [128, 2])
        c.scratch = c.sb("scratch", [128, 16])
        c.diag = c.sb("diagonal", [128, RD])
        c.h0 = c.sb("h0", [128, KT, B])
        c.wh2 = c.sb("rnn_Wh", [128, KT, D])
        c.wa2 = c.sb("rnn_Wh_high", [128, KT, D], f16)
        c.wb2 = c.sb("rnn_Wh_low", [128, KT, D], f16)
        c.xT = c.sb("xT", [128, KT, TOK])
        c.rT = c.sb("rT", [128, KT, TOK])
        c.r0 = c.sb("r0_products", [128, KT, B])
        s1 = ExitStack()
        with s1:
            c.wh = c.sb("lstm_Wh", [128, KT, G4], f32, s1)
            c.wa = c.sb("lstm_Wh_high", [128, KT, G4], f16, s1)
            c.wb = c.sb("lstm_Wh_low", [128, KT, G4], f16, s1)
            c.xz = c.sb("lstm_xz", [128, T, G4 // 128, B], f32, s1)
            c.hT = c.sb("hT", [128, KT, TOK], f32, s1)
            phase_load(c)
            phases_recurrent(c)
        c.hT = c.rT
        s5 = ExitStack()
        with s5:
            c.qT, c.kT = (c.sb(n, [128, 4, TOK], f32, s5) for n in ("q_heads", "k_heads"))
            c.oT = c.qT
            c.vt = c.sb("v_rows", [128, B * T // 128, AH, 32], f32, s5)
            c.rowmax = c.sb("score_max", [128, T // 128, 4, 32], f32, s5)
            c.mask_q, c.mask_k, c.ident16 = (c.sb(n, [128, 128], bf16, s5) for n in ("mask_q", "mask_k", "identity_bf16"))
            c.dsel = c.sb("sum_row_of_head", [128, 128], f32, s5)
            phase_heads(c)
            phase_attend(c)
            phase_attn_out(c)
        phase_layernorm(c, "norm1", None, c.hT, "L0_ffn_g1", "L0_ffn_b1", False)
        s6 = ExitStack()
        with s6:
            c.wT = c.sb("expert_weights", [EX, TOK], f32, s6)
            c.y = c.sb("expert_sum_y", [128, KT, TOK], f32, s6)
            phase_router(c)
            phase_experts(c)
            phase_layernorm(c, "norm2", c.y, c.xT, "L0_ffn_g2", "L0_ffn_b2", True)
        phase_store(c, c.xT)


_INS = ['x', 'cond_1024', 'L0_cond_Wx', 'L0_cond_Wh', 'L0_cond_b', 'L0_attn_Wq', 'L0_attn_Wk', 'L0_attn_Wv',
        'L0_attn_Wf1', 'L0_attn_Wf2', 'L0_attn_Wbeta', 'L0_attn_Wog1', 'L0_attn_Wog2', 'L0_attn_norm_w', 'L0_attn_Wo',
        'L0_cond2_Wx', 'L0_cond2_Wh', 'L0_cond2_b', 'L0_ffn_w_qkv', 'L0_ffn_w_o', 'L0_ffn_g1', 'L0_ffn_b1',
        'L0_ffn_wg', 'L0_ffn_w1', 'L0_ffn_bb1', 'L0_ffn_w2', 'L0_ffn_bb2', 'L0_ffn_g2', 'L0_ffn_b2']


def kernel(**inputs):
    import numpy as _np
    import concourse.bacc as _bacc
    from concourse import mybir as _mybir
    from concourse.bass_utils import run_bass_kernel_spmd as _run

    nc = _bacc.Bacc("TRN2", target_bir_lowering=False, num_devices=1)
    arrays, args = {}, {}
    for name in _INS:
        x = _np.ascontiguousarray(inputs[name])
        arrays[f"in_{name}_dram"] = x
        args[name] = nc.dram_tensor(f"in_{name}_dram", x.shape, _mybir.dt.from_np(x.dtype), kind="ExternalInput").ap()
    args["out"] = nc.dram_tensor("out_0_dram", (B, T, D), _mybir.dt.float32, kind="ExternalOutput").ap()
    program(nc, args)
    r = _run(nc, [arrays], core_ids=[0])
    return r.results[0]["out_0_dram"]
```
